# Optimizing a Trainium2 kernel written in Bass

```python
import numpy as np
import jax
import jax.numpy as jnp

def _softmax(x, axis=-1):
    return jax.nn.softmax(x, axis=axis)

def _gelu(x):
    return jax.nn.gelu(x, approximate=True)

def _silu(x):
    return jax.nn.silu(x)

def _sigmoid(x):
    return jax.nn.sigmoid(x)

def _layernorm(x, axis=-1, eps=1e-05):
    m = jnp.mean(x, axis=axis, keepdims=True)
    v = jnp.var(x, axis=axis, keepdims=True)
    return (x - m) / jnp.sqrt(v + eps)

def _scatter_add(tgt, idx, src, axis=0):
    return tgt.at[idx].add(src)

def _segment_sum(src, seg, n):
    return jax.ops.segment_sum(src, seg, n)
kernel_name = 'mk_flamingo_gated_d2_seqx_r8_78e6f4'

def setup_inputs(seed: int=0):
    np.random.seed(seed)
    _w = jnp.asarray

    def _rec_inputs():
        import jax
        import jax.numpy as jnp
        _rk = jax.random.key(seed)
        x = -0.0002928 + 1 * jax.random.normal(jax.random.fold_in(_rk, 1), (8, 256, 128), jnp.float32)
        _lenS = 256 - jax.random.randint(jax.random.fold_in(_rk, 7), (8,), 0, max(1, 256 // 4) + 1, jnp.int32)
        _lenS2 = 1601 - jax.random.randint(jax.random.fold_in(_rk, 8), (8,), 0, max(1, 1601 // 4) + 1, jnp.int32)
        _ctx_1024P = jax.random.normal(jax.random.fold_in(_rk, 11), (8, 16, 128), jnp.float32)
        _ctx_1024c = jax.random.dirichlet(jax.random.fold_in(_rk, 511), 0.3 * jnp.ones((16,), jnp.float32), (8, 1601))
        _ctx_1024t = jnp.einsum('bsk,bkd->bsd', _ctx_1024c, _ctx_1024P)
        _ctx_1024t = _ctx_1024t * jax.lax.rsqrt(jnp.mean(jnp.square(_ctx_1024t)) + 1e-12) * 0.953939
        ctx_1024 = -1.39393e-06 + 0.999914 * (_ctx_1024t + 0.3 * jax.random.normal(jax.random.fold_in(_rk, 611), (8, 1601, 128), jnp.float32))
        fside_Bx16xSxS2_0 = 9.80324e-06 + 0.100009 * jax.random.normal(jax.random.fold_in(_rk, 12), (8, 16, 256, 1601), jnp.float32)
        fside_SxS2_0 = -2.64403e-05 + 0.100002 * jax.random.normal(jax.random.fold_in(_rk, 14), (256, 1601), jnp.float32)
        _validS = jnp.arange(256)[None, :] < _lenS[:, None]
        _validS2 = jnp.arange(1601)[None, :] < _lenS2[:, None]
        _causal = jnp.tril(jnp.ones((256, 256), dtype=bool))
        mask_BxS2_bf0 = jnp.logical_not(jnp.ones((8, 1601), dtype=bool))
        _g = jax.random.normal(jax.random.fold_in(_rk, 9001), (2, 2), jnp.float32)
        _g = jnp.sign(_g) * jnp.maximum(jnp.abs(_g), 1.0) + (_g == 0) * 1.0
        g_xattn = _g[0]
        g_ffn = _g[1]
        return (x, ctx_1024, fside_Bx16xSxS2_0, fside_SxS2_0, _lenS2, mask_BxS2_bf0, g_xattn, g_ffn)
    x, ctx_1024, fside_Bx16xSxS2_0, fside_SxS2_0, _lenS2, mask_BxS2_bf0, g_xattn, g_ffn = _rec_inputs()

    def _L0_xattn_setup():
        import jax, jax.numpy as jnp
        import numpy as np
        E = 128
        H = 16
        D = E // H
        key = jax.random.key(seed)
        ks = jax.random.split(key, 12)
        B, T, S = (2, 256, 256)
        inp = {'query': jax.random.normal(ks[0], (B, T, E), jnp.float32), 'key': jax.random.normal(ks[1], (B, S, E), jnp.float32), 'value': jax.random.normal(ks[2], (B, S, E), jnp.float32), 'spatial_bias': jax.random.normal(ks[3], (B, H, T, S), jnp.float32) * 0.1, 'directional_bias': jax.random.normal(ks[4], (B, H, T, S), jnp.float32) * 0.1, 'key_padding_mask': jnp.zeros((B, S), dtype=bool), 'attn_mask': jax.random.normal(ks[5], (T, S), jnp.float32) * 0.1, 'Wq': jax.random.normal(ks[6], (E, E), jnp.float32) / np.sqrt(E), 'bq': jnp.zeros((E,), jnp.float32), 'Wk': jax.random.normal(ks[7], (E, E), jnp.float32) / np.sqrt(E), 'bk': jnp.zeros((E,), jnp.float32), 'Wv': jax.random.normal(ks[8], (E, E), jnp.float32) / np.sqrt(E), 'bv': jnp.zeros((E,), jnp.float32), 'Wo': jax.random.normal(ks[9], (E, E), jnp.float32) / np.sqrt(E), 'bo': jnp.zeros((E,), jnp.float32)}
        return inp
    _L0_xattn_all = _L0_xattn_setup()
    _L0_xattn_in = {k: v for k, v in _L0_xattn_all.items() if k in ('Wq', 'bq', 'Wk', 'bk', 'Wv', 'bv', 'Wo', 'bo')}
    del _L0_xattn_all

    def _L0_ffn_setup():
        import jax, jax.numpy as jnp
        import numpy as np
        key = jax.random.key(seed)
        k0, k1, k2, k3 = jax.random.split(key, 4)
        B, S, D, F, E = (8, 256, 128, 256, 8)
        x = jax.random.normal(k0, (B, S, D), dtype=jnp.float32)
        Wg = jax.random.normal(k1, (D, E), dtype=jnp.float32) * 0.02
        W1 = jax.random.normal(k2, (E, D, F), dtype=jnp.float32) * 0.02
        W2 = jax.random.normal(k3, (E, F, D), dtype=jnp.float32) * 0.02
        return {'x': x, 'Wg': Wg, 'W1': W1, 'W2': W2}
    _L0_ffn_all = _L0_ffn_setup()
    _L0_ffn_in = {k: v for k, v in _L0_ffn_all.items() if k in ('Wg', 'W1', 'W2')}
    del _L0_ffn_all

    def _L1_xattn_setup():
        import jax, jax.numpy as jnp
        import numpy as np
        D_MODEL = 128
        N_HEADS = 16
        D_Q = 64
        D_V = 64
        D_OUT = 128
        B, S = (4, 256)

        def _layer_norm(x, g, b, eps=1e-05):
            mu = jnp.mean(x, axis=-1, keepdims=True)
            var = jnp.mean((x - mu) ** 2, axis=-1, keepdims=True)
            return (x - mu) * jax.lax.rsqrt(var + eps) * g + b

        def _rope(x, theta=10000.0):
            D = x.shape[-1]
            inv_freq = 1.0 / theta ** (jnp.arange(0, D, 2, dtype=jnp.float32) / D)
            t = jnp.arange(x.shape[-2], dtype=jnp.float32)
            freqs = t[:, None] * inv_freq[None, :]
            freqs = jnp.repeat(freqs, 2, axis=-1)
            cos, sin = (jnp.cos(freqs), jnp.sin(freqs))
            x1, x2 = (x[..., 0::2], x[..., 1::2])
            rot = jnp.stack([-x2, x1], axis=-1).reshape(x.shape)
            return x * cos + rot * sin
        key = jax.random.key(seed)
        ks = jax.random.split(key, 10)
        x = jax.random.normal(ks[0], (B, S, D_MODEL), dtype=jnp.float32)
        sc = 1.0 / np.sqrt(D_MODEL)
        return {'query_sequences': x, 'key_sequences': x, 'value_sequences': x, 'key_value_sequence_lengths': jax.random.randint(ks[1], (B,), 1, S + 1), 'ln_g': jnp.ones((D_MODEL,), jnp.float32), 'ln_b': jnp.zeros((D_MODEL,), jnp.float32), 'Wq': jax.random.normal(ks[2], (D_MODEL, N_HEADS * D_Q), jnp.float32) * sc, 'bq': jnp.zeros((N_HEADS * D_Q,), jnp.float32), 'Wk': jax.random.normal(ks[3], (D_MODEL, N_HEADS * D_Q), jnp.float32) * sc, 'bk': jnp.zeros((N_HEADS * D_Q,), jnp.float32), 'Wv': jax.random.normal(ks[4], (D_MODEL, N_HEADS * D_V), jnp.float32) * sc, 'bv': jnp.zeros((N_HEADS * D_V,), jnp.float32), 'Wo': jax.random.normal(ks[5], (N_HEADS * D_V, D_OUT), jnp.float32) * (1.0 / np.sqrt(N_HEADS * D_V)), 'bo': jnp.zeros((D_OUT,), jnp.float32)}
    _L1_xattn_all = _L1_xattn_setup()
    _L1_xattn_in = {k: v for k, v in _L1_xattn_all.items() if k in ('ln_g', 'ln_b', 'Wq', 'bq', 'Wk', 'bk', 'Wv', 'bv', 'Wo', 'bo')}
    del _L1_xattn_all

    def _L1_ffn_setup():
        import jax, jax.numpy as jnp
        import numpy as np
        H = 128
        I = 64
        E = 32
        TOP_K = 6
        N_GROUP = 8
        TOPK_GROUP = 4
        SCALE = 2.5
        N_SHARED = 2
        SI = I * N_SHARED
        B, S = (2, 128)
        key = jax.random.key(seed)
        ks = jax.random.split(key, 8)
        x = jax.random.normal(ks[0], (B, S, H), jnp.float32)
        gate_weight = jax.random.normal(ks[1], (E, H), jnp.float32) * 0.02
        e_score_correction_bias = jax.random.normal(ks[2], (E,), jnp.float32) * 0.01
        experts_gate_up = jax.random.normal(ks[3], (E, 2 * I, H), jnp.float32) * 0.02
        experts_down = jax.random.normal(ks[4], (E, H, I), jnp.float32) * 0.02
        shared_gate_w = jax.random.normal(ks[5], (SI, H), jnp.float32) * 0.02
        shared_up_w = jax.random.normal(ks[6], (SI, H), jnp.float32) * 0.02
        shared_down_w = jax.random.normal(ks[7], (H, SI), jnp.float32) * 0.02
        return {'x': x, 'gate_weight': gate_weight, 'e_score_correction_bias': e_score_correction_bias, 'experts_gate_up': experts_gate_up, 'experts_down': experts_down, 'shared_gate_w': shared_gate_w, 'shared_up_w': shared_up_w, 'shared_down_w': shared_down_w}
    _L1_ffn_all = _L1_ffn_setup()
    _L1_ffn_in = {k: v for k, v in _L1_ffn_all.items() if k in ('gate_weight', 'e_score_correction_bias', 'experts_gate_up', 'experts_down', 'shared_gate_w', 'shared_up_w', 'shared_down_w')}
    del _L1_ffn_all
    return {'x': x, 'ctx_1024': ctx_1024, 'fside_Bx16xSxS2_0': fside_Bx16xSxS2_0, 'fside_SxS2_0': fside_SxS2_0, '_lenS2': _lenS2, 'mask_BxS2_bf0': mask_BxS2_bf0, 'g_xattn': g_xattn, 'g_ffn': g_ffn, 'L0_xattn_Wq': _L0_xattn_in['Wq'], 'L0_xattn_bq': _L0_xattn_in['bq'], 'L0_xattn_Wk': _L0_xattn_in['Wk'], 'L0_xattn_bk': _L0_xattn_in['bk'], 'L0_xattn_Wv': _L0_xattn_in['Wv'], 'L0_xattn_bv': _L0_xattn_in['bv'], 'L0_xattn_Wo': _L0_xattn_in['Wo'], 'L0_xattn_bo': _L0_xattn_in['bo'], 'L0_ffn_Wg': _L0_ffn_in['Wg'], 'L0_ffn_W1': _L0_ffn_in['W1'], 'L0_ffn_W2': _L0_ffn_in['W2'], 'L1_xattn_ln_g': _L1_xattn_in['ln_g'], 'L1_xattn_ln_b': _L1_xattn_in['ln_b'], 'L1_xattn_Wq': _L1_xattn_in['Wq'], 'L1_xattn_bq': _L1_xattn_in['bq'], 'L1_xattn_Wk': _L1_xattn_in['Wk'], 'L1_xattn_bk': _L1_xattn_in['bk'], 'L1_xattn_Wv': _L1_xattn_in['Wv'], 'L1_xattn_bv': _L1_xattn_in['bv'], 'L1_xattn_Wo': _L1_xattn_in['Wo'], 'L1_xattn_bo': _L1_xattn_in['bo'], 'L1_ffn_gate_weight': _L1_ffn_in['gate_weight'], 'L1_ffn_e_score_correction_bias': _L1_ffn_in['e_score_correction_bias'], 'L1_ffn_experts_gate_up': _L1_ffn_in['experts_gate_up'], 'L1_ffn_experts_down': _L1_ffn_in['experts_down'], 'L1_ffn_shared_gate_w': _L1_ffn_in['shared_gate_w'], 'L1_ffn_shared_up_w': _L1_ffn_in['shared_up_w'], 'L1_ffn_shared_down_w': _L1_ffn_in['shared_down_w']}

def reference(x, ctx_1024, fside_Bx16xSxS2_0, fside_SxS2_0, _lenS2, mask_BxS2_bf0, g_xattn, g_ffn, L0_xattn_Wq, L0_xattn_bq, L0_xattn_Wk, L0_xattn_bk, L0_xattn_Wv, L0_xattn_bv, L0_xattn_Wo, L0_xattn_bo, L0_ffn_Wg, L0_ffn_W1, L0_ffn_W2, L1_xattn_ln_g, L1_xattn_ln_b, L1_xattn_Wq, L1_xattn_bq, L1_xattn_Wk, L1_xattn_bk, L1_xattn_Wv, L1_xattn_bv, L1_xattn_Wo, L1_xattn_bo, L1_ffn_gate_weight, L1_ffn_e_score_correction_bias, L1_ffn_experts_gate_up, L1_ffn_experts_down, L1_ffn_shared_gate_w, L1_ffn_shared_up_w, L1_ffn_shared_down_w):
    import jax
    import jax.numpy as jnp

    def _L0_xattn_ref(query, key, value, spatial_bias, directional_bias, key_padding_mask, attn_mask, Wq, bq, Wk, bk, Wv, bv, Wo, bo):
        import jax, jax.numpy as jnp
        import numpy as np
        E = 128
        H = 16
        D = E // H
        B, T, _ = query.shape
        S = key.shape[1]
        scale = D ** (-0.5)
        q = (query @ Wq.T + bq).reshape(B, T, H, D).transpose(0, 2, 1, 3)
        k = (key @ Wk.T + bk).reshape(B, S, H, D).transpose(0, 2, 1, 3)
        v = (value @ Wv.T + bv).reshape(B, S, H, D).transpose(0, 2, 1, 3)
        scores = jnp.einsum('bhtd,bhsd->bhts', q, k) * scale
        scores = scores + attn_mask[None, None, :, :]
        pad = key_padding_mask[:, None, None, :]
        scores = jnp.where(pad, -jnp.inf, scores)
        if T == S:
            scores = scores + spatial_bias + directional_bias
        probs = jax.nn.softmax(scores, axis=-1)
        out = jnp.einsum('bhts,bhsd->bhtd', probs, v)
        out = out.transpose(0, 2, 1, 3).reshape(B, T, E)
        return out @ Wo.T + bo

    def _L0_ffn_ref(x, Wg, W1, W2):
        import jax, jax.numpy as jnp
        import numpy as np
        B, S, D = x.shape
        E = Wg.shape[1]
        T = B * S
        cap = max(1, T // E)
        xt = x.reshape(T, D)
        logits = xt @ Wg
        probs = jax.nn.softmax(logits, axis=-1)
        pT = probs.T
        _, top_idx = jax.lax.top_k(pT, cap)
        sel = jnp.zeros((E, T), dtype=bool).at[jnp.arange(E)[:, None], top_idx].set(True)
        masked = jnp.where(sel, pT, -jnp.inf)
        assigned = sel.any(axis=0)
        tok2exp = jnp.where(assigned, jnp.argmax(masked, axis=0), jnp.argmax(pT, axis=0))
        weights = jnp.take_along_axis(probs, tok2exp[:, None], axis=1)[:, 0]
        out = jnp.zeros_like(xt)
        for e in range(E):
            gate = jnp.where(tok2exp == e, weights, 0.0)
            h = jax.nn.gelu(xt @ W1[e], approximate=False) @ W2[e]
            out = out + gate[:, None] * h
        return out.reshape(B, S, D)

    def _L1_xattn_ref(query_sequences, key_sequences, value_sequences, key_value_sequence_lengths, ln_g, ln_b, Wq, bq, Wk, bk, Wv, bv, Wo, bo):
        import jax, jax.numpy as jnp
        import numpy as np
        D_MODEL = 128
        N_HEADS = 16
        D_Q = 64
        D_V = 64
        D_OUT = 128
        B, S = (4, 256)

        def _layer_norm(x, g, b, eps=1e-05):
            mu = jnp.mean(x, axis=-1, keepdims=True)
            var = jnp.mean((x - mu) ** 2, axis=-1, keepdims=True)
            return (x - mu) * jax.lax.rsqrt(var + eps) * g + b

        def _rope(x, theta=10000.0):
            D = x.shape[-1]
            inv_freq = 1.0 / theta ** (jnp.arange(0, D, 2, dtype=jnp.float32) / D)
            t = jnp.arange(x.shape[-2], dtype=jnp.float32)
            freqs = t[:, None] * inv_freq[None, :]
            freqs = jnp.repeat(freqs, 2, axis=-1)
            cos, sin = (jnp.cos(freqs), jnp.sin(freqs))
            x1, x2 = (x[..., 0::2], x[..., 1::2])
            rot = jnp.stack([-x2, x1], axis=-1).reshape(x.shape)
            return x * cos + rot * sin
        b, sq, _ = query_sequences.shape
        sk = key_sequences.shape[1]
        q_in = _layer_norm(query_sequences, ln_g, ln_b)
        k_in = _layer_norm(key_sequences, ln_g, ln_b)
        v_in = _layer_norm(value_sequences, ln_g, ln_b)
        q = (q_in @ Wq + bq).reshape(b, sq, N_HEADS, D_Q).transpose(0, 2, 1, 3)
        k = (k_in @ Wk + bk).reshape(b, sk, N_HEADS, D_Q).transpose(0, 2, 1, 3)
        v = (v_in @ Wv + bv).reshape(b, sk, N_HEADS, D_V).transpose(0, 2, 1, 3)
        q = _rope(q)
        k = _rope(k)
        scores = jnp.einsum('bhqd,bhkd->bhqk', q, k) * (1.0 / np.sqrt(D_Q))
        valid = jnp.arange(sk)[None, :] < key_value_sequence_lengths[:, None]
        scores = jnp.where(valid[:, None, None, :], scores, -jnp.inf)
        attn = jax.nn.softmax(scores, axis=-1)
        out = jnp.einsum('bhqk,bhkd->bhqd', attn, v)
        out = out.transpose(0, 2, 1, 3).reshape(b, sq, N_HEADS * D_V)
        return out @ Wo + bo

    def _L1_ffn_ref(x, gate_weight, e_score_correction_bias, experts_gate_up, experts_down, shared_gate_w, shared_up_w, shared_down_w):
        import jax, jax.numpy as jnp
        import numpy as np
        H = 128
        I = 64
        E = 32
        TOP_K = 6
        N_GROUP = 8
        TOPK_GROUP = 4
        SCALE = 2.5
        N_SHARED = 2
        SI = I * N_SHARED
        B, S = (2, 128)
        b, s, h = x.shape
        xf = x.reshape(-1, h)
        T = xf.shape[0]
        logits = xf.astype(jnp.float32) @ gate_weight.astype(jnp.float32).T
        scores = jax.nn.sigmoid(logits)
        sfc = scores + e_score_correction_bias[None, :]
        gs = E // N_GROUP
        group_scores = sfc.reshape(T, N_GROUP, gs).max(axis=-1)
        _, gidx = jax.lax.top_k(group_scores, TOPK_GROUP)
        gmask = jnp.zeros((T, N_GROUP), bool).at[jnp.arange(T)[:, None], gidx].set(True)
        smask = jnp.repeat(gmask, gs, axis=1)
        masked = jnp.where(smask, sfc, 0.0)
        _, topk_idx = jax.lax.top_k(masked, TOP_K)
        tw = jnp.take_along_axis(scores, topk_idx, axis=1)
        tw = tw / (tw.sum(-1, keepdims=True) + 1e-20)
        tw = (tw * SCALE).astype(xf.dtype)
        combine = jnp.zeros((T, E), xf.dtype).at[jnp.arange(T)[:, None], topk_idx].add(tw)

        def expert_step(acc, inp):
            gu, dn, c = inp
            g = xf @ gu[:I].T
            u = xf @ gu[I:].T
            o = jax.nn.silu(g) * u @ dn.T
            return (acc + c[:, None] * o, None)
        routed, _ = jax.lax.scan(expert_step, jnp.zeros_like(xf), (experts_gate_up, experts_down, combine.T))
        sh = jax.nn.silu(xf @ shared_gate_w.T) * (xf @ shared_up_w.T)
        shared_out = sh @ shared_down_w.T
        return (routed + shared_out).reshape(b, s, h)
    x = x + jnp.tanh(g_xattn[0]) * _L0_xattn_ref(_layernorm(x, axis=-1), ctx_1024, ctx_1024, fside_Bx16xSxS2_0, fside_Bx16xSxS2_0, mask_BxS2_bf0, fside_SxS2_0, L0_xattn_Wq, L0_xattn_bq, L0_xattn_Wk, L0_xattn_bk, L0_xattn_Wv, L0_xattn_bv, L0_xattn_Wo, L0_xattn_bo)
    x = x + jnp.tanh(g_ffn[0]) * _L0_ffn_ref(_layernorm(x, axis=-1), L0_ffn_Wg, L0_ffn_W1, L0_ffn_W2)
    x = x + jnp.tanh(g_xattn[1]) * _L1_xattn_ref(_layernorm(x, axis=-1), ctx_1024, ctx_1024, _lenS2, L1_xattn_ln_g, L1_xattn_ln_b, L1_xattn_Wq, L1_xattn_bq, L1_xattn_Wk, L1_xattn_bk, L1_xattn_Wv, L1_xattn_bv, L1_xattn_Wo, L1_xattn_bo)
    x = x + jnp.tanh(g_ffn[1]) * _L1_ffn_ref(_layernorm(x, axis=-1), L1_ffn_gate_weight, L1_ffn_e_score_correction_bias, L1_ffn_experts_gate_up, L1_ffn_experts_down, L1_ffn_shared_gate_w, L1_ffn_shared_up_w, L1_ffn_shared_down_w)
    return x

_drawn_inputs = setup_inputs


def setup_inputs(seed=0):
    import zlib

    import numpy as np

    out = dict(_drawn_inputs(seed))
    spreads = {'g_ffn': (-1.0, 0.6),
     'L0_xattn_bq': (0.0, 0.498),
     'L0_xattn_bk': (0.0, 0.8),
     'L0_xattn_bv': (0.0, 0.1),
     'L0_xattn_bo': (0.0, 0.1),
     'L1_xattn_ln_g': (1.0, 0.2),
     'L1_xattn_ln_b': (0.0, 0.1),
     'L1_xattn_bq': (0.0, 0.8),
     'L1_xattn_bk': (0.0, 0.8),
     'L1_xattn_bv': (0.0, 0.1),
     'L1_xattn_bo': (0.0, 0.1)}
    factors = {'fside_SxS2_0': 8.0,
     'L0_ffn_Wg': 8.0,
     'L0_ffn_W1': 8.0,
     'L0_ffn_W2': 8.0,
     'L1_ffn_gate_weight': 8.0,
     'L1_ffn_e_score_correction_bias': 8.0,
     'L1_ffn_experts_gate_up': 8.0,
     'L1_ffn_experts_down': 8.0,
     'L1_ffn_shared_gate_w': 8.0,
     'L1_ffn_shared_up_w': 8.0,
     'L1_ffn_shared_down_w': 8.0}
    for name, (base, spread) in spreads.items():
        noise = np.random.default_rng([zlib.crc32(name.encode()), seed]).standard_normal(out[name].shape)
        drawn = base * np.exp(spread * noise) if base else spread * noise
        out[name] = jnp.asarray(drawn.astype(out[name].dtype))
    for name, factor in factors.items():
        out[name] = (out[name] * factor).astype(out[name].dtype)
    return out
```

```python
from contextlib import ExitStack

import numpy as np

import concourse.bass as bass
import concourse.mybir as mybir
from concourse.alu_op_type import AluOpType as ALU

ACT = mybir.ActivationFunctionType
AX = mybir.AxisListType
F32 = mybir.dt.float32
F16 = mybir.dt.float16
I32 = mybir.dt.int32
U8 = mybir.dt.uint8

P = 128
B, T, E = 8, 256, 128
S = 1601
H = 16
TT = T // P
NT = B * TT
TOK = B * T
SC = -(-S // P)
FULL = S // P
REST = S - FULL * P
BANK = 512
SPANS = [(o, min(BANK, S - o)) for o in range(0, S, BANK)]
GROUPS = [range(4 * g, min(4 * g + 4, SC)) for g in range(4)]
D0 = E // H
D1 = 64
EPS = 1e-5
NEG = -1e30
LOWEST = -3e38
X0, CAP = 8, TOK // 8
F0 = 256
X1, I1 = 32, 64
PAIRS = X1 * I1 // P
GR, KEEP, TOP = 8, 4, 6
SCALE1 = 2.5
UB = H * TT


def on_its_own(eng, s):
    eng.sem_inc(s.passed, 1)


def rows(c):
    return P if c < FULL else REST


class Named:
    pass


def prime(nc, s):
    with nc.Block() as block:
        @block.sync
        def _(sp):
            for semaphore in s.to_prime:
                sp.sem_inc(semaphore, 1)
    s.to_prime.clear()


def ln_vector(nc, dve, m, s, src, dst, done_before):
    base = 6 * done_before
    for k in range(NT):
        ins = nc.vector.bn_stats(m.stats[:, k, :], src[:, k, :])
    ins.then_inc(s.ln, 1)
    dve.wait_ge(s.ln, base + 1)
    for k in range(NT):
        ins = nc.vector.bn_aggr(m.mv[:, k, :], m.stats[:, k, :])
    ins.then_inc(s.ln, 1)
    dve.wait_ge(s.ln, base + 2)
    nc.vector.tensor_scalar(m.var[:, 0:NT], m.mv[:, 0:NT, 1], EPS, None, ALU.add).then_inc(s.ln, 1)
    dve.wait_ge(s.ln_sqrt, done_before + 1)
    nc.vector.reciprocal(m.rstd[:, 0:NT], m.var[:, 0:NT]).then_inc(s.ln, 1)
    dve.wait_ge(s.ln, base + 4)
    for k in range(NT):
        ins = nc.vector.tensor_scalar(dst[:, k, :], src[:, k, :], m.mv[:, k, 0:1], m.rstd[:, k:k + 1],
                                      ALU.subtract, ALU.mult)
    ins.then_inc(s.ln, 2)
    dve.wait_ge(s.ln, base + 6)


def ln_scalar(nc, act, m, s, done_before):
    act.wait_ge(s.ln, 6 * done_before + 3)
    nc.scalar.activation(m.var[:, 0:NT], m.var[:, 0:NT], ACT.Sqrt).then_inc(s.ln_sqrt, 1)


def pe_scores(nc, pe, m, a, use, lhsT, rhs):
    for q, (o, w) in enumerate(SPANS):
        pe.wait_ge(a.bank_free[q], 1 + use)
        nc.tensor.matmul(m.psS[:, o:o + w], lhsT, rhs(o, w), start=True, stop=True).then_inc(a.bank_full, 1)


def pe_transpose(nc, pe, m, a, n, buf):
    pe.wait_ge(a.exp_done, n + 1)
    for g, chunks in enumerate(GROUPS):
        pe.wait_ge(a.copied_act if g % 2 == 0 else a.copied_dve, 1 + 2 * n + g // 2)
        for c in chunks:
            o = (c % 4) * P
            ins = nc.tensor.transpose(m.psT[g % 2][0:rows(c), o:o + P],
                                      m.probs[:, buf, c * P:c * P + rows(c)], m.ident[:, :])
        ins.then_inc(a.group_full, 1)


def pe_values(nc, pe, m, a, n, buf, values, d):
    pe.wait_ge(a.out_taken, 1 + n)
    for g, chunks in enumerate(GROUPS):
        pe.wait_ge(a.copied_act if g % 2 == 0 else a.copied_dve, 1 + 2 * n + g // 2 + 1)
        for c in chunks:
            r = rows(c)
            ins = nc.tensor.matmul(m.psO[:, 0:d], m.probsT[0:r, buf, c, :], values(c, r),
                                   start=(c == 0), stop=(c == SC - 1))
    ins.then_inc(a.out_full, 1)


def dve_mask_max(nc, dve, m, a, n, use, buf, mask, spans):
    for q in spans:
        o, w = SPANS[q]
        dve.wait_ge(a.bank_full, 4 * use + q + 1)
        on_its_own(dve, m.s)
        nc.vector.tensor_tensor_reduce(m.probs[:, buf, o:o + w], m.psS[:, o:o + w], mask(o, w), 1.0, LOWEST,
                                       ALU.add, ALU.max, m.max4[:, buf, q:q + 1]).then_inc(a.bank_free[q], 1)
    if spans[-1] == 3:
        for q in range(4):
            dve.wait_ge(a.bank_free[q], 1 + use + 1)
        nc.vector.tensor_reduce(m.negmax[:, buf:buf + 1], m.max4[:, buf, :], AX.X, ALU.max,
                                negate=True).then_inc(a.max_done, 1)


def act_exp(nc, act, m, a, n, buf):
    act.wait_ge(a.max_done, n + 1)
    nc.scalar.activation(m.probs[:, buf, 0:S], m.probs[:, buf, 0:S], ACT.Exp, bias=m.negmax[:, buf:buf + 1],
                         accum_out=m.sums[:, buf:buf + 1]).then_inc(a.exp_done, 1)


def copy_group(nc, eng, m, a, n, buf, g, copied):
    copy = nc.scalar.copy if g % 2 == 0 else nc.vector.tensor_copy
    eng.wait_ge(a.group_full, 4 * n + g + 1)
    chunks = GROUPS[g]
    r = rows(chunks[-1])
    src = m.psT[g % 2][0:r, 0:len(chunks) * P].rearrange("p (c t) -> p c t", t=P)
    copy(m.probsT[0:r, buf, chunks[0]:chunks[-1] + 1, :], src).then_inc(copied, 1)


def dve_take_out(nc, dve, m, a, n, buf, dst, bias, d):
    dve.wait_ge(a.exp_done, n + 1)
    nc.vector.reciprocal(m.rsum[:, buf:buf + 1], m.sums[:, buf:buf + 1]).then_inc(a.recip_done, 1)
    dve.wait_ge(a.recip_done, n + 1)
    dve.wait_ge(a.out_full, 1 + n + 1)
    nc.vector.scalar_tensor_tensor(dst, m.psO[:, 0:d], m.rsum[:, buf:buf + 1], bias,
                                   ALU.mult, ALU.add).then_inc(a.out_taken, 1)


def attention_sems(s, tag):
    a = Named()
    a.bank_full, a.exp_done, a.group_full = (s.sem(f"{tag}_{n}") for n in ("bank_full", "exp_done", "group_full"))
    a.max_done, a.recip_done = (s.sem(f"{tag}_{n}") for n in ("max_done", "recip_done"))
    a.copied_act, a.copied_dve = (s.from_one(f"{tag}_{n}") for n in ("copied_act", "copied_dve"))
    a.out_taken, a.out_full = (s.from_one(f"{tag}_{n}") for n in ("out_taken", "out_full"))
    a.bank_free = [s.from_one(f"{tag}_bank_free{q}") for q in range(4)]
    return a


def block_load(nc, m, s, dram):
    with nc.Block() as block:
        @block.sync
        def _(sp):
            sp.dma_start(m.x[:, :, :], dram["x"].rearrange("b (t p) d -> p (b t) d", p=P)).then_inc(s.load, 16)
            for name in LOADED:
                getdst = m.loaded[name]
                sp.dma_start(getdst, m.source[name]).then_inc(s.load, 16)
            sp.wait_ge(s.load, 16 * (1 + len(LOADED)))

        @block.scalar
        def _(act):
            ln_scalar(nc, act, m, s, 0)
            act.wait_ge(s.load, 16 * (1 + len(LOADED)))
            nc.scalar.activation(m.gates[:, :], m.gates[:, :], ACT.Tanh).then_inc(s.tanh, 1)
            act.wait_ge(s.tanh, 1)

        @block.vector
        def _(dve):
            dve.wait_ge(s.load, 16 * (1 + len(LOADED)))
            ln_vector(nc, dve, m, s, m.x, m.xn, 0)


LOADED = ["ident", "fold", "below", "cos_sin", "earlier", "weight8", "headmask", "scanreset", "ones",
          "gates", "wq0", "wk0", "wv0", "wo0", "bq0", "bk0", "bv0", "bo0"]


def block_attention0(nc, m, s, dram):
    with ExitStack() as stack:
        def sb(name, shape, dt=F32):
            return stack.enter_context(nc.sbuf_tensor(name, shape, dt))

        m.attn_mask, m.mask = sb("attn_mask", [P, TT, S]), sb("mask", [P, TT, S])
        m.pad8 = sb("pad8", [P, S], U8)
        m.o0 = sb("o0", [P, TT, E])
        m.k32, m.q32 = sb("k32", [P, S]), sb("q32", [P, T])
        m.khi, m.klo = sb("khi", [P, S], F16), sb("klo", [P, S], F16)
        m.qhi, m.qlo = sb("qhi", [P, T], F16), sb("qlo", [P, T], F16)
        m.kfan, m.qfan = sb("kfan", [P, 4, S], F16), sb("qfan", [P, 4, T], F16)
        m.qhead, m.vhead = sb("qhead", [P, 4, T], F16), sb("vhead", [P, 4, SC, D0])
        m.v0 = sb("v0", [P, SC, E])
        attention0(nc, m, s, dram)


def attention0(nc, m, s, dram):
    a = attention_sems(s, "a0")
    ctx_ready, mask_ready = s.sem("a0_ctx_ready"), s.sem("a0_mask_ready")
    pe_step, act_step, dve_step, pool_step = (s.sem(f"a0_{e}_step") for e in ("pe", "act", "dve", "pool"))
    split_done, fanned, batch_done = s.sem("a0_split_done"), s.sem("a0_fanned"), s.from_one("a0_batch_done")
    prime(nc, s)
    head_ready, mask_loaded = s.sem("a0_head_ready"), s.sem("a0_mask_loaded")
    PE_STEPS, ACT_STEPS, DVE_STEPS = 7, 4, 6
    GH = 4
    NG = H // GH
    GU = GH * TT

    def unit(b, g, u):
        return b * UB + g * GU + u

    with nc.Block() as block:
        @block.sync
        def _(sp):
            sp.dma_start(m.attn_mask[:, :, :], dram["attn_mask"].rearrange("(t p) s -> p t s", p=P)).then_inc(mask_loaded, 16)
            with sp.Fori(0, B) as b:
                sp.wait_ge(batch_done, 1 + b)
                sp.dma_start(m.ctx[:, 0:FULL, :], dram["ctx"][bass.ds(b, 1), 0:FULL * P, :]
                             .rearrange("a (c p) d -> p (a c) d", p=P)).then_inc(ctx_ready, 16)
                sp.dma_start(m.ctx[0:REST, FULL, :], dram["ctx"][bass.ds(b, 1), FULL * P:S, :]
                             .rearrange("a p d -> p (a d)")).then_inc(ctx_ready, 16)
                sp.dma_start(m.pad8[:, :], dram["pad"][bass.ds(b, 1), :].to_broadcast([P, S])).then_inc(ctx_ready, 16)
                sp.wait_ge(split_done, 4 * b + 4)
                for r in range(4):
                    kpart = m.khi if r % 2 == 0 else m.klo
                    qpart = m.qhi if r < 2 else m.qlo
                    for g in range(NG):
                        sp.dma_start(m.kfan[32 * r:32 * r + 32, g, :],
                                     kpart[32 * g:32 * g + 32, :]).then_inc(fanned, 16)
                        sp.dma_start(m.qfan[32 * r:32 * r + 32, g, :],
                                     qpart[32 * g:32 * g + 32, :]).then_inc(fanned, 16)

        @block.gpsimd
        def _(pool):
            with pool.Fori(0, B) as b:
                pool.wait_ge(act_step, ACT_STEPS * b + 3)
                on_its_own(pool, s)
                nc.gpsimd.tensor_copy(m.khi[:, :], m.k32[:, :]).then_inc(split_done, 1)
                pool.wait_ge(split_done, 4 * b + 1)
                nc.gpsimd.tensor_tensor(m.klo[:, :], m.k32[:, :], m.khi[:, :], ALU.subtract).then_inc(split_done, 1)
                pool.wait_ge(dve_step, DVE_STEPS * b + 3)
                on_its_own(pool, s)
                nc.gpsimd.tensor_copy(m.qhi[:, :], m.q32[:, :]).then_inc(split_done, 1)
                pool.wait_ge(split_done, 4 * b + 3)
                nc.gpsimd.tensor_tensor(m.qlo[:, :], m.q32[:, :], m.qhi[:, :], ALU.subtract).then_inc(split_done, 1)
                pool.wait_ge(fanned, 16 * 8 * NG * (b + 1))
                pool.wait_ge(act_step, ACT_STEPS * b + 4)
                pool.wait_ge(dve_step, DVE_STEPS * b + 4)
                on_its_own(pool, s)
                with pool.Fori(0, NG) as g:
                    for j in range(GH):
                        if j == 0:
                            pool.wait_ge(a.out_full, 1 + unit(b, g, 0))
                            on_its_own(pool, s)
                        nc.gpsimd.tensor_copy(m.vhead[:, j, :, :],
                                              m.v0[:, :, bass.ds(g * (GH * D0) + j * D0, D0)]).then_inc(head_ready, 1)
                        nc.gpsimd.tensor_tensor(m.qhead[:, j, :], m.qfan[:, bass.ds(g, 1), :].rearrange("p a t -> p (a t)"),
                                                m.headmask[:, j:j + 1].to_broadcast([P, T]), ALU.mult).then_inc(head_ready, 1)

        def heads_before(b, g):
            return (b * NG + g) * GH

        @block.tensor
        def _(pe):
            with pe.Fori(0, B) as b:
                pe.wait_ge(ctx_ready, 48 * (b + 1))
                pe.wait_ge(batch_done, 1 + b)
                for c in range(SC):
                    r = rows(c)
                    ins = nc.tensor.transpose(m.psS[:, c * P:c * P + r], m.ctx[0:r, c, :], m.ident[0:r, 0:r])
                ins.then_inc(pe_step, 1)
                pe.wait_ge(mask_ready, b + 1)
                for t in range(TT):
                    ins = nc.tensor.transpose(m.psT[0][:, t * P:(t + 1) * P], m.xb[:, t, :], m.ident[:, :])
                ins.then_inc(pe_step, 1)
                pe.wait_ge(act_step, ACT_STEPS * b + 1)
                pe.wait_ge(dve_step, DVE_STEPS * b + 1)
                for o, w in SPANS:
                    ins = nc.tensor.matmul(m.psS[:, o:o + w], m.wk0[:, :], m.ctxT[:, o:o + w], start=True, stop=True)
                ins.then_inc(pe_step, 1)
                pe.wait_ge(dve_step, DVE_STEPS * b + 2)
                nc.tensor.matmul(m.psT[1][:, 0:T], m.wq0[:, :], m.xT[:, 0:T], start=True, stop=True).then_inc(pe_step, 1)
                pe.wait_ge(act_step, ACT_STEPS * b + 3)
                for c in range(SC):
                    r = rows(c)
                    ins = nc.tensor.matmul(m.psS[0:r, c * P:(c + 1) * P], m.ctxT[:, c * P:c * P + r], m.wv0[:, :],
                                           start=True, stop=True)
                ins.then_inc(pe_step, 1)
                pe.wait_ge(act_step, ACT_STEPS * b + 4)
                pe.wait_ge(dve_step, DVE_STEPS * b + 4)
                on_its_own(pe, s)

                def scores(g, u):
                    n = unit(b, g, u)
                    j, t = u // TT, u % TT
                    if t == 0:
                        pe.wait_ge(head_ready, 2 * (heads_before(b, g) + j) + 2)
                    pe_scores(nc, pe, m, a, n, m.qhead[:, j, t * P:(t + 1) * P],
                              lambda o, w: m.kfan[:, bass.ds(g, 1), o:o + w].rearrange("p a s -> p (a s)"))

                def group(g, last):
                    for u in range(GU):
                        n = unit(b, g, u)
                        if u + 1 < GU:
                            scores(g, u + 1)
                        pe_transpose(nc, pe, m, a, n, u % 2)
                        pe_values(nc, pe, m, a, n, u % 2, lambda c, r: m.vhead[0:r, u // TT, c, :], D0)

                with pe.Fori(0, NG) as g:
                    scores(g, 0)
                    group(g, False)

                pe.wait_ge(a.out_taken, 1 + UB * (b + 1))
                for t in range(TT):
                    ins = nc.tensor.transpose(m.psS[:, t * P:(t + 1) * P], m.o0[:, t, :], m.ident[:, :])
                ins.then_inc(pe_step, 1)
                pe.wait_ge(dve_step, DVE_STEPS * b + 5)
                for t in range(TT):
                    ins = nc.tensor.matmul(m.psM[:, t * P:(t + 1) * P], m.oT[:, t * P:(t + 1) * P], m.wo0[:, :],
                                           start=True, stop=True)
                ins.then_inc(pe_step, 1)

        @block.scalar
        def _(act):
            with act.Fori(0, B) as b:
                act.wait_ge(pe_step, PE_STEPS * b + 1)
                nc.scalar.copy(m.ctxT[:, 0:2 * BANK], m.psS[:, 0:2 * BANK]).then_inc(act_step, 1)
                act.wait_ge(act_step, ACT_STEPS * b + 1)
                act.wait_ge(pe_step, PE_STEPS * b + 3)
                nc.scalar.activation(m.k32[:, 0:2 * BANK], m.psS[:, 0:2 * BANK], ACT.Identity,
                                     bias=m.bk0[:, 0:1]).then_inc(act_step, 1)
                nc.scalar.activation(m.k32[:, 2 * BANK:S], m.psS[:, 2 * BANK:S], ACT.Identity,
                                     bias=m.bk0[:, 0:1]).then_inc(act_step, 1)
                act.wait_ge(pe_step, PE_STEPS * b + 5)
                nc.scalar.copy(m.v0[:, 0:8, :], m.psS[:, 0:8 * P].rearrange("p (c d) -> p c d", d=E)).then_inc(act_step, 1)

                def group(g):
                    for u in range(GU):
                        n = unit(b, g, u)
                        copy_group(nc, act, m, a, n, u % 2, 0, a.copied_act)
                        copy_group(nc, act, m, a, n, u % 2, 2, a.copied_act)
                        if u + 1 < GU:
                            act_exp(nc, act, m, a, n + 1, (u + 1) % 2)

                with act.Fori(0, NG) as g:
                    act_exp(nc, act, m, a, unit(b, g, 0), 0)
                    group(g)

        @block.vector
        def _(dve):
            nc.vector.memset(m.v0[:, FULL, :], 0.0)
            dve.wait_ge(mask_loaded, 16)
            with dve.Fori(0, B) as b:
                nc.vector.tensor_copy(m.xb[:, :, :], m.xn[:, bass.ds(b * TT, TT), :])
                dve.wait_ge(ctx_ready, 48 * (b + 1))
                for t in range(TT):
                    ins = nc.vector.scalar_tensor_tensor(m.mask[:, t, :], m.pad8[:, :], NEG, m.attn_mask[:, t, :],
                                                         ALU.mult, ALU.add)
                ins.then_inc(mask_ready, 1)
                dve.wait_ge(mask_ready, b + 1)
                dve.wait_ge(pe_step, PE_STEPS * b + 1)
                nc.vector.tensor_copy(m.ctxT[:, 2 * BANK:S], m.psS[:, 2 * BANK:S]).then_inc(dve_step, 1)
                dve.wait_ge(pe_step, PE_STEPS * b + 2)
                nc.vector.tensor_copy(m.xT[:, 0:T], m.psT[0][:, 0:T]).then_inc(dve_step, 1)
                dve.wait_ge(pe_step, PE_STEPS * b + 4)
                nc.vector.tensor_scalar(m.q32[:, :], m.psT[1][:, 0:T], m.bq0[:, 0:1], float(D0) ** -0.5,
                                        ALU.add, ALU.mult).then_inc(dve_step, 1)
                dve.wait_ge(pe_step, PE_STEPS * b + 5)
                nc.vector.tensor_copy(m.v0[:, 8:FULL, :],
                                      m.psS[:, 8 * P:FULL * P].rearrange("p (c d) -> p c d", d=E))
                nc.vector.tensor_copy(m.v0[0:REST, FULL, :], m.psS[0:REST, FULL * P:SC * P]).then_inc(dve_step, 1)

                def mask_max(g, u, spans):
                    n = unit(b, g, u)
                    dve_mask_max(nc, dve, m, a, n, n, u % 2, lambda o, w: m.mask[:, u % TT, o:o + w], spans)

                with dve.Fori(0, NG) as g:
                    mask_max(g, 0, range(4))
                    for u in range(GU):
                        n = unit(b, g, u)
                        if u + 1 < GU:
                            mask_max(g, u + 1, range(0, 2))
                        copy_group(nc, dve, m, a, n, u % 2, 1, a.copied_dve)
                        if u + 1 < GU:
                            mask_max(g, u + 1, range(2, 4))
                        copy_group(nc, dve, m, a, n, u % 2, 3, a.copied_dve)
                        o = g * (GH * D0) + (u // TT) * D0
                        dve_take_out(nc, dve, m, a, n, u % 2, m.o0[:, u % TT, bass.ds(o, D0)],
                                     m.bv0[:, bass.ds(o, D0)], D0)

                dve.wait_ge(pe_step, PE_STEPS * b + 6)
                nc.vector.tensor_copy(m.oT[:, 0:T], m.psS[:, 0:T]).then_inc(dve_step, 1)
                dve.wait_ge(pe_step, PE_STEPS * b + 7)
                for t in range(TT):
                    ins = nc.vector.tensor_tensor(m.tmp[:, t, :], m.psM[:, t * P:(t + 1) * P], m.bo0[:, :], ALU.add)
                ins.then_inc(dve_step, 1)
                dve.wait_ge(dve_step, DVE_STEPS * b + 6)
                xs = m.x[:, bass.ds(b * TT, TT), :]
                nc.vector.scalar_tensor_tensor(xs, m.tmp[:, :, :], m.gates[:, 0:1], xs,
                                               ALU.mult, ALU.add).then_inc(batch_done, 1)


def chain(eng, sem):
    count = [0]

    def step(ins):
        count[0] += 1
        ins.then_inc(sem, 1)
        eng.wait_ge(sem, count[0])
    return step, count


def to_tokens(t):
    return t.unsqueeze(2)


def pe_turn_x(nc, pe, m, normed, turned):
    pe.wait_ge(normed, 1)
    for k in range(NT):
        ins = nc.tensor.transpose(m.psS[:, k * P:(k + 1) * P], m.xn[:, k, :], m.ident[:, :])
        if k in (NT // 2 - 1, NT - 1):
            ins.then_inc(turned, 1)


def block_route0(nc, m, s, dram):
    normed, turned, xt_act, xt_dve = (s.sem(f"r0_{n}") for n in ("normed", "turned", "xt_act", "xt_dve"))
    logits_done, exp_done, counts, counted, steps = (s.sem(f"r0_{n}") for n in ("logits", "exp", "counts", "counted", "steps"))
    BITS, STEPS = 30, 6
    with ExitStack() as stack:
        def sb(name, shape, dt=F32):
            return stack.enter_context(nc.sbuf_tensor(name, shape, dt))

        wg = sb("wg", [P, X0])
        probs, ge, flag, val = (sb(n, [P, NT, X0]) for n in ("r0_probs", "r0_ge", "r0_flag", "r0_val"))
        gt, eq, before = (sb(n, [P, NT, X0]) for n in ("r0_gt", "r0_eq", "r0_before"))
        geT = sb("r0_geT", [P, X0, NT])
        top, total = sb("r0_top", [P, NT]), sb("r0_total", [P, NT])
        count, need = sb("r0_count", [P, X0]), sb("r0_need", [P, X0])
        bit, cur, cand, take = (sb(n, [P, X0], I32) for n in ("r0_bit", "r0_cur", "r0_cand", "r0_take"))
        lg = m.psM[:, 0:NT * X0].rearrange("p (k e) -> p k e", e=X0)
        rank = lg
        sums = m.psO[:, 0:X0]
        curf, candf = cur[:, :].bitcast(F32), cand[:, :].bitcast(F32)

        def over_k(ap):
            return ap.unsqueeze(1).to_broadcast([P, NT, X0])

        def over_e(ap):
            return ap.unsqueeze(2).to_broadcast([P, NT, X0])

        with nc.Block() as block:
            @block.sync
            def _(sp):
                sp.dma_start(wg[:, :], dram["wg"]).then_inc(s.weights, 16)

            @block.tensor
            def _(pe):
                pe_turn_x(nc, pe, m, normed, turned)
                pe.wait_ge(xt_act, 1)
                pe.wait_ge(xt_dve, 1)
                pe.wait_ge(s.weights, 16)
                for k in range(NT):
                    ins = nc.tensor.matmul(lg[:, k, :], m.xT[:, k * P:(k + 1) * P], wg[:, :], start=True, stop=True)
                ins.then_inc(logits_done, 1)
                with pe.Fori(0, BITS) as i:
                    pe.wait_ge(counts, i + 1)
                    nc.tensor.matmul(sums, m.ones[:, :], count[:, :], start=True, stop=True).then_inc(counted, 1)
                pe.wait_ge(counts, BITS + 1)
                nc.tensor.matmul(sums, m.ones[:, :], count[:, :], start=True, stop=True).then_inc(counted, 1)
                pe.wait_ge(counts, BITS + 2)
                eq2, before2 = (v[:, :, :].rearrange("p k e -> p (k e)") for v in (eq, before))
                nc.tensor.matmul(m.psM[:, 0:NT * X0], m.below[:, :], eq2, start=True, stop=False)
                nc.tensor.matmul(m.psM[:, 0:NT * X0], m.ones[:, :], before2, start=False, stop=True).then_inc(counted, 1)

            @block.scalar
            def _(act):
                ln_scalar(nc, act, m, s, 1)
                act.wait_ge(turned, 1)
                nc.scalar.copy(m.xT[:, 0:TOK // 2], m.psS[:, 0:TOK // 2]).then_inc(xt_act, 1)
                act.wait_ge(steps, 2)
                nc.scalar.activation(probs[:, :, :], probs[:, :, :], ACT.Exp).then_inc(exp_done, 1)

            @block.vector
            def _(dve):
                ln_vector(nc, dve, m, s, m.x, m.xn, 1)
                nc.vector.memset(cur[:, :], 0).then_inc(normed, 1)
                nc.vector.memset(bit[:, :], 1 << (BITS - 1))
                dve.wait_ge(turned, 2)
                nc.vector.tensor_copy(m.xT[:, TOK // 2:TOK], m.psS[:, TOK // 2:TOK]).then_inc(xt_dve, 1)
                step, done = chain(dve, steps)
                dve.wait_ge(logits_done, 1)
                step(nc.vector.tensor_reduce(top[:, :], lg, AX.X, ALU.max))
                step(nc.vector.tensor_tensor(probs[:, :, :], lg, over_e(top[:, :]), ALU.subtract))
                dve.wait_ge(exp_done, 1)
                step(nc.vector.tensor_reduce(total[:, :], probs[:, :, :], AX.X, ALU.add))
                step(nc.vector.reciprocal(top[:, :], total[:, :]))
                step(nc.vector.tensor_tensor(probs[:, :, :], probs[:, :, :], over_e(top[:, :]), ALU.mult))
                first = done[0]
                with dve.Fori(0, BITS) as i:
                    now = i * STEPS + first
                    nc.vector.tensor_tensor(cand[:, :], cur[:, :], bit[:, :], ALU.bitwise_or).then_inc(steps, 1)
                    dve.wait_ge(steps, now + 1)
                    nc.vector.tensor_tensor(ge[:, :, :], probs[:, :, :], over_k(candf), ALU.is_ge).then_inc(steps, 1)
                    dve.wait_ge(steps, now + 2)
                    nc.vector.tensor_reduce(count[:, :], ge[:, :, :].rearrange("p k e -> p e k"), AX.X,
                                            ALU.add).then_inc(counts, 1)
                    nc.vector.tensor_scalar(bit[:, :], bit[:, :], 1, None, ALU.logical_shift_right).then_inc(steps, 1)
                    dve.wait_ge(counted, i + 1)
                    nc.vector.tensor_scalar(take[:, :], sums, float(CAP), None, ALU.is_ge).then_inc(steps, 1)
                    dve.wait_ge(steps, now + 4)
                    on_its_own(dve, s)
                    nc.vector.copy_predicated(cur[:, :], take[:, :], cand[:, :]).then_inc(steps, 2)
                    dve.wait_ge(steps, now + STEPS)
                    on_its_own(dve, s)
                done[0] = first + BITS * STEPS
                step(nc.vector.tensor_tensor(gt[:, :, :], probs[:, :, :], over_k(curf), ALU.is_gt))
                step(nc.vector.tensor_tensor(eq[:, :, :], probs[:, :, :], over_k(curf), ALU.is_equal))
                nc.vector.tensor_reduce(count[:, :], gt[:, :, :].rearrange("p k e -> p e k"), AX.X,
                                        ALU.add).then_inc(counts, 1)
                step(nc.vector.memset(before[:, 0, :], 0.0))
                for k in range(NT - 1):
                    step(nc.vector.tensor_tensor(before[:, k + 1, :], before[:, k, :], eq[:, k, :], ALU.add))
                nc.vector.memset(flag[:, :, :], 0.0).then_inc(counts, 1)
                dve.wait_ge(counted, BITS + 1)
                step(nc.vector.tensor_scalar(need[:, :], sums, -1.0, float(CAP), ALU.mult, ALU.add))
                dve.wait_ge(counted, BITS + 2)
                dve.wait_ge(counts, BITS + 2)
                step(nc.vector.tensor_tensor(flag[:, :, :], rank, over_k(need[:, :]), ALU.is_lt))
                step(nc.vector.tensor_tensor(flag[:, :, :], flag[:, :, :], eq[:, :, :], ALU.mult))
                step(nc.vector.tensor_tensor(flag[:, :, :], flag[:, :, :], gt[:, :, :], ALU.add))
                step(nc.vector.tensor_reduce(top[:, :], flag[:, :, :], AX.X, ALU.max))
                step(nc.vector.tensor_scalar(top[:, :], top[:, :], -1.0, 1.0, ALU.mult, ALU.add))
                step(nc.vector.tensor_tensor(flag[:, :, :], flag[:, :, :], over_e(top[:, :]), ALU.add))
                step(nc.vector.tensor_tensor(val[:, :, :], probs[:, :, :], flag[:, :, :], ALU.mult))
                step(nc.vector.scalar_tensor_tensor(val[:, :, :], flag[:, :, :], -1.0, val[:, :, :], ALU.add, ALU.add))
                step(nc.vector.tensor_reduce(top[:, :], val[:, :, :], AX.X, ALU.max))
                step(nc.vector.tensor_tensor(flag[:, :, :], val[:, :, :], over_e(top[:, :]), ALU.is_equal))
                step(nc.vector.tensor_tensor(flag[:, :, :], flag[:, :, :], over_k(m.weight8[:, :]), ALU.mult))
                step(nc.vector.tensor_reduce(top[:, :], flag[:, :, :], AX.X, ALU.max))
                step(nc.vector.tensor_tensor(flag[:, :, :], flag[:, :, :], over_e(top[:, :]), ALU.is_equal))
                nc.vector.tensor_tensor(m.gate[:, :, :], flag[:, :, :], probs[:, :, :], ALU.mult)


def block_experts0(nc, m, s, dram):
    hidden = s.sem("e0_hidden")
    gelu_done, out_full, added = (s.from_one(f"e0_{n}") for n in ("gelu_done", "out_full", "added"))
    KB = BANK // P
    with ExitStack() as stack:
        def sb(name, shape, dt=F32):
            return stack.enter_context(nc.sbuf_tensor(name, shape, dt))

        w1, w2 = sb("w1", [P, X0, F0]), sb("w2", [P, X0, F0 // P, E])
        act_out = sb("e0_gelu", [P, 2, 2 * BANK])
        acc = sb("e0_acc", [P, NT, E])
        loaded, zeroed = s.sem("e0_loaded"), s.sem("e0_zeroed")
        prime(nc, s)

        def turn(blk, e):
            return blk * X0 + e

        with nc.Block() as block:
            @block.sync
            def _(sp):
                sp.dma_start(w1[:, :, :], dram["w1"].rearrange("e d f -> d e f")).then_inc(loaded, 16)
                sp.dma_start(w2[:, :, :, :], dram["w2"].rearrange("e (h f) d -> f e h d", f=P)).then_inc(loaded, 16)

            @block.tensor
            def _(pe):
                pe.wait_ge(loaded, 32)

                def up(blk, e):
                    n = turn(blk, e)
                    if e >= 2:
                        pe.wait_ge(gelu_done, 1 + n - 1)
                    else:
                        pe.wait_ge(gelu_done, 1 + blk * X0)
                    for h in range(2):
                        o = (2 * (e % 2) + h) * BANK
                        ins = nc.tensor.matmul(m.psS[:, o:o + BANK], w1[:, e, h * P:(h + 1) * P],
                                               m.xT[:, bass.ds(blk * BANK, BANK)], start=True, stop=True)
                    ins.then_inc(hidden, 1)

                def down(blk, e):
                    n = turn(blk, e)
                    pe.wait_ge(gelu_done, 1 + n + 1)
                    if e >= 2:
                        pe.wait_ge(added, 1 + n - 1)
                    else:
                        pe.wait_ge(added, 1 + blk * X0)
                    for k in range(KB):
                        for h in range(2):
                            o = h * BANK + k * P
                            ins = nc.tensor.matmul(m.psT[e % 2][:, k * P:(k + 1) * P], act_out[:, e % 2, o:o + P],
                                                   w2[:, e, h, :], start=(h == 0), stop=(h == 1))
                    ins.then_inc(out_full, 1)

                with pe.Fori(0, TOK // BANK) as blk:
                    up(blk, 0)
                    for e in range(X0):
                        if e + 1 < X0:
                            up(blk, e + 1)
                        down(blk, e)

            @block.scalar
            def _(act):
                with act.Fori(0, TOK // BANK) as blk:
                    for e in range(X0):
                        n = turn(blk, e)
                        act.wait_ge(hidden, n + 1)
                        if e >= 2:
                            act.wait_ge(out_full, 1 + n - 1)
                        else:
                            act.wait_ge(out_full, 1 + blk * X0)
                        o = 2 * (e % 2) * BANK
                        nc.scalar.activation(act_out[:, e % 2, :], m.psS[:, o:o + 2 * BANK], ACT.Gelu).then_inc(gelu_done, 1)

            @block.vector
            def _(dve):
                nc.vector.memset(acc[:, :, :], 0.0).then_inc(zeroed, 1)
                dve.wait_ge(zeroed, 1)
                with dve.Fori(0, TOK // BANK) as blk:
                    for e in range(X0):
                        n = turn(blk, e)
                        dve.wait_ge(out_full, 1 + n + 1)
                        dve.wait_ge(added, 1 + n)
                        for k in range(KB):
                            tile = acc[:, bass.ds(blk * KB + k, 1), :].rearrange("p a d -> p (a d)")
                            ins = nc.vector.scalar_tensor_tensor(
                                tile, m.psT[e % 2][:, k * P:(k + 1) * P],
                                m.gate[:, bass.ds(blk * KB + k, 1), e:e + 1].rearrange("p a e -> p (a e)"), tile,
                                ALU.mult, ALU.add)
                        ins.then_inc(added, 1)
                dve.wait_ge(added, 1 + X0 * TOK // BANK)
                nc.vector.scalar_tensor_tensor(m.x[:, :, :], acc[:, :, :], m.gates[:, 1:2], m.x[:, :, :],
                                               ALU.mult, ALU.add).then_inc(zeroed, 1)
                dve.wait_ge(zeroed, 2)


def block_norm1(nc, m, s, dram):
    with nc.Block() as block:
        @block.scalar
        def _(act):
            ln_scalar(nc, act, m, s, 2)
            ln_scalar(nc, act, m, s, 3)

        @block.vector
        def _(dve):
            ln_vector(nc, dve, m, s, m.x, m.xn, 2)
            ln_vector(nc, dve, m, s, m.xn, m.xn, 3)


def block_attention1(nc, m, s, dram):
    a = attention_sems(s, "a1")
    ctx_ready, loaded = s.sem("a1_ctx_ready"), s.sem("a1_loaded")
    pe_step, act_step, dve_step = (s.sem(f"a1_{e}_step") for e in ("pe", "act", "dve"))
    batch_done = s.from_one("a1_batch_done")
    weight_ready = [s.sem(f"a1_weight_ready{j}") for j in range(2)]
    PE_STEPS, ACT_STEPS, DVE_STEPS = 4, 3, 12
    KEY, VALUE, SCORE = 0, 1, 2
    WV, BK, BQ, HW = 2 * P, 2 * P + D1, 2 * P + D1 + 1, 2 * P + D1 + 2
    HP = H // 2

    def use(b, h, kind):
        return b * (4 * H) + h * 4 + kind

    def unit(b, i, u):
        return b * UB + i * 4 + u

    with ExitStack() as stack:
        def sb(name, shape, dt=F32):
            return stack.enter_context(nc.sbuf_tensor(name, shape, dt))

        mask, position = sb("a1_mask", [P, S]), sb("position", [P, S])
        lens, lensf = sb("lens", [P, B], I32), sb("lensf", [P, B])
        gain, shift = sb("ln_g", [P, 1]), sb("ln_b", [P, 1])
        wo, bv, bo = sb("wo1", [P, 8, E]), sb("bv1", [P, H * D1]), sb("bo1", [P, E])
        head_w = sb("head_w", [P, 2, HW])
        keys = sb("keys1", [P, S])
        q_rot, q_both = sb("q_rot", [P, T]), sb("q_both", [P, T])
        values = sb("values1", [P, 2, SC, D1])
        out = sb("out1", [P, TT, H * D1])
        stats, mv = sb("a1_stats", [P, SC, 6]), sb("a1_mv", [P, SC, 2])
        var, rstd = sb("a1_var", [P, SC]), sb("a1_rstd", [P, SC])
        normed = sb("a1_normed", [P, SC, E])
        prime(nc, s)

        with nc.Block() as block:
            @block.sync
            def _(sp):
                for dst, src in ((position[:, :], dram["position"].to_broadcast([P, S])),
                                 (lens[:, :], dram["lens"].to_broadcast([P, B])), (gain[:, :], dram["ln_g"]),
                                 (shift[:, :], dram["ln_b"]), (wo[:, :, :], dram["wo1"]),
                                 (bv[:, :], dram["bv1"].to_broadcast([P, H * D1])),
                                 (bo[:, :], dram["bo1"].to_broadcast([P, E]))):
                    sp.dma_start(dst, src).then_inc(loaded, 16)

                for j in range(2):
                    sp.dma_start(head_w[:, j, :], dram["head_w"][j, :, :]).then_inc(weight_ready[j], 16)
                with sp.Fori(0, B) as b:
                    sp.wait_ge(batch_done, 1 + b)
                    sp.dma_start(m.ctx[:, 0:FULL, :], dram["ctx"][bass.ds(b, 1), 0:FULL * P, :]
                                 .rearrange("a (c p) d -> p (a c) d", p=P)).then_inc(ctx_ready, 16)
                    sp.dma_start(m.ctx[0:REST, FULL, :], dram["ctx"][bass.ds(b, 1), FULL * P:S, :]
                                 .rearrange("a p d -> p (a d)")).then_inc(ctx_ready, 16)

                    def next_weights(i, to):
                        for j in range(2):
                            sp.wait_ge(a.bank_full, 4 * (use(b, i * 2 + j, VALUE)) + 4)
                            sp.dma_start(head_w[:, j, :], dram["head_w"][bass.ds(to + j, 1), :, :]
                                         .rearrange("a p w -> p (a w)")).then_inc(weight_ready[j], 16)

                    with sp.Fori(0, HP - 1) as i:
                        next_weights(i, i * 2 + 2)
                    next_weights(HP - 1, 0)
                for j in range(2):
                    sp.wait_ge(weight_ready[j], 16 * (1 + B * HP))

            @block.tensor
            def _(pe):
                pe.wait_ge(loaded, 16 * 7)
                with pe.Fori(0, B) as b:
                    pe.wait_ge(batch_done, 1 + b)
                    pe.wait_ge(dve_step, DVE_STEPS * b + 7)
                    for c in range(SC):
                        r = rows(c)
                        ins = nc.tensor.transpose(m.psS[:, c * P:c * P + r], normed[0:r, c, :], m.ident[0:r, 0:r])
                    ins.then_inc(pe_step, 1)
                    for t in range(TT):
                        ins = nc.tensor.transpose(m.psT[0][:, t * P:(t + 1) * P], m.xb[:, t, :], m.ident[:, :])
                    ins.then_inc(pe_step, 1)
                    pe.wait_ge(act_step, ACT_STEPS * b + 2)
                    pe.wait_ge(dve_step, DVE_STEPS * b + 9)
                    on_its_own(pe, s)

                    def project(j, h, pair):
                        pe.wait_ge(weight_ready[j], 16 * (pair + 1))
                        for q, (o, w) in enumerate(SPANS):
                            pe.wait_ge(a.bank_free[q], 1 + use(b, h, KEY))
                            nc.tensor.matmul(m.psS[:, o:o + w], head_w[:, j, 0:P], m.ctxT[:, o:o + w],
                                             start=True, stop=True).then_inc(a.bank_full, 1)
                        for q, chunks in enumerate((range(0, 8), range(8, SC))):
                            pe.wait_ge(a.bank_free[q], 1 + use(b, h, VALUE))
                            for c in chunks:
                                r = rows(c)
                                o = q * BANK + (c - 8 * q) * D1
                                ins = nc.tensor.matmul(m.psS[0:r, o:o + D1], m.ctxT[:, c * P:c * P + r],
                                                       head_w[:, j, WV:WV + D1], start=True, stop=True)
                            ins.then_inc(a.bank_full, 1)
                        pe.wait_ge(a.bank_free[2], 1 + use(b, h, VALUE))
                        nc.tensor.matmul(m.psS[:, 2 * BANK:2 * BANK + T], head_w[:, j, P:2 * P], m.xT[:, 0:T],
                                         start=True, stop=True).then_inc(a.bank_full, 1)

                    def double_query(h):
                        pe.wait_ge(a.bank_free[2], 1 + use(b, h, VALUE) + 1)
                        pe.wait_ge(a.bank_free[3], 1 + use(b, h, VALUE))
                        nc.tensor.matmul(m.psS[:, 3 * BANK:3 * BANK + T], m.fold[:, :], q_rot[:, :],
                                         start=True, stop=True).then_inc(a.bank_full, 1)

                    def scores(n, h, t):
                        if t == 0:
                            for q in (3, 1, 0):
                                pe.wait_ge(a.bank_free[q], 1 + use(b, h, SCORE))
                        pe_scores(nc, pe, m, a, use(b, h, SCORE + t), q_both[:, t * P:(t + 1) * P],
                                  lambda o, w: keys[:, o:o + w])

                    def pair(i, last):
                        for u in range(4):
                            n, h, t = unit(b, i, u), i * 2 + u // 2, u % 2
                            j = (u // 2 + 1) % 2
                            more = not (last and u >= 2)
                            if t == 0:
                                scores(n + 1, h, 1)
                                if more:
                                    project(j, h + 1, b * HP + i + u // 2)
                            elif more or u < 3:
                                scores(n + 1, h + 1, 0)
                            pe_transpose(nc, pe, m, a, n, u % 2)
                            if t == 0 and more:
                                double_query(h + 1)
                            pe_values(nc, pe, m, a, n, u % 2, lambda c, r: values[0:r, u // 2, c, :], D1)

                    project(0, 0, b * HP)
                    double_query(0)
                    scores(unit(b, 0, 0), 0, 0)
                    on_its_own(pe, s)
                    with pe.Fori(0, HP - 1) as i:
                        pair(i, False)
                    pair(HP - 1, True)

                    pe.wait_ge(a.out_taken, 1 + UB * (b + 1))
                    for t in range(TT):
                        for c in range(8):
                            o = (t * 8 + c) * P
                            ins = nc.tensor.transpose(m.psS[:, o:o + P], out[:, t, c * P:(c + 1) * P], m.ident[:, :])
                    ins.then_inc(pe_step, 1)
                    pe.wait_ge(act_step, ACT_STEPS * b + 3)
                    pe.wait_ge(dve_step, DVE_STEPS * b + 10)
                    for t in range(TT):
                        for c in range(8):
                            o = (t * 8 + c) * P
                            ins = nc.tensor.matmul(m.psM[:, t * P:(t + 1) * P], m.oT[:, o:o + P], wo[:, c, :],
                                                   start=(c == 0), stop=(c == 7))
                    ins.then_inc(pe_step, 1)

            @block.scalar
            def _(act):
                act.wait_ge(loaded, 16 * 7)
                with act.Fori(0, B) as b:
                    act.wait_ge(dve_step, DVE_STEPS * b + 4)
                    nc.scalar.activation(var[:, :], var[:, :], ACT.Sqrt).then_inc(act_step, 1)
                    act.wait_ge(pe_step, PE_STEPS * b + 1)
                    nc.scalar.activation(m.ctxT[:, 0:2 * BANK], m.psS[:, 0:2 * BANK], ACT.Identity, bias=shift[:, :],
                                         scale=gain[:, :]).then_inc(act_step, 1)

                    def take_values(h, j):
                        act.wait_ge(a.bank_full, 4 * use(b, h, VALUE) + 1)
                        nc.scalar.copy(values[:, j, 0:8, :],
                                       m.psS[:, 0:BANK].rearrange("p (c d) -> p c d", d=D1)).then_inc(a.bank_free[0], 1)
                        act.wait_ge(a.bank_full, 4 * use(b, h, VALUE) + 2)
                        nc.scalar.copy(values[:, j, 8:FULL, :],
                                       m.psS[:, BANK:BANK + 4 * D1].rearrange("p (c d) -> p c d", d=D1))
                        nc.scalar.copy(values[0:REST, j, FULL, :],
                                       m.psS[0:REST, BANK + 4 * D1:BANK + 5 * D1]).then_inc(a.bank_free[1], 1)

                    def take_query(h):
                        act.wait_ge(a.bank_full, 4 * use(b, h, VALUE) + 4)
                        nc.scalar.activation(q_both[:, :], m.psS[:, 3 * BANK:3 * BANK + T], ACT.Copy,
                                             scale=float(D1) ** -0.5).then_inc(a.bank_free[3], 1)

                    def pair(i, last):
                        for u in range(4):
                            n, h, t = unit(b, i, u), i * 2 + u // 2, u % 2
                            more = not (last and u >= 2)
                            if t == 0:
                                act_exp(nc, act, m, a, n + 1, 1)
                                if more:
                                    take_values(h + 1, (u // 2 + 1) % 2)
                            copy_group(nc, act, m, a, n, u % 2, 0, a.copied_act)
                            copy_group(nc, act, m, a, n, u % 2, 2, a.copied_act)
                            if t == 0 and more:
                                take_query(h + 1)
                            if t == 1 and (more or u < 3):
                                act_exp(nc, act, m, a, n + 1, 0)

                    take_values(0, 0)
                    take_query(0)
                    act_exp(nc, act, m, a, unit(b, 0, 0), 0)
                    with act.Fori(0, HP - 1) as i:
                        pair(i, False)
                    pair(HP - 1, True)
                    act.wait_ge(pe_step, PE_STEPS * b + 3)
                    nc.scalar.copy(m.oT[:, 0:1024], m.psS[:, 0:1024]).then_inc(act_step, 1)

            @block.vector
            def _(dve):
                dve.wait_ge(loaded, 16 * 7)
                nc.vector.tensor_copy(lensf[:, :], lens[:, :])
                nc.vector.memset(mv[:, :, :], 0.0).then_inc(dve_step, 1)
                dve.wait_ge(dve_step, 1)
                with dve.Fori(0, B) as b:
                    base = DVE_STEPS * b + 1
                    dve.wait_ge(ctx_ready, 32 * (b + 1))
                    for c in range(SC):
                        ins = nc.vector.bn_stats(stats[0:rows(c), c, :], m.ctx[0:rows(c), c, :])
                    ins.then_inc(dve_step, 1)
                    dve.wait_ge(dve_step, base + 1)
                    on_its_own(dve, s)
                    for c in range(SC):
                        ins = nc.vector.bn_aggr(mv[0:rows(c), c, :], stats[0:rows(c), c, :])
                    ins.then_inc(dve_step, 1)
                    dve.wait_ge(dve_step, base + 2)
                    nc.vector.tensor_scalar(var[:, :], mv[:, :, 1], EPS, None, ALU.add).then_inc(dve_step, 1)
                    dve.wait_ge(act_step, ACT_STEPS * b + 1)
                    nc.vector.reciprocal(rstd[:, :], var[:, :]).then_inc(dve_step, 1)
                    dve.wait_ge(dve_step, base + 4)
                    nc.vector.tensor_copy(m.xb[:, :, :], m.xn[:, bass.ds(b * TT, TT), :]).then_inc(dve_step, 1)
                    for c in range(SC):
                        r = rows(c)
                        ins = nc.vector.tensor_scalar(normed[0:r, c, :], m.ctx[0:r, c, :], mv[0:r, c, 0:1],
                                                      rstd[0:r, c:c + 1], ALU.subtract, ALU.mult)
                    ins.then_inc(dve_step, 1)
                    nc.vector.tensor_scalar(mask[:, :], position[:, :], lensf[:, bass.ds(b, 1)], NEG,
                                            ALU.is_ge, ALU.mult).then_inc(dve_step, 1)
                    dve.wait_ge(pe_step, PE_STEPS * b + 1)
                    nc.vector.tensor_scalar(m.ctxT[:, 2 * BANK:S], m.psS[:, 2 * BANK:S], gain[:, :], shift[:, :],
                                            ALU.mult, ALU.add)
                    dve.wait_ge(pe_step, PE_STEPS * b + 2)
                    nc.vector.tensor_scalar(m.xT[:, 0:T], m.psT[0][:, 0:T], gain[:, :], shift[:, :],
                                            ALU.mult, ALU.add).then_inc(dve_step, 1)
                    dve.wait_ge(dve_step, base + 8)

                    def rotate(h, j):
                        for q, (o, w) in enumerate(SPANS):
                            dve.wait_ge(a.bank_full, 4 * use(b, h, KEY) + q + 1)
                            nc.vector.scalar_tensor_tensor(keys[:, o:o + w], m.psS[:, o:o + w], head_w[:, j, BK:BK + 1],
                                                           m.cos_sin[:, o:o + w], ALU.add,
                                                           ALU.mult).then_inc(a.bank_free[q], 1)
                        dve.wait_ge(a.bank_full, 4 * use(b, h, VALUE) + 3)
                        nc.vector.scalar_tensor_tensor(q_rot[:, :], m.psS[:, 2 * BANK:2 * BANK + T],
                                                       head_w[:, j, BQ:BQ + 1], m.cos_sin[:, 0:T], ALU.add,
                                                       ALU.mult).then_inc(a.bank_free[2], 1)

                    def mask_max(n, h, t, spans):
                        dve_mask_max(nc, dve, m, a, n, use(b, h, SCORE + t), t, lambda o, w: mask[:, o:o + w], spans)

                    def pair(i, last):
                        for u in range(4):
                            n, h, t = unit(b, i, u), i * 2 + u // 2, u % 2
                            more = not (last and u >= 2)
                            if t == 0:
                                mask_max(n + 1, h, 1, range(4))
                                if more:
                                    rotate(h + 1, (u // 2 + 1) % 2)
                            elif more or u < 3:
                                mask_max(n + 1, h + 1, 0, range(2))
                            copy_group(nc, dve, m, a, n, u % 2, 1, a.copied_dve)
                            if t == 1 and (more or u < 3):
                                mask_max(n + 1, h + 1, 0, range(2, 4))
                            copy_group(nc, dve, m, a, n, u % 2, 3, a.copied_dve)
                            dve_take_out(nc, dve, m, a, n, u % 2, out[:, t, bass.ds(h * D1, D1)],
                                         bv[:, bass.ds(h * D1, D1)], D1)

                    rotate(0, 0)
                    mask_max(unit(b, 0, 0), 0, 0, range(4))
                    with dve.Fori(0, HP - 1) as i:
                        pair(i, False)
                    pair(HP - 1, True)

                    dve.wait_ge(pe_step, PE_STEPS * b + 3)
                    nc.vector.tensor_copy(m.oT[:, 1024:2048], m.psS[:, 1024:2048]).then_inc(dve_step, 1)
                    dve.wait_ge(pe_step, PE_STEPS * b + 4)
                    for t in range(TT):
                        ins = nc.vector.tensor_tensor(m.tmp[:, t, :], m.psM[:, t * P:(t + 1) * P], bo[:, :], ALU.add)
                    ins.then_inc(dve_step, 3)
                    dve.wait_ge(dve_step, base + 12)
                    xs = m.x[:, bass.ds(b * TT, TT), :]
                    nc.vector.scalar_tensor_tensor(xs, m.tmp[:, :, :], m.gates[:, 2:3], xs,
                                                   ALU.mult, ALU.add).then_inc(batch_done, 1)


def block_route1(nc, m, s, dram):
    normed, turned, xt_act, xt_dve = (s.sem(f"r1_{n}") for n in ("normed", "turned", "xt_act", "xt_dve"))
    logits_done, sig_done, steps, loaded = (s.sem(f"r1_{n}") for n in ("logits", "sig", "steps", "loaded"))
    with ExitStack() as stack:
        def sb(name, shape, dt=F32):
            return stack.enter_context(nc.sbuf_tensor(name, shape, dt))

        wg, bias = sb("r1_wg", [P, X1]), sb("r1_bias", [P, X1])
        score, masked, above, equal, seen = (sb(f"r1_{n}", [P, NT, X1]) for n in
                                             ("score", "masked", "above", "equal", "seen"))
        best = sb("r1_best", [P, NT, GR])
        first, level = sb("r1_first", [P, NT, GR, GR]), sb("r1_level", [P, NT, GR, GR])
        keep, top8 = sb("r1_keep", [P, NT, GR]), sb("r1_top8", [P, NT, 8])
        total = sb("r1_total", [P, NT])
        lg = m.psM[:, :].rearrange("p (k e) -> p k e", e=X1)

        def over_e(ap):
            return ap.to_broadcast([P, NT, X1])

        with nc.Block() as block:
            @block.sync
            def _(sp):
                sp.dma_start(wg[:, :], dram["wg1"]).then_inc(loaded, 16)
                sp.dma_start(bias[:, :], dram["expert_bias"].to_broadcast([P, X1])).then_inc(loaded, 16)

            @block.tensor
            def _(pe):
                pe_turn_x(nc, pe, m, normed, turned)
                pe.wait_ge(xt_act, 1)
                pe.wait_ge(xt_dve, 1)
                pe.wait_ge(loaded, 32)
                for k in range(NT):
                    ins = nc.tensor.matmul(lg[:, k, :], m.xT[:, k * P:(k + 1) * P], wg[:, :], start=True, stop=True)
                ins.then_inc(logits_done, 1)

            @block.scalar
            def _(act):
                ln_scalar(nc, act, m, s, 4)
                act.wait_ge(turned, 1)
                nc.scalar.copy(m.xT[:, 0:TOK // 2], m.psS[:, 0:TOK // 2]).then_inc(xt_act, 1)
                act.wait_ge(logits_done, 1)
                nc.scalar.activation(score[:, :, :], lg, ACT.Sigmoid).then_inc(sig_done, 1)

            @block.vector
            def _(dve):
                ln_vector(nc, dve, m, s, m.x, m.xn, 4)
                nc.vector.memset(total[:, :], 0.0).then_inc(normed, 1)
                dve.wait_ge(turned, 2)
                nc.vector.tensor_copy(m.xT[:, TOK // 2:TOK], m.psS[:, TOK // 2:TOK]).then_inc(xt_dve, 1)
                dve.wait_ge(sig_done, 1)
                dve.wait_ge(loaded, 32)
                step, _ = chain(dve, steps)
                step(nc.vector.tensor_tensor(masked[:, :, :], score[:, :, :],
                                             bias[:, :].unsqueeze(1).to_broadcast([P, NT, X1]), ALU.add))
                step(nc.vector.tensor_reduce(best[:, :, :], masked[:, :, :].rearrange("p k (g i) -> p k g i", g=GR),
                                             AX.X, ALU.max))
                four = [P, NT, GR, GR]
                other, own = best[:, :, :].unsqueeze(2).to_broadcast(four), best[:, :, :].unsqueeze(3).to_broadcast(four)
                step(nc.vector.tensor_tensor(first[:, :, :, :], other, own, ALU.is_gt))
                step(nc.vector.tensor_tensor(level[:, :, :, :], other, own, ALU.is_equal))
                step(nc.vector.tensor_tensor(level[:, :, :, :], level[:, :, :, :],
                                             m.earlier[:, :, :].unsqueeze(1).to_broadcast(four), ALU.mult))
                step(nc.vector.tensor_tensor(first[:, :, :, :], first[:, :, :, :], level[:, :, :, :], ALU.add))
                step(nc.vector.tensor_reduce(keep[:, :, :], first[:, :, :, :], AX.X, ALU.add))
                step(nc.vector.tensor_scalar(keep[:, :, :], keep[:, :, :], float(KEEP), None, ALU.is_lt))
                grouped = masked[:, :, :].rearrange("p k (g i) -> p k g i", g=GR)
                step(nc.vector.tensor_tensor(grouped, grouped,
                                             keep[:, :, :].unsqueeze(3).to_broadcast([P, NT, GR, X1 // GR]), ALU.mult))
                for k in range(NT):
                    ins = nc.vector.max(top8[:, k, :], masked[:, k, :])
                step(ins)
                least = over_e(top8[:, :, TOP - 1:TOP])
                step(nc.vector.tensor_tensor(above[:, :, :], masked[:, :, :], least, ALU.is_gt))
                step(nc.vector.tensor_tensor(equal[:, :, :], masked[:, :, :], least, ALU.is_equal))
                step(nc.vector.tensor_reduce(total[:, :], above[:, :, :], AX.X, ALU.add))
                step(nc.vector.tensor_tensor_scan(seen[:, :, :].rearrange("p k e -> p (k e)"), m.scanreset[:, :],
                                                  equal[:, :, :].rearrange("p k e -> p (k e)"), 0.0,
                                                  ALU.mult, ALU.add))
                step(nc.vector.tensor_tensor(seen[:, :, :], seen[:, :, :], over_e(total[:, :].unsqueeze(2)), ALU.add))
                step(nc.vector.scalar_tensor_tensor(equal[:, :, :], seen[:, :, :], float(TOP), equal[:, :, :],
                                                    ALU.is_le, ALU.mult))
                step(nc.vector.tensor_tensor(above[:, :, :], above[:, :, :], equal[:, :, :], ALU.add))
                step(nc.vector.tensor_tensor(score[:, :, :], score[:, :, :], above[:, :, :], ALU.mult))
                step(nc.vector.tensor_reduce(total[:, :], score[:, :, :], AX.X, ALU.add))
                step(nc.vector.tensor_scalar(total[:, :], total[:, :], 1e-20, None, ALU.add))
                step(nc.vector.reciprocal(total[:, :], total[:, :]))
                step(nc.vector.tensor_tensor(score[:, :, :], score[:, :, :], over_e(total[:, :].unsqueeze(2)), ALU.mult))
                step(nc.vector.tensor_scalar(m.combine[:, :, :], score[:, :, :], SCALE1, None, ALU.mult))


def block_experts1(nc, m, s, dram):
    N = PAIRS + 1
    KB = BANK // P
    loaded, weights_turned, weights_ready, mixed = (s.sem(f"e1_{n}") for n in ("loaded", "turned", "ready", "mixed"))
    projected, silu_done = s.sem("e1_projected"), s.sem("e1_silu")
    inner_done, out_full, added = (s.from_one(f"e1_{n}") for n in ("inner_done", "out_full", "added"))
    with ExitStack() as stack:
        def sb(name, shape, dt=F32):
            return stack.enter_context(nc.sbuf_tensor(name, shape, dt))

        wgate, wup, wdown = (sb(n, [P, N, P]) for n in ("e1_gate", "e1_up", "e1_down"))
        spread = sb("e1_spread", [X1 + 1, N, P])
        cT = sb("e1_cT", [X1 + 1, TOK])
        silu, prod, inner = (sb(f"e1_{n}", [P, 2, BANK]) for n in ("silu", "prod", "inner"))
        prime(nc, s)

        def turn(blk, p):
            return blk * N + p

        banks = [(m.psS[:, 0:BANK], m.psS[:, BANK:2 * BANK], m.psT[0][:, :]),
                 (m.psS[:, 2 * BANK:3 * BANK], m.psS[:, 3 * BANK:4 * BANK], m.psT[1][:, :])]

        with nc.Block() as block:
            @block.sync
            def _(sp):
                for dst, src in ((wgate, dram["e1_gate"]), (wup, dram["e1_up"]), (wdown, dram["e1_down"]), (spread, dram["spread"])):
                    sp.dma_start(dst[:, :, :], src).then_inc(loaded, 16)

            @block.tensor
            def _(pe):
                pe.wait_ge(loaded, 64)
                for k in range(NT):
                    ins = nc.tensor.transpose(m.psS[0:X1, k * P:(k + 1) * P], m.combine[:, k, :], m.ident[:, :])
                ins.then_inc(weights_turned, 1)
                pe.wait_ge(weights_ready, 2)

                def up(blk, p):
                    n = turn(blk, p)
                    gate, upper, weight = banks[p % 2]
                    if p >= 2:
                        pe.wait_ge(inner_done, 1 + n - 1)
                    else:
                        pe.wait_ge(inner_done, 1 + blk * N)
                    x = m.xT[:, bass.ds(blk * BANK, BANK)]
                    nc.tensor.matmul(gate, wgate[:, p, :], x, start=True, stop=True)
                    nc.tensor.matmul(upper, wup[:, p, :], x, start=True, stop=True)
                    nc.tensor.matmul(weight, spread[:, p, :], cT[:, bass.ds(blk * BANK, BANK)],
                                     start=True, stop=True).then_inc(projected, 1)

                def down(blk, p):
                    pe.wait_ge(inner_done, 1 + turn(blk, p) + 1)
                    if p == 0:
                        pe.wait_ge(added, 1 + blk)
                    for k in range(KB):
                        ins = nc.tensor.matmul(m.psO[:, k * P:(k + 1) * P], inner[:, p % 2, k * P:(k + 1) * P],
                                               wdown[:, p, :], start=(p == 0 and k == 0), stop=(p == N - 1),
                                               skip_group_check=True)
                    ins.then_inc(out_full, 1)

                with pe.Fori(0, TOK // BANK) as blk:
                    up(blk, 0)
                    for p in range(N):
                        if p + 1 < N:
                            up(blk, p + 1)
                        down(blk, p)

            @block.scalar
            def _(act):
                act.wait_ge(weights_turned, 1)
                nc.scalar.copy(cT[0:X1, :], m.psS[0:X1, :]).then_inc(weights_ready, 1)
                with act.Fori(0, TOK // BANK) as blk:
                    for p in range(N):
                        n = turn(blk, p)
                        act.wait_ge(projected, n + 1)
                        nc.scalar.activation(silu[:, p % 2, :], banks[p % 2][0], ACT.Silu).then_inc(silu_done, 1)

            @block.vector
            def _(dve):
                nc.vector.memset(cT[X1:X1 + 1, :], 1.0).then_inc(weights_ready, 1)
                with dve.Fori(0, TOK // BANK) as blk:
                    for p in range(N):
                        n = turn(blk, p)
                        dve.wait_ge(silu_done, n + 1)
                        nc.vector.tensor_tensor(prod[:, p % 2, :], banks[p % 2][1], silu[:, p % 2, :],
                                                ALU.mult).then_inc(mixed, 1)
                        dve.wait_ge(mixed, n + 1)
                        if p >= 2:
                            dve.wait_ge(out_full, 1 + n - 1)
                        else:
                            dve.wait_ge(out_full, 1 + blk * N)
                        nc.vector.tensor_tensor(inner[:, p % 2, :], banks[p % 2][2], prod[:, p % 2, :],
                                                ALU.mult).then_inc(inner_done, 1)
                    dve.wait_ge(out_full, 1 + turn(blk, N))
                    xs = m.x[:, bass.ds(blk * KB, KB), :]
                    nc.vector.scalar_tensor_tensor(xs, m.psO[:, :].rearrange("p (k d) -> p k d", d=E),
                                                   m.gates[:, 3:4], xs, ALU.mult, ALU.add).then_inc(added, 1)
                dve.wait_ge(added, 1 + TOK // BANK)


def build(nc, dram):
    with ExitStack() as stack:
        def sb(name, shape, dt=F32):
            return stack.enter_context(nc.sbuf_tensor(name, shape, dt))

        def sem(name):
            return stack.enter_context(nc.semaphore(name))

        to_prime = []

        def from_one(name):
            to_prime.append(sem(name))
            return to_prime[-1]

        m, s = Named(), Named()
        m.s = s
        s.sem, s.from_one, s.to_prime = sem, from_one, to_prime
        s.load, s.ln, s.ln_sqrt, s.tanh = (sem(n) for n in ("load", "ln", "ln_sqrt", "tanh"))
        s.stored, s.passed, s.weights = (sem(n) for n in ("stored", "passed", "weights"))
        m.x, m.xn, m.xT = sb("x", [P, NT, E]), sb("xn", [P, NT, E]), sb("xT", [P, TOK])
        m.stats, m.mv = sb("stats", [P, NT, 6]), sb("mv", [P, NT, 2])
        m.var, m.rstd = sb("var", [P, NT]), sb("rstd", [P, NT])
        m.ident, m.fold, m.below, m.ones = (sb(n, [P, P]) for n in ("ident", "fold", "below", "ones"))
        m.cos_sin = sb("cos_sin", [P, S])
        m.earlier, m.weight8 = sb("earlier", [P, GR, GR]), sb("weight8", [P, X0])
        m.headmask, m.scanreset = sb("headmask", [P, 4]), sb("scanreset", [P, NT * X1])
        m.gates = sb("gates", [P, 4])
        m.probs, m.probsT = sb("probs", [P, 2, S]), sb("probsT", [P, 2, SC, P])
        m.max4, m.negmax = sb("max4", [P, 2, 4]), sb("negmax", [P, 2])
        m.sums, m.rsum = sb("sums", [P, 2]), sb("rsum", [P, 2])
        m.psS = stack.enter_context(nc.psum_tensor("psS", [P, 4 * BANK], F32))
        m.psT = [stack.enter_context(nc.psum_tensor(f"psT{i}", [P, BANK], F32)) for i in range(2)]
        m.psO = stack.enter_context(nc.psum_tensor("psO", [P, BANK], F32))
        m.psM = stack.enter_context(nc.psum_tensor("psM", [P, BANK], F32))
        m.ctx, m.ctxT = sb("ctx", [P, SC, E]), sb("ctxT", [P, S])
        m.xb, m.tmp, m.oT = sb("xb", [P, TT, E]), sb("tmp", [P, TT, E]), sb("oT", [P, TT * 1024])
        m.wq0, m.wk0, m.wv0, m.wo0 = (sb(n, [P, P]) for n in ("wq0", "wk0", "wv0", "wo0"))
        m.bq0, m.bk0 = sb("bq0", [P, 1]), sb("bk0", [P, 1])
        m.bv0, m.bo0 = sb("bv0", [P, E]), sb("bo0", [P, E])
        m.gate = sb("gate", [P, NT, X0])
        m.combine = sb("combine", [P, NT, X1])

        m.loaded = dict(ident=m.ident[:, :], fold=m.fold[:, :], below=m.below[:, :], cos_sin=m.cos_sin[:, :],
                        earlier=m.earlier[:, :, :], weight8=m.weight8[:, :], headmask=m.headmask[:, :],
                        scanreset=m.scanreset[:, :], ones=m.ones[:, :], gates=m.gates[:, :],
                        wq0=m.wq0[:, :], wk0=m.wk0[:, :], wv0=m.wv0[:, :],
                        wo0=m.wo0[:, :], bq0=m.bq0[:, :], bk0=m.bk0[:, :], bv0=m.bv0[:, :], bo0=m.bo0[:, :])
        d = dram
        m.source = dict(ident=d["ident"], fold=d["fold"], below=d["below"], cos_sin=d["cos_sin"], earlier=d["earlier"],
                        weight8=d["weight8"], headmask=d["headmask"], scanreset=d["scanreset"], ones=d["ones"],
                        gates=d["gates"].to_broadcast([P, 4]),
                        wq0=d["wq0"], wk0=d["wk0"], wv0=d["wv0"], wo0=d["wo0"], bq0=d["bq0"], bk0=d["bk0"],
                        bv0=d["bv0"].to_broadcast([P, E]), bo0=d["bo0"].to_broadcast([P, E]))

        block_load(nc, m, s, dram)
        block_attention0(nc, m, s, dram)
        block_route0(nc, m, s, dram)
        block_experts0(nc, m, s, dram)
        block_norm1(nc, m, s, dram)
        block_attention1(nc, m, s, dram)
        block_route1(nc, m, s, dram)
        block_experts1(nc, m, s, dram)
        with nc.Block() as block:
            @block.sync
            def _(sp):
                sp.dma_start(dram["out"].rearrange("b (t p) d -> p (b t) d", p=P), m.x[:, :, :]).then_inc(s.stored, 16)
                sp.wait_ge(s.stored, 16)


def constants():
    p = np.arange(P)
    f = np.float32
    inv = (1.0 / np.float64(10000.0) ** (np.arange(0, D1, 2, dtype=np.float64) / D1)).astype(f)
    ang = np.repeat(np.arange(S, dtype=f)[:, None] * inv[None, :], 2, axis=1).T
    sign = np.where(np.arange(D1) % 2 == 0, -1.0, 1.0).astype(f)[:, None]
    return dict(
        ident=np.eye(P, dtype=f),
        fold=(p[:, None] % D1 == p[None, :] % D1).astype(f),
        below=(p[:, None] < p[None, :]).astype(f),
        ones=np.ones((P, P), f),
        cos_sin=np.concatenate([np.cos(ang), np.sin(ang) * sign]).astype(f),
        earlier=np.broadcast_to((np.arange(GR)[None, :] < np.arange(GR)[:, None]).astype(f), (P, GR, GR)).copy(),
        weight8=np.broadcast_to(np.arange(X0, 0, -1).astype(f), (P, X0)).copy(),
        position=np.arange(S, dtype=f)[None, :],
        spread=spread(),
        headmask=((p[:, None] % 32) // D0 == np.arange(4)[None, :]).astype(f),
        scanreset=np.broadcast_to((np.arange(NT * X1) % X1 != 0).astype(f), (P, NT * X1)).copy(),
    )


def spread():
    out = np.zeros((X1 + 1, PAIRS + 1, P), np.float32)
    for e in range(X1):
        out[e, e // 2, e % 2 * I1:(e % 2 + 1) * I1] = 1
    out[X1, PAIRS] = 1
    return out


def pairs(routed, shared):
    return np.concatenate([routed.reshape(PAIRS, P, E), shared[None]]).transpose(2, 0, 1)


def head_weights(a):
    swap = np.arange(D1) ^ 1

    def both(name):
        w = a[f"L1_xattn_{name}"].reshape(-1, H, D1)
        return np.concatenate([w, w[:, :, swap]], axis=2).transpose(1, 0, 2)

    wv = a["L1_xattn_Wv"].reshape(E, H, D1).transpose(1, 0, 2)
    return np.concatenate([both("Wk"), both("Wq"), wv, both("bk").transpose(0, 2, 1),
                           both("bq").transpose(0, 2, 1)], axis=2)


def kernel(**inputs):
    import concourse.bacc as bacc
    from concourse.bass_utils import run_bass_kernel_spmd

    a = {k: np.asarray(v) for k, v in inputs.items()}
    arrays = dict(constants())
    arrays.update(
        x=a["x"], ctx=a["ctx_1024"], attn_mask=a["fside_SxS2_0"], pad=a["mask_BxS2_bf0"],
        gates=np.stack([a["g_xattn"], a["g_ffn"]], axis=1).reshape(1, 4),
        wq0=a["L0_xattn_Wq"].T, wk0=a["L0_xattn_Wk"].T, wv0=a["L0_xattn_Wv"].T, wo0=a["L0_xattn_Wo"].T,
        bq0=a["L0_xattn_bq"][:, None], bk0=a["L0_xattn_bk"][:, None],
        wg=a["L0_ffn_Wg"], w1=a["L0_ffn_W1"], w2=a["L0_ffn_W2"],
        lens=a["_lenS2"][None, :], ln_g=a["L1_xattn_ln_g"][:, None], ln_b=a["L1_xattn_ln_b"][:, None],
        head_w=head_weights(a), wo1=a["L1_xattn_Wo"].reshape(8, P, E).transpose(1, 0, 2),
        bv1=a["L1_xattn_bv"][None, :], bo1=a["L1_xattn_bo"][None, :],
        wg1=a["L1_ffn_gate_weight"].T, expert_bias=a["L1_ffn_e_score_correction_bias"][None, :],
        e1_gate=pairs(a["L1_ffn_experts_gate_up"][:, :I1], a["L1_ffn_shared_gate_w"]),
        e1_up=pairs(a["L1_ffn_experts_gate_up"][:, I1:], a["L1_ffn_shared_up_w"]),
        e1_down=np.concatenate([a["L1_ffn_experts_down"].transpose(0, 2, 1).reshape(PAIRS, P, E),
                                a["L1_ffn_shared_down_w"].T[None]]).transpose(1, 0, 2),
        bv0=a["L0_xattn_bv"][None, :], bo0=a["L0_xattn_bo"][None, :],
    )
    nc = bacc.Bacc("TRN2", target_bir_lowering=False, num_devices=1)
    dram, given = {}, {}
    for name, v in arrays.items():
        v = np.ascontiguousarray(v)
        given[f"in_{name}"] = v
        dram[name] = nc.dram_tensor(f"in_{name}", v.shape, mybir.dt.from_np(v.dtype), kind="ExternalInput").ap()
    dram["out"] = nc.dram_tensor("out_x", (B, T, E), F32, kind="ExternalOutput").ap()
    build(nc, dram)
    result = run_bass_kernel_spmd(nc, [given], core_ids=[0])
    return result.results[0]["out_x"]
```

```python
from contextlib import ExitStack

import numpy as np

import concourse.bass as bass
import concourse.mybir as mybir
from concourse.alu_op_type import AluOpType as ALU

ACT = mybir.ActivationFunctionType
AX = mybir.AxisListType
F32 = mybir.dt.float32
F16 = mybir.dt.float16
I32 = mybir.dt.int32
U8 = mybir.dt.uint8

P = 128
B, T, E = 8, 256, 128
S = 1601
H = 16
TT = T // P
NT = B * TT
TOK = B * T
SC = -(-S // P)
FULL = S // P
REST = S - FULL * P
BANK = 512
SPANS = [(o, min(BANK, S - o)) for o in range(0, S, BANK)]
GROUPS = [range(4 * g, min(4 * g + 4, SC)) for g in range(4)]
D0 = E // H
D1 = 64
EPS = 1e-5
NEG = -1e30
LOWEST = -3e38
X0, CAP = 8, TOK // 8
F0 = 256
X1, I1 = 32, 64
PAIRS = X1 * I1 // P
GR, KEEP, TOP = 8, 4, 6
SCALE1 = 2.5
UB = H * TT
AHEAD = 2
SLOTS = 4


def on_its_own(eng, s):
    eng.sem_inc(s.passed, 1)


def rows(c):
    return P if c < FULL else REST


class Named:
    pass


def prime(nc, s):
    with nc.Block() as block:
        @block.sync
        def _(sp):
            for semaphore in s.to_prime:
                sp.sem_inc(semaphore[0], semaphore[1])
    s.to_prime.clear()


def ln_vector(nc, dve, m, s, src, dst, done_before):
    base = 6 * done_before
    for k in range(NT):
        ins = nc.vector.bn_stats(m.stats[:, k, :], src[:, k, :])
    ins.then_inc(s.ln, 1)
    dve.wait_ge(s.ln, base + 1)
    for k in range(NT):
        ins = nc.vector.bn_aggr(m.mv[:, k, :], m.stats[:, k, :])
    ins.then_inc(s.ln, 1)
    dve.wait_ge(s.ln, base + 2)
    nc.vector.tensor_scalar(m.var[:, 0:NT], m.mv[:, 0:NT, 1], EPS, None, ALU.add).then_inc(s.ln, 1)
    dve.wait_ge(s.ln_sqrt, done_before + 1)
    nc.vector.reciprocal(m.rstd[:, 0:NT], m.var[:, 0:NT]).then_inc(s.ln, 1)
    dve.wait_ge(s.ln, base + 4)
    for k in range(NT):
        ins = nc.vector.tensor_scalar(dst[:, k, :], src[:, k, :], m.mv[:, k, 0:1], m.rstd[:, k:k + 1],
                                      ALU.subtract, ALU.mult)
    ins.then_inc(s.ln, 2)
    dve.wait_ge(s.ln, base + 6)


def ln_scalar(nc, act, m, s, done_before):
    act.wait_ge(s.ln, 6 * done_before + 3)
    nc.scalar.activation(m.var[:, 0:NT], m.var[:, 0:NT], ACT.Sqrt).then_inc(s.ln_sqrt, 1)


def pe_scores(nc, pe, m, a, use, products, banks=range(4)):
    for q in banks:
        o, w = SPANS[q]
        pe.wait_ge(a.bank_free[q], 1 + use[q])
        terms = products(o, w)
        for i, (lhsT, rhs) in enumerate(terms):
            ins = nc.tensor.matmul(m.psS[:, o:o + w], lhsT, rhs, start=(i == 0), stop=(i == len(terms) - 1))
        ins.then_inc(a.bank_full, 1)


def pe_transpose(nc, pe, m, a, n, slot, g):
    if g == 0:
        pe.wait_ge(a.exp_done, n + 1)
        pe.wait_ge(a.copied_lo, 1 + 4 * n)
    if g == 3:
        pe.wait_ge(a.copied_lo, 1 + 4 * n + 1)
    for c in GROUPS[g]:
        o = (c % 4) * P
        ins = nc.tensor.transpose(m.psT[g % 3][0:rows(c), o:o + P],
                                  m.probs[:, slot, c * P:c * P + rows(c)], m.ident[:, :])
    ins.then_inc(a.group_full, 1)


def pe_values(nc, pe, m, a, n, buf, values, d, g):
    if g == 0:
        pe.wait_ge(a.out_taken, 1 + n)
    pe.wait_ge(a.copied_lo, 1 + 4 * n + g + 1)
    for c in GROUPS[g]:
        r = rows(c)
        nc.tensor.matmul(m.psO[:, 0:2 * d], m.probsT_hi[0:r, buf, c, :], values(c, r, 2 * d),
                         start=(c == 0), stop=False)
        ins = nc.tensor.matmul(m.psO[:, 0:d], m.probsT_lo[0:r, buf, c, :], values(c, r, d),
                               start=False, stop=(c == SC - 1))
    if g == 3:
        ins.then_inc(a.out_full, 1)


def pe_unit(ahead, turn, values, before, finish, between=None):
    ahead((0, 1))
    if before is not None:
        before(0)
        before(1)
    turn(0)
    if before is not None:
        before(2)
    if between is not None:
        between()
    turn(1)
    ahead((2, 3))
    if before is not None:
        before(3)
    turn(2)
    turn(3)
    if finish:
        for g in range(4):
            values(g)


def dve_mask_max(nc, dve, m, a, fulls, use, slot, mask, q):
    if q is not None:
        o, w = SPANS[q]
        dve.wait_ge(a.bank_full, fulls[q])
        on_its_own(dve, m.s)
        nc.vector.tensor_tensor_reduce(m.probs[:, slot, o:o + w], m.psS[:, o:o + w], mask(o, w), 1.0, LOWEST,
                                       ALU.add, ALU.max, m.max4[:, slot, q:q + 1]).then_inc(a.bank_free[q], 1)
    return use, slot


def dve_negmax(nc, dve, m, a, use, slot):
    for k in range(4):
        dve.wait_ge(a.bank_free[k], 1 + use[k] + 1)
    nc.vector.tensor_reduce(m.negmax[:, slot:slot + 1], m.max4[:, slot, :], AX.X, ALU.max,
                            negate=True).then_inc(a.max_done, 1)


def act_exp(nc, act, m, a, n, slot):
    act.wait_ge(a.max_done, n + 1)
    nc.scalar.activation(m.probs[:, slot, 0:S], m.probs[:, slot, 0:S], ACT.Exp, bias=m.negmax[:, slot:slot + 1],
                         accum_out=m.sums[:, slot:slot + 1]).then_inc(a.exp_done, 1)


def group_views(m, buf, g):
    chunks = GROUPS[g]
    r = rows(chunks[-1])
    src = m.psT[g % 3][0:r, 0:len(chunks) * P].rearrange("p (c t) -> p c t", t=P)
    hi, lo = (v[0:r, buf, chunks[0]:chunks[-1] + 1, :] for v in (m.probsT_hi, m.probsT_lo))
    return src, hi, lo


def act_group_hi(nc, act, m, a, n, buf, g):
    src, hi, _ = group_views(m, buf, g)
    act.wait_ge(a.group_full, 4 * n + g + 1)
    nc.scalar.copy(hi, src).then_inc(a.copied_hi, 1)


def dve_group_lo(nc, dve, m, a, n, buf, g):
    src, hi, lo = group_views(m, buf, g)
    dve.wait_ge(a.copied_hi, 4 * n + g + 1)
    nc.vector.tensor_tensor(lo, src, hi, ALU.subtract).then_inc(a.copied_lo, 1)


def dve_unit(nc, dve, m, a, n, buf, ahead, before, finish, between=None):
    def rest(g):
        dve_group_lo(nc, dve, m, a, n, buf, g)

    if before is not None:
        before[0]()
    ahead(0)
    ahead(1)
    rest(0)
    if between is not None:
        between()
    ahead(2)
    rest(1)
    ahead(3)
    if before is not None:
        before[1]()
    dve_negmax(nc, dve, m, a, *ahead(None))
    rest(2)
    if before is not None:
        before[2]()
    rest(3)
    if finish is not None:
        for part in finish:
            part()


def dve_take_out(nc, dve, m, a, n, slot, dst, bias, d):
    def over():
        dve.wait_ge(a.out_taken, 1 + n)
        dve.wait_ge(a.exp_done, n + 1)
        nc.vector.reciprocal(m.rsum[:, 0:1], m.sums[:, slot:slot + 1]).then_inc(a.recip_done, 1)

    def low():
        dve.wait_ge(a.recip_done, 2 * n + 1)
        dve.wait_ge(a.out_full, OUT_START + n + 1)
        nc.vector.scalar_tensor_tensor(m.part[:, 0:d], m.psO[:, d:2 * d], m.rsum[:, 0:1], bias,
                                       ALU.mult, ALU.add).then_inc(a.recip_done, 1)

    def high():
        dve.wait_ge(a.recip_done, 2 * n + 2)
        nc.vector.scalar_tensor_tensor(dst, m.psO[:, 0:d], m.rsum[:, 0:1], m.part[:, 0:d],
                                       ALU.mult, ALU.add).then_inc(a.out_taken, 1)

    return [over, low, high]


OUT_START = 8


def attention_sems(s, tag):
    a = Named()
    a.bank_full, a.exp_done, a.group_full = (s.sem(f"{tag}_{n}") for n in ("bank_full", "exp_done", "group_full"))
    a.max_done, a.recip_done, a.copied_hi = (s.sem(f"{tag}_{n}") for n in ("max_done", "recip_done", "copied_hi"))
    a.copied_lo, a.out_taken = (s.from_one(f"{tag}_{n}") for n in ("copied_lo", "out_taken"))
    a.out_full = s.from_one(f"{tag}_out_full", OUT_START)
    a.bank_free = [s.from_one(f"{tag}_bank_free{q}") for q in range(4)]
    return a


def block_load(nc, m, s, dram):
    with nc.Block() as block:
        @block.sync
        def _(sp):
            sp.dma_start(m.x[:, :, :], dram["x"].rearrange("b (t p) d -> p (b t) d", p=P)).then_inc(s.load, 16)
            for name in LOADED:
                getdst = m.loaded[name]
                sp.dma_start(getdst, m.source[name]).then_inc(s.load, 16)
            sp.wait_ge(s.load, 16 * (1 + len(LOADED)))

        @block.scalar
        def _(act):
            ln_scalar(nc, act, m, s, 0)
            act.wait_ge(s.load, 16 * (1 + len(LOADED)))
            nc.scalar.activation(m.gates[:, :], m.gates[:, :], ACT.Tanh).then_inc(s.tanh, 1)
            act.wait_ge(s.tanh, 1)

        @block.vector
        def _(dve):
            dve.wait_ge(s.load, 16 * (1 + len(LOADED)))
            ln_vector(nc, dve, m, s, m.x, m.xn, 0)
            nc.vector.memset(m.xn[:, NT:NT + TT, :], 0.0)


LOADED = ["ident", "fold", "below", "cos_sin", "earlier", "weight8", "headmask", "scanreset", "ones",
          "gates", "wq0", "wk0", "wv0", "wo0", "bq0", "bk0", "bv0", "bo0"]


def block_attention0(nc, m, s, dram):
    with ExitStack() as stack:
        def sb(name, shape, dt=F32):
            return stack.enter_context(nc.sbuf_tensor(name, shape, dt))

        m.attn_mask, m.mask = sb("attn_mask", [P, TT, S]), sb("mask", [P, TT, S])
        m.pad8 = sb("pad8", [P, S], U8)
        m.o0 = sb("o0", [P, TT, E])
        m.k32, m.q32 = sb("k32", [P, S]), sb("q32", [P, T])
        m.khi, m.klo = sb("khi", [P, S], F16), sb("klo", [P, S], F16)
        m.qhi, m.qlo = sb("qhi", [P, T], F16), sb("qlo", [P, T], F16)
        m.kfan, m.qfan = sb("kfan", [P, 4, S], F16), sb("qfan", [P, 4, T], F16)
        m.qhead, m.vhead = sb("qhead", [P, 4, T], F16), sb("vhead", [P, 4, SC, 2, D0], F16)
        m.v0 = sb("v0", [P, SC, 2, E], F16)
        attention0(nc, m, s, dram)


def attention0(nc, m, s, dram):
    a = attention_sems(s, "a0")
    ctx_ready, x_fixed, x_turned = s.sem("a0_ctx_ready"), s.sem("a0_x_fixed"), s.sem("a0_x_turned")
    mask_loaded, mask_done, x_taken = s.sem("a0_mask_loaded"), s.sem("a0_mask_done"), s.sem("a0_x_taken")
    q_full, q_taken, k_hi, q_hi = (s.sem(f"a0_{n}") for n in ("q_full", "q_taken", "k_hi", "q_hi"))
    k_lo, q_lo, v_hi, head_ready = (s.sem(f"a0_{n}") for n in ("k_lo", "q_lo", "v_hi", "head_ready"))
    fanned, fanned_last, pe_out, dve_out = (s.sem(f"a0_{n}") for n in ("fanned", "fanned_last", "pe_out", "dve_out"))
    batch_done = s.from_one("a0_batch_done")
    GH = 4
    NG = H // GH
    GU = GH * TT
    LAST = (NG - 1) * GU
    USES = UB + 3
    prime(nc, s)

    def unit(b, g, u):
        return b * UB + g * GU + u

    def score_use(b, step):
        return b * USES + 5 + step + max(0, min(3, step - LAST))

    def group_use(b, g, u):
        return b * USES + g * GU + 5 + u if not isinstance(g, int) else score_use(b, g * GU + u)

    def prep_use(b, kind):
        return b * USES + 5 + LAST + 1 + 2 * kind

    def all4(use):
        return [use] * 4

    def finishes(last, u):
        return u == GU - 1 or (last and u in (0, 1))

    with nc.Block() as block:
        @block.sync
        def _(sp):
            def load(nb, batch):
                sp.dma_start(m.ctx[:, 0:FULL, :], dram["ctx"][bass.ds(batch, 1), 0:FULL * P, :]
                             .rearrange("a (c p) d -> p (a c) d", p=P)).then_inc(ctx_ready, 16)
                sp.dma_start(m.ctx[0:REST, FULL, :], dram["ctx"][bass.ds(batch, 1), FULL * P:S, :]
                             .rearrange("a p d -> p (a d)")).then_inc(ctx_ready, 16)
                sp.dma_start(m.pad8[:, :], dram["pad"][bass.ds(batch, 1), :].to_broadcast([P, S])).then_inc(ctx_ready, 16)

            def fan(groups, done):
                n = len(groups)
                for r in range(4):
                    kpart = m.khi if r % 2 == 0 else m.klo
                    qpart = m.qhi if r < 2 else m.qlo
                    for g in groups:
                        sp.dma_start(m.kfan[32 * r:32 * r + 32, g, :], kpart[32 * g:32 * g + 32, :]).then_inc(done, 16)
                        sp.dma_start(m.qfan[32 * r:32 * r + 32, g, :], qpart[32 * g:32 * g + 32, :]).then_inc(done, 16)

            sp.dma_start(m.attn_mask[:, :, :], dram["attn_mask"].rearrange("(t p) s -> p t s", p=P)).then_inc(mask_loaded, 16)
            load(0, 0)
            sp.wait_ge(k_lo, 1)
            sp.wait_ge(q_lo, 1)
            fan(range(NG - 1), fanned)
            fan([NG - 1], fanned_last)

            def prefetch(b, batch):
                def after(semaphore, value):
                    sp.wait_ge(semaphore, value)
                    on_its_own(sp, s)

                after(x_turned, b + 1)
                after(mask_done, b + 1)
                load(b + 1, batch)
                after(k_lo, b + 2)
                after(q_lo, b + 2)
                after(head_ready, 2 * H * (b + 1))
                after(a.bank_full, 4 * score_use(b, LAST - AHEAD - 1) + 4)
                fan(range(NG - 1), fanned)
                after(a.bank_full, 4 * score_use(b, UB - AHEAD - 1) + 4)
                fan([NG - 1], fanned_last)

            with sp.Fori(0, B - 1) as b:
                prefetch(b, b + 1)
            prefetch(B - 1, 0)
            sp.wait_ge(fanned, 16 * 8 * (NG - 1) * (B + 1))
            sp.wait_ge(fanned_last, 16 * 8 * (B + 1))

        @block.gpsimd
        def _(pool):
            def split(nb):
                pool.wait_ge(k_hi, nb + 1)
                nc.gpsimd.tensor_tensor(m.klo[:, :], m.k32[:, :], m.khi[:, :], ALU.subtract).then_inc(k_lo, 1)
                pool.wait_ge(q_hi, nb + 1)
                nc.gpsimd.tensor_tensor(m.qlo[:, :], m.q32[:, :], m.qhi[:, :], ALU.subtract).then_inc(q_lo, 1)

            def heads(nb, g, first_unit):
                for j in range(GH):
                    if first_unit is not None:
                        pool.wait_ge(a.out_full, OUT_START + first_unit + 2 * j + 2 - GU)
                        on_its_own(pool, s)
                    nc.gpsimd.tensor_copy(m.vhead[:, j, :, :, :],
                                          m.v0[:, :, :, bass.ds(g * (GH * D0) + j * D0, D0)]).then_inc(head_ready, 1)
                    nc.gpsimd.tensor_tensor(m.qhead[:, j, :], m.qfan[:, bass.ds(g, 1), :].rearrange("p a t -> p (a t)"),
                                            m.headmask[:, j:j + 1].to_broadcast([P, T]), ALU.mult).then_inc(head_ready, 1)

            def values_ready(use):
                for q in range(4):
                    pool.wait_ge(a.bank_free[q], 1 + use + 1)
                on_its_own(pool, s)

            split(0)
            values_ready(2)
            pool.wait_ge(fanned, 16 * 8 * (NG - 1))
            heads(0, 0, None)
            with pool.Fori(0, B) as b:
                with pool.Fori(1, NG - 1) as g:
                    heads(b, g, unit(b, g, 0))
                pool.wait_ge(fanned_last, 16 * 8 * (b + 1))
                heads(b, NG - 1, unit(b, NG - 1, 0))
                split(b + 1)
                values_ready(prep_use(b, 2))
                pool.wait_ge(fanned, 16 * 8 * (NG - 1) * (b + 2))
                heads(b + 1, 0, unit(b + 1, 0, 0))

        @block.tensor
        def _(pe):
            def turn_context(nb, use):
                pe.wait_ge(ctx_ready, 48 * (nb + 1))
                for q, chunks in enumerate(GROUPS):
                    pe.wait_ge(a.bank_free[q], 1 + use)
                    for c in chunks:
                        r = rows(c)
                        ins = nc.tensor.transpose(m.psS[:, c * P:c * P + r], m.ctx[0:r, c, :], m.ident[0:r, 0:r])
                    ins.then_inc(a.bank_full, 1)
                pe.wait_ge(x_fixed, nb + 1)
                if not isinstance(nb, int):
                    pe.wait_ge(batch_done, nb)
                for t in range(TT):
                    ins = nc.tensor.transpose(m.psM[:, t * P:(t + 1) * P], m.xb[:, t, :], m.ident[:, :])
                ins.then_inc(x_turned, 1)

            def project_keys(nb, use, units=None):
                for q in (2, 3, 0, 1):
                    pe.wait_ge(a.bank_free[q], 1 + use)
                for o, w in SPANS:
                    nc.tensor.matmul(m.psS[:, o:o + w], m.wk0[:, :], m.ctxT[:, o:o + w],
                                     start=True, stop=True).then_inc(a.bank_full, 1)
                pe.wait_ge(x_taken, nb + 1)
                if units is not None:
                    pe.wait_ge(a.out_taken, 1 + units)
                nc.tensor.matmul(m.psM[:, 0:T], m.wq0[:, :], m.xT[:, 0:T], start=True, stop=True).then_inc(q_full, 1)

            def project_values(nb, use):
                for q, chunks in enumerate(GROUPS):
                    pe.wait_ge(a.bank_free[q], 1 + use)
                    for c in chunks:
                        r = rows(c)
                        ins = nc.tensor.matmul(m.psS[0:r, c * P:(c + 1) * P], m.ctxT[:, c * P:c * P + r], m.wv0[:, :],
                                               start=True, stop=True)
                    ins.then_inc(a.bank_full, 1)

            def scores(head, g, j, t, use, banks=range(4)):
                pe.wait_ge(head_ready, 2 * head + 2)
                pe_scores(nc, pe, m, a, all4(use), lambda o, w: [
                    (m.qhead[:, j, t * P:(t + 1) * P],
                     m.kfan[:, bass.ds(g, 1), o:o + w].rearrange("p a s -> p (a s)"))], banks)

            def group(b, g, last):
                def values(u):
                    return lambda k: pe_values(
                        nc, pe, m, a, unit(b, g, u), u % 2,
                        lambda c, r, d: m.vhead[0:r, u // TT, c, :, :].rearrange("p a d -> p (a d)")[:, 0:d], D0, k)

                for u in range(GU):
                    n = unit(b, g, u)
                    v = (u + AHEAD) % GU
                    if u + AHEAD < GU:
                        to = (b * NG + g) * GH, g
                    elif not last:
                        to = (b * NG + g + 1) * GH, g + 1
                    else:
                        to = (b + 1) * H, 0
                    pe_unit(lambda banks: scores(to[0] + v // TT, to[1], v // TT, v % TT, group_use(b, g, u), banks),
                            lambda k: pe_transpose(nc, pe, m, a, n, u % SLOTS, k),
                            values(u), None if u == 0 or finishes(last, u - 1) else values(u - 1), finishes(last, u))
                    if last and u == 0:
                        turn_context(b + 1, prep_use(b, 0))
                    if last and u == 1:
                        project_keys(b + 1, prep_use(b, 1), n + 1)
                    if last and u == 2:
                        project_values(b + 1, prep_use(b, 2))

            pe.wait_ge(mask_loaded, 16)
            turn_context(0, 0)
            project_keys(0, 1)
            project_values(0, 2)
            for u in range(AHEAD):
                scores(0, 0, 0, u, 3 + u)
            with pe.Fori(0, B) as b:
                with pe.Fori(0, NG - 1) as g:
                    group(b, g, False)
                group(b, NG - 1, True)
                pe.wait_ge(a.out_taken, 1 + UB * (b + 1))
                pe.wait_ge(q_taken, b + 2)
                for t in range(TT):
                    ins = nc.tensor.transpose(m.psM[:, t * P:(t + 1) * P], m.o0[:, t, :], m.ident[:, :])
                ins.then_inc(pe_out, 1)
                pe.wait_ge(dve_out, 2 * b + 1)
                for t in range(TT):
                    ins = nc.tensor.matmul(m.psM[:, t * P:(t + 1) * P], m.oT[:, t * P:(t + 1) * P], m.wo0[:, :],
                                           start=True, stop=True)
                ins.then_inc(pe_out, 1)

        @block.scalar
        def _(act):
            def take_context(nb, use):
                for q in range(2):
                    act.wait_ge(a.bank_full, 4 * use + q + 1)
                    o, w = SPANS[q]
                    nc.scalar.copy(m.ctxT[:, o:o + w], m.psS[:, o:o + w]).then_inc(a.bank_free[q], 1)

            def take_keys(nb, use):
                if not isinstance(nb, int):
                    act.wait_ge(k_lo, nb)
                for q in range(2):
                    act.wait_ge(a.bank_full, 4 * use + q + 1)
                    o, w = SPANS[q]
                    nc.scalar.activation(m.k32[:, o:o + w], m.psS[:, o:o + w], ACT.Identity,
                                         bias=m.bk0[:, 0:1]).then_inc(a.bank_free[q], 1)
                for q in range(4):
                    act.wait_ge(a.bank_free[q], 1 + use + 1)
                nc.scalar.copy(m.khi[:, :], m.k32[:, :]).then_inc(k_hi, 1)
                act.wait_ge(q_taken, nb + 1)
                nc.scalar.copy(m.qhi[:, :], m.q32[:, :]).then_inc(q_hi, 1)

            def take_values(nb, use):
                if not isinstance(nb, int):
                    act.wait_ge(head_ready, 2 * H * nb)
                for q, chunks in enumerate(GROUPS):
                    act.wait_ge(a.bank_full, 4 * use + q + 1)
                    c0, c1 = chunks[0], chunks[-1] + 1
                    r = rows(c1 - 1)
                    nc.scalar.copy(m.v0[0:r, c0:c1, 0, :],
                                   m.psS[0:r, c0 * P:c1 * P].rearrange("p (c d) -> p c d", d=E)).then_inc(v_hi, 1)

            def group(b, g, last):
                for u in range(GU):
                    n = unit(b, g, u)
                    for k in range(4):
                        act_group_hi(nc, act, m, a, n, u % 2, k)
                    act_exp(nc, act, m, a, n + AHEAD, (u + AHEAD) % SLOTS)
                    if last and u == 0:
                        take_context(b + 1, prep_use(b, 0))
                    if last and u == 1:
                        take_keys(b + 1, prep_use(b, 1))
                    if last and u == 2:
                        take_values(b + 1, prep_use(b, 2))

            take_context(0, 0)
            take_keys(0, 1)
            take_values(0, 2)
            for u in range(AHEAD):
                act_exp(nc, act, m, a, u, u)
            with act.Fori(0, B) as b:
                with act.Fori(0, NG - 1) as g:
                    group(b, g, False)
                group(b, NG - 1, True)

        @block.vector
        def _(dve):
            def next_mask(nb):
                dve.wait_ge(ctx_ready, 48 * (nb + 1))
                for t in range(TT):
                    ins = nc.vector.scalar_tensor_tensor(m.mask[:, t, :], m.pad8[:, :], NEG, m.attn_mask[:, t, :],
                                                         ALU.mult, ALU.add)
                ins.then_inc(mask_done, 1)
                dve.wait_ge(mask_done, nb + 1)

            def fix_x(nb):
                if not isinstance(nb, int):
                    dve.wait_ge(x_turned, nb)
                nc.vector.tensor_copy(m.xb[:, :, :], m.xn[:, bass.ds(nb * TT, TT), :]).then_inc(x_fixed, 1)

            def take_context(nb, use):
                for q in range(2, 4):
                    dve.wait_ge(a.bank_full, 4 * use + q + 1)
                    o, w = SPANS[q]
                    nc.vector.tensor_copy(m.ctxT[:, o:o + w], m.psS[:, o:o + w]).then_inc(a.bank_free[q], 1)
                dve.wait_ge(x_turned, nb + 1)
                nc.vector.tensor_copy(m.xT[:, 0:T], m.psM[:, 0:T]).then_inc(x_taken, 1)

            def take_keys(nb, use):
                if not isinstance(nb, int):
                    dve.wait_ge(k_lo, nb)
                for q in range(2, 4):
                    dve.wait_ge(a.bank_full, 4 * use + q + 1)
                    o, w = SPANS[q]
                    nc.vector.tensor_scalar(m.k32[:, o:o + w], m.psS[:, o:o + w], m.bk0[:, 0:1], None,
                                            ALU.add).then_inc(a.bank_free[q], 1)
                dve.wait_ge(q_full, nb + 1)
                if not isinstance(nb, int):
                    dve.wait_ge(q_lo, nb)
                nc.vector.tensor_scalar(m.q32[:, :], m.psM[:, 0:T], m.bq0[:, 0:1], float(D0) ** -0.5,
                                        ALU.add, ALU.mult).then_inc(q_taken, 1)

            def take_values(nb, use):
                for q, chunks in enumerate(GROUPS):
                    dve.wait_ge(v_hi, 4 * nb + q + 1)
                    c0, c1 = chunks[0], chunks[-1] + 1
                    r = rows(c1 - 1)
                    nc.vector.tensor_tensor(m.v0[0:r, c0:c1, 1, :],
                                            m.psS[0:r, c0 * P:c1 * P].rearrange("p (c d) -> p c d", d=E),
                                            m.v0[0:r, c0:c1, 0, :], ALU.subtract).then_inc(a.bank_free[q], 1)

            def mask_max(use, t, slot, q):
                return dve_mask_max(nc, dve, m, a, [4 * use + k + 1 for k in range(4)], all4(use), slot, lambda o, w: m.mask[:, t, o:o + w], q)

            def group(b, g, last):
                def take_out(u):
                    o = g * (GH * D0) + (u // TT) * D0
                    return dve_take_out(nc, dve, m, a, unit(b, g, u), u % SLOTS,
                                        m.o0[:, u % TT, bass.ds(o, D0)], m.bv0[:, bass.ds(o, D0)], D0)

                for u in range(GU):
                    n = unit(b, g, u)
                    if last and u == GU - AHEAD:
                        next_mask(b + 1)
                    dve_unit(nc, dve, m, a, n, u % 2,
                             lambda q: mask_max(group_use(b, g, u), u % TT, (u + AHEAD) % SLOTS, q),
                             None if u == 0 or finishes(last, u - 1) else take_out(u - 1),
                             take_out(u) if finishes(last, u) else None)
                    if last and u == 0:
                        fix_x(b + 1)
                        take_context(b + 1, prep_use(b, 0))
                    if last and u == 1:
                        take_keys(b + 1, prep_use(b, 1))
                    if last and u == 2:
                        take_values(b + 1, prep_use(b, 2))

            nc.vector.memset(m.v0[:, FULL, :, :], 0.0)
            dve.wait_ge(mask_loaded, 16)
            fix_x(0)
            next_mask(0)
            take_context(0, 0)
            take_keys(0, 1)
            take_values(0, 2)
            for u in range(AHEAD):
                for q in range(4):
                    mask_max(3 + u, u, u, q)
                dve_negmax(nc, dve, m, a, all4(3 + u), u)
            with dve.Fori(0, B) as b:
                with dve.Fori(0, NG - 1) as g:
                    group(b, g, False)
                group(b, NG - 1, True)
                dve.wait_ge(pe_out, 2 * b + 1)
                nc.vector.tensor_copy(m.oT[:, 0:T], m.psM[:, 0:T]).then_inc(dve_out, 1)
                dve.wait_ge(pe_out, 2 * b + 2)
                for t in range(TT):
                    ins = nc.vector.tensor_tensor(m.tmp[:, t, :], m.psM[:, t * P:(t + 1) * P], m.bo0[:, :], ALU.add)
                ins.then_inc(dve_out, 1)
                dve.wait_ge(dve_out, 2 * b + 2)
                xs = m.x[:, bass.ds(b * TT, TT), :]
                nc.vector.scalar_tensor_tensor(xs, m.tmp[:, :, :], m.gates[:, 0:1], xs,
                                               ALU.mult, ALU.add).then_inc(batch_done, 1)


def chain(eng, sem):
    count = [0]

    def step(ins):
        count[0] += 1
        ins.then_inc(sem, 1)
        eng.wait_ge(sem, count[0])
    return step, count


def to_tokens(t):
    return t.unsqueeze(2)


def pe_turn_x(nc, pe, m, normed, turned):
    pe.wait_ge(normed, 1)
    for k in range(NT):
        ins = nc.tensor.transpose(m.psS[:, k * P:(k + 1) * P], m.xn[:, k, :], m.ident[:, :])
        if k in (NT // 2 - 1, NT - 1):
            ins.then_inc(turned, 1)


def block_route0(nc, m, s, dram):
    normed, turned, xt_act, xt_dve = (s.sem(f"r0_{n}") for n in ("normed", "turned", "xt_act", "xt_dve"))
    logits_done, exp_done, counts, counted, steps = (s.sem(f"r0_{n}") for n in ("logits", "exp", "counts", "counted", "steps"))
    BITS, STEPS = 30, 6
    with ExitStack() as stack:
        def sb(name, shape, dt=F32):
            return stack.enter_context(nc.sbuf_tensor(name, shape, dt))

        wg = sb("wg", [P, X0])
        probs, ge, flag, val = (sb(n, [P, NT, X0]) for n in ("r0_probs", "r0_ge", "r0_flag", "r0_val"))
        gt, eq, before = (sb(n, [P, NT, X0]) for n in ("r0_gt", "r0_eq", "r0_before"))
        geT = sb("r0_geT", [P, X0, NT])
        top, total = sb("r0_top", [P, NT]), sb("r0_total", [P, NT])
        count, need = sb("r0_count", [P, X0]), sb("r0_need", [P, X0])
        bit, cur, cand, take = (sb(n, [P, X0], I32) for n in ("r0_bit", "r0_cur", "r0_cand", "r0_take"))
        lg = m.psT[2][:, 0:NT * X0].rearrange("p (k e) -> p k e", e=X0)
        rank = lg
        sums = m.psO[:, 0:X0]
        curf, candf = cur[:, :].bitcast(F32), cand[:, :].bitcast(F32)

        def over_k(ap):
            return ap.unsqueeze(1).to_broadcast([P, NT, X0])

        def over_e(ap):
            return ap.unsqueeze(2).to_broadcast([P, NT, X0])

        with nc.Block() as block:
            @block.sync
            def _(sp):
                sp.dma_start(wg[:, :], dram["wg"]).then_inc(s.weights, 16)

            @block.tensor
            def _(pe):
                pe_turn_x(nc, pe, m, normed, turned)
                pe.wait_ge(xt_act, 1)
                pe.wait_ge(xt_dve, 1)
                pe.wait_ge(s.weights, 16)
                for k in range(NT):
                    ins = nc.tensor.matmul(lg[:, k, :], m.xT[:, k * P:(k + 1) * P], wg[:, :], start=True, stop=True)
                ins.then_inc(logits_done, 1)
                with pe.Fori(0, BITS) as i:
                    pe.wait_ge(counts, i + 1)
                    nc.tensor.matmul(sums, m.ones[:, :], count[:, :], start=True, stop=True).then_inc(counted, 1)
                pe.wait_ge(counts, BITS + 1)
                nc.tensor.matmul(sums, m.ones[:, :], count[:, :], start=True, stop=True).then_inc(counted, 1)
                pe.wait_ge(counts, BITS + 2)
                eq2, before2 = (v[:, :, :].rearrange("p k e -> p (k e)") for v in (eq, before))
                nc.tensor.matmul(m.psT[2][:, 0:NT * X0], m.below[:, :], eq2, start=True, stop=False)
                nc.tensor.matmul(m.psT[2][:, 0:NT * X0], m.ones[:, :], before2, start=False, stop=True).then_inc(counted, 1)

            @block.scalar
            def _(act):
                ln_scalar(nc, act, m, s, 1)
                act.wait_ge(turned, 1)
                nc.scalar.copy(m.xT[:, 0:TOK // 2], m.psS[:, 0:TOK // 2]).then_inc(xt_act, 1)
                act.wait_ge(steps, 2)
                nc.scalar.activation(probs[:, :, :], probs[:, :, :], ACT.Exp).then_inc(exp_done, 1)

            @block.vector
            def _(dve):
                ln_vector(nc, dve, m, s, m.x, m.xn, 1)
                nc.vector.memset(cur[:, :], 0).then_inc(normed, 1)
                nc.vector.memset(bit[:, :], 1 << (BITS - 1))
                dve.wait_ge(turned, 2)
                nc.vector.tensor_copy(m.xT[:, TOK // 2:TOK], m.psS[:, TOK // 2:TOK]).then_inc(xt_dve, 1)
                step, done = chain(dve, steps)
                dve.wait_ge(logits_done, 1)
                step(nc.vector.tensor_reduce(top[:, :], lg, AX.X, ALU.max))
                step(nc.vector.tensor_tensor(probs[:, :, :], lg, over_e(top[:, :]), ALU.subtract))
                dve.wait_ge(exp_done, 1)
                step(nc.vector.tensor_reduce(total[:, :], probs[:, :, :], AX.X, ALU.add))
                step(nc.vector.reciprocal(top[:, :], total[:, :]))
                step(nc.vector.tensor_tensor(probs[:, :, :], probs[:, :, :], over_e(top[:, :]), ALU.mult))
                first = done[0]
                with dve.Fori(0, BITS) as i:
                    now = i * STEPS + first
                    nc.vector.tensor_tensor(cand[:, :], cur[:, :], bit[:, :], ALU.bitwise_or).then_inc(steps, 1)
                    dve.wait_ge(steps, now + 1)
                    nc.vector.tensor_tensor(ge[:, :, :], probs[:, :, :], over_k(candf), ALU.is_ge).then_inc(steps, 1)
                    dve.wait_ge(steps, now + 2)
                    nc.vector.tensor_reduce(count[:, :], ge[:, :, :].rearrange("p k e -> p e k"), AX.X,
                                            ALU.add).then_inc(counts, 1)
                    nc.vector.tensor_scalar(bit[:, :], bit[:, :], 1, None, ALU.logical_shift_right).then_inc(steps, 1)
                    dve.wait_ge(counted, i + 1)
                    nc.vector.tensor_scalar(take[:, :], sums, float(CAP), None, ALU.is_ge).then_inc(steps, 1)
                    dve.wait_ge(steps, now + 4)
                    on_its_own(dve, s)
                    nc.vector.copy_predicated(cur[:, :], take[:, :], cand[:, :]).then_inc(steps, 2)
                    dve.wait_ge(steps, now + STEPS)
                    on_its_own(dve, s)
                done[0] = first + BITS * STEPS
                step(nc.vector.tensor_tensor(gt[:, :, :], probs[:, :, :], over_k(curf), ALU.is_gt))
                step(nc.vector.tensor_tensor(eq[:, :, :], probs[:, :, :], over_k(curf), ALU.is_equal))
                nc.vector.tensor_reduce(count[:, :], gt[:, :, :].rearrange("p k e -> p e k"), AX.X,
                                        ALU.add).then_inc(counts, 1)
                step(nc.vector.memset(before[:, 0, :], 0.0))
                for k in range(NT - 1):
                    step(nc.vector.tensor_tensor(before[:, k + 1, :], before[:, k, :], eq[:, k, :], ALU.add))
                nc.vector.memset(flag[:, :, :], 0.0).then_inc(counts, 1)
                dve.wait_ge(counted, BITS + 1)
                step(nc.vector.tensor_scalar(need[:, :], sums, -1.0, float(CAP), ALU.mult, ALU.add))
                dve.wait_ge(counted, BITS + 2)
                dve.wait_ge(counts, BITS + 2)
                step(nc.vector.tensor_tensor(flag[:, :, :], rank, over_k(need[:, :]), ALU.is_lt))
                step(nc.vector.tensor_tensor(flag[:, :, :], flag[:, :, :], eq[:, :, :], ALU.mult))
                step(nc.vector.tensor_tensor(flag[:, :, :], flag[:, :, :], gt[:, :, :], ALU.add))
                step(nc.vector.tensor_reduce(top[:, :], flag[:, :, :], AX.X, ALU.max))
                step(nc.vector.tensor_scalar(top[:, :], top[:, :], -1.0, 1.0, ALU.mult, ALU.add))
                step(nc.vector.tensor_tensor(flag[:, :, :], flag[:, :, :], over_e(top[:, :]), ALU.add))
                step(nc.vector.tensor_tensor(val[:, :, :], probs[:, :, :], flag[:, :, :], ALU.mult))
                step(nc.vector.scalar_tensor_tensor(val[:, :, :], flag[:, :, :], -1.0, val[:, :, :], ALU.add, ALU.add))
                step(nc.vector.tensor_reduce(top[:, :], val[:, :, :], AX.X, ALU.max))
                step(nc.vector.tensor_tensor(flag[:, :, :], val[:, :, :], over_e(top[:, :]), ALU.is_equal))
                step(nc.vector.tensor_tensor(flag[:, :, :], flag[:, :, :], over_k(m.weight8[:, :]), ALU.mult))
                step(nc.vector.tensor_reduce(top[:, :], flag[:, :, :], AX.X, ALU.max))
                step(nc.vector.tensor_tensor(flag[:, :, :], flag[:, :, :], over_e(top[:, :]), ALU.is_equal))
                nc.vector.tensor_tensor(m.gate[:, :, :], flag[:, :, :], probs[:, :, :], ALU.mult)


def block_experts0(nc, m, s, dram):
    hidden = s.sem("e0_hidden")
    gelu_done, out_full, added = (s.from_one(f"e0_{n}") for n in ("gelu_done", "out_full", "added"))
    KB = BANK // P
    with ExitStack() as stack:
        def sb(name, shape, dt=F32):
            return stack.enter_context(nc.sbuf_tensor(name, shape, dt))

        w1, w2 = sb("w1", [P, X0, F0]), sb("w2", [P, X0, F0 // P, E])
        act_out = sb("e0_gelu", [P, 2, 2 * BANK])
        acc = sb("e0_acc", [P, NT, E])
        loaded, zeroed = s.sem("e0_loaded"), s.sem("e0_zeroed")
        prime(nc, s)

        def turn(blk, e):
            return blk * X0 + e

        with nc.Block() as block:
            @block.sync
            def _(sp):
                sp.dma_start(w1[:, :, :], dram["w1"].rearrange("e d f -> d e f")).then_inc(loaded, 16)
                sp.dma_start(w2[:, :, :, :], dram["w2"].rearrange("e (h f) d -> f e h d", f=P)).then_inc(loaded, 16)

            @block.tensor
            def _(pe):
                pe.wait_ge(loaded, 32)

                def up(blk, e):
                    n = turn(blk, e)
                    if e >= 2:
                        pe.wait_ge(gelu_done, 1 + n - 1)
                    else:
                        pe.wait_ge(gelu_done, 1 + blk * X0)
                    for h in range(2):
                        o = (2 * (e % 2) + h) * BANK
                        ins = nc.tensor.matmul(m.psS[:, o:o + BANK], w1[:, e, h * P:(h + 1) * P],
                                               m.xT[:, bass.ds(blk * BANK, BANK)], start=True, stop=True)
                    ins.then_inc(hidden, 1)

                def down(blk, e):
                    n = turn(blk, e)
                    pe.wait_ge(gelu_done, 1 + n + 1)
                    if e >= 2:
                        pe.wait_ge(added, 1 + n - 1)
                    else:
                        pe.wait_ge(added, 1 + blk * X0)
                    for k in range(KB):
                        for h in range(2):
                            o = h * BANK + k * P
                            ins = nc.tensor.matmul(m.psT[e % 2][:, k * P:(k + 1) * P], act_out[:, e % 2, o:o + P],
                                                   w2[:, e, h, :], start=(h == 0), stop=(h == 1))
                    ins.then_inc(out_full, 1)

                with pe.Fori(0, TOK // BANK) as blk:
                    up(blk, 0)
                    for e in range(X0):
                        if e + 1 < X0:
                            up(blk, e + 1)
                        down(blk, e)

            @block.scalar
            def _(act):
                with act.Fori(0, TOK // BANK) as blk:
                    for e in range(X0):
                        n = turn(blk, e)
                        act.wait_ge(hidden, n + 1)
                        if e >= 2:
                            act.wait_ge(out_full, 1 + n - 1)
                        else:
                            act.wait_ge(out_full, 1 + blk * X0)
                        o = 2 * (e % 2) * BANK
                        nc.scalar.activation(act_out[:, e % 2, :], m.psS[:, o:o + 2 * BANK], ACT.Gelu).then_inc(gelu_done, 1)

            @block.vector
            def _(dve):
                nc.vector.memset(acc[:, :, :], 0.0).then_inc(zeroed, 1)
                dve.wait_ge(zeroed, 1)
                with dve.Fori(0, TOK // BANK) as blk:
                    for e in range(X0):
                        n = turn(blk, e)
                        dve.wait_ge(out_full, 1 + n + 1)
                        dve.wait_ge(added, 1 + n)
                        for k in range(KB):
                            tile = acc[:, bass.ds(blk * KB + k, 1), :].rearrange("p a d -> p (a d)")
                            ins = nc.vector.scalar_tensor_tensor(
                                tile, m.psT[e % 2][:, k * P:(k + 1) * P],
                                m.gate[:, bass.ds(blk * KB + k, 1), e:e + 1].rearrange("p a e -> p (a e)"), tile,
                                ALU.mult, ALU.add)
                        ins.then_inc(added, 1)
                dve.wait_ge(added, 1 + X0 * TOK // BANK)
                nc.vector.scalar_tensor_tensor(m.x[:, :, :], acc[:, :, :], m.gates[:, 1:2], m.x[:, :, :],
                                               ALU.mult, ALU.add).then_inc(zeroed, 1)
                dve.wait_ge(zeroed, 2)


def block_norm1(nc, m, s, dram):
    with nc.Block() as block:
        @block.scalar
        def _(act):
            ln_scalar(nc, act, m, s, 2)
            ln_scalar(nc, act, m, s, 3)

        @block.vector
        def _(dve):
            ln_vector(nc, dve, m, s, m.x, m.xn, 2)
            ln_vector(nc, dve, m, s, m.xn, m.xn, 3)


def block_attention1(nc, m, s, dram):
    with ExitStack() as stack:
        def sb(name, shape, dt=F32):
            return stack.enter_context(nc.sbuf_tensor(name, shape, dt))

        w = Named()
        w.mask, w.position = sb("a1_mask", [P, S]), sb("position", [P, S])
        w.lens, w.lensf = sb("lens", [P, B], I32), sb("lensf", [P, B + 1])
        w.gain, w.shift = sb("ln_g", [P, 1]), sb("ln_b", [P, 1])
        w.wo, w.bv, w.bo = sb("wo1", [P, 8, E]), sb("bv1", [P, H * D1]), sb("bo1", [P, E])
        w.head_w = sb("head_w", [P, 2, HEAD_WIDTH])
        w.y32 = sb("y32", [P, S])
        w.y_hi, w.y_lo = sb("y_hi", [P, 2, S], F16), sb("y_lo", [P, 2, S], F16)
        w.q_rot = sb("q_rot", [P, T])
        w.q_hi, w.q_lo = sb("q_hi", [P, 2, T], F16), sb("q_lo", [P, 2, T], F16)
        w.values = sb("values1", [P, 4, SC, 2, D1], F16)
        w.out = sb("out1", [P, TT, H * D1])
        w.stats, w.mv = sb("a1_stats", [P, SC, 6]), sb("a1_mv", [P, SC, 2])
        w.var, w.rstd = sb("a1_var", [P, SC]), sb("a1_rstd", [P, SC])
        w.normed = sb("a1_normed", [P, SC, E])
        attention1(nc, m, s, dram, w)


WV, BK, BQ, HEAD_WIDTH = 2 * P, 2 * P + D1, 2 * P + D1 + 1, 2 * P + D1 + 2


def attention1(nc, m, s, dram, w):
    a = attention_sems(s, "a1")
    ctx_ready, loaded, stat, root = (s.sem(f"a1_{n}") for n in ("ctx_ready", "loaded", "stat", "root"))
    normed_ready, x_fixed, turned, x_taken = (s.sem(f"a1_{n}") for n in ("normed_ready", "x_fixed", "turned", "x_taken"))
    k_hi, keys_ready, lens_ready = (s.sem(f"a1_{n}") for n in ("k_hi", "keys_ready", "lens_ready"))
    q_hi, v_hi, fin_full = (s.sem(f"a1_{n}") for n in ("q_hi", "v_hi", "fin_full"))
    biased, batch_done, mask_done = s.sem("a1_biased"), s.sem("a1_batch_done"), s.sem("a1_mask_done")
    weight_ready = [s.sem(f"a1_weight_ready{j}") for j in range(2)]
    LOADS = 7
    GH = 4
    NG = H // GH
    GU = GH * TT
    START, USES, PREP_HEAD = 7, 4 * H + 2, H - 2
    prime(nc, s)

    def unit(b, g, u):
        return b * UB + g * GU + u

    def use(b, g, v, last):
        return b * USES + g * (4 * GH) + START + 4 * v + (1 if last and v >= 2 else 0)

    def score_uses(before, t):
        if t == 0:
            return [before] * 4, [4 * before + q + 1 for q in range(4)]
        return [before + 2, before + 2, before + 3, before + 3], [4 * before + f for f in (10, 11, 13, 14)]

    def prep_use(b):
        return b * USES + START + 4 * PREP_HEAD

    def fin_use(b):
        return b * USES + START + 4 * H + 1

    def head(b, g, v):
        return b * H + g * GH + v

    def finishes(last, u):
        return u == GU - 1 or (last and u == TT * (GH - 2) - 1)

    with nc.Block() as block:
        @block.sync
        def _(sp):
            def after(semaphore, value):
                sp.wait_ge(semaphore, value)
                on_its_own(sp, s)

            def load_context(batch):
                sp.dma_start(m.ctx[:, 0:FULL, :], dram["ctx"][bass.ds(batch, 1), 0:FULL * P, :]
                             .rearrange("a (c p) d -> p (a c) d", p=P)).then_inc(ctx_ready, 16)
                sp.dma_start(m.ctx[0:REST, FULL, :], dram["ctx"][bass.ds(batch, 1), FULL * P:S, :]
                             .rearrange("a p d -> p (a d)")).then_inc(ctx_ready, 16)

            def load_weights(j, h):
                sp.dma_start(w.head_w[:, j, :], dram["head_w"][bass.ds(h, 1), :, :]
                             .rearrange("a p w -> p (a w)")).then_inc(weight_ready[j], 16)

            load_context(0)
            for dst, src in ((w.position[:, :], dram["position"].to_broadcast([P, S])),
                             (w.lens[:, :], dram["lens"].to_broadcast([P, B])), (w.gain[:, :], dram["ln_g"]),
                             (w.shift[:, :], dram["ln_b"]), (w.wo[:, :, :], dram["wo1"]),
                             (w.bv[:, :], dram["bv1"].to_broadcast([P, H * D1])),
                             (w.bo[:, :], dram["bo1"].to_broadcast([P, E]))):
                sp.dma_start(dst, src).then_inc(loaded, 16)
            for h in range(2):
                load_weights(h, h)
            for h in range(2):
                sp.wait_ge(a.bank_full, 4 + 8 * (h + 1))
                load_weights(h, h + 2)

            def turn(b, g, last):
                for v in range(GH):
                    after(a.bank_full, 4 * use(b, g, v, last) + 16)
                    load_weights(v % 2, v if last else g * GH + v + GH)

            def batch(b, following):
                after(normed_ready, b + 1)
                load_context(following)
                with sp.Fori(0, NG - 1) as g:
                    turn(b, g, False)
                turn(b, NG - 1, True)

            with sp.Fori(0, B - 1) as b:
                batch(b, b + 1)
            batch(B - 1, 0)
            for j in range(2):
                sp.wait_ge(weight_ready[j], 16 * (2 + B * H // 2))

        @block.gpsimd
        def _(pool):
            def norm_context(nb):
                pool.wait_ge(stat, 4 * nb + 4)
                on_its_own(pool, s)
                if not isinstance(nb, int):
                    pool.wait_ge(turned, nb)
                    on_its_own(pool, s)
                for c in range(SC):
                    r = rows(c)
                    ins = nc.gpsimd.tensor_scalar(w.normed[0:r, c, :], m.ctx[0:r, c, :], w.mv[0:r, c, 0:1],
                                                  w.rstd[0:r, c:c + 1], ALU.subtract, ALU.mult)
                ins.then_inc(normed_ready, 1)

            def key_rest(k, j):
                for q, (o, width) in enumerate(SPANS):
                    pool.wait_ge(k_hi, 4 * k + q + 1)
                    nc.gpsimd.tensor_tensor(w.y_lo[:, j, o:o + width], w.y32[:, o:o + width],
                                            w.y_hi[:, j, o:o + width], ALU.subtract).then_inc(keys_ready, 1)

            def turn(b, g, last):
                for v in range(GH):
                    if last and v == 1:
                        norm_context(b + 1)
                    key_rest(head(b, g, v) + 2, v % 2)

            norm_context(0)
            key_rest(0, 0)
            key_rest(1, 1)
            with pool.Fori(0, B) as b:
                with pool.Fori(0, NG - 1) as g:
                    turn(b, g, False)
                turn(b, NG - 1, True)

        @block.tensor
        def _(pe):
            def turn_context(nb, before):
                pe.wait_ge(normed_ready, nb + 1)
                for q, chunks in enumerate(GROUPS):
                    pe.wait_ge(a.bank_free[q], 1 + before)
                    for c in chunks:
                        r = rows(c)
                        ins = nc.tensor.transpose(m.psS[:, c * P:c * P + r], w.normed[0:r, c, :], m.ident[0:r, 0:r])
                    ins.then_inc(a.bank_full, 1)
                pe.wait_ge(x_fixed, nb + 1)
                for t in range(TT):
                    ins = nc.tensor.transpose(m.psM[:, t * P:(t + 1) * P], m.xb[:, t, :], m.ident[:, :])
                ins.then_inc(turned, 1)

            def project_keys(nb, j, uses):
                for q, (o, width) in enumerate(SPANS):
                    pe.wait_ge(a.bank_free[q], 1 + uses[0])
                    nc.tensor.matmul(m.psS[:, o:o + width], w.head_w[:, j, 0:P], m.ctxT[:, o:o + width],
                                     start=True, stop=True).then_inc(a.bank_full, 1)
                pe.wait_ge(x_taken, nb + 1)
                pe.wait_ge(a.bank_free[2], 1 + uses[1])
                nc.tensor.matmul(m.psS[:, 2 * BANK:2 * BANK + T], w.head_w[:, j, P:2 * P], m.xT[:, 0:T],
                                 start=True, stop=True).then_inc(a.bank_full, 1)

            def double_query(taken, before):
                pe.wait_ge(a.bank_free[2], 1 + taken)
                pe.wait_ge(a.bank_free[3], 1 + before)
                nc.tensor.matmul(m.psS[:, 3 * BANK:3 * BANK + T], m.fold[:, :], w.q_rot[:, :],
                                 start=True, stop=True).then_inc(a.bank_full, 1)

            def project_values(j, before):
                for q, chunks in enumerate((range(0, 8), range(8, SC))):
                    pe.wait_ge(a.bank_free[q], 1 + before)
                    for c in chunks:
                        r = rows(c)
                        o = q * BANK + (c - 8 * q) * D1
                        ins = nc.tensor.matmul(m.psS[0:r, o:o + D1], m.ctxT[:, c * P:c * P + r],
                                               w.head_w[:, j, WV:WV + D1], start=True, stop=True)
                    ins.then_inc(a.bank_full, 1)

            def scores(k, j, t, uses, banks=range(4)):
                if t == 0 and banks[0] == 0:
                    pe.wait_ge(keys_ready, 4 * k + 4)
                    pe.wait_ge(a.bank_free[3], uses[3])
                qh, ql = (v[:, j, t * P:(t + 1) * P] for v in (w.q_hi, w.q_lo))
                pe_scores(nc, pe, m, a, uses, lambda o, n: [
                    (qh, w.y_hi[:, j, o:o + n]), (ql, w.y_hi[:, j, o:o + n]), (qh, w.y_lo[:, j, o:o + n])], banks)

            def turn(b, g, last):
                def values(u):
                    return lambda k: pe_values(
                        nc, pe, m, a, unit(b, g, u), u % 2,
                        lambda c, r, n: w.values[0:r, u // TT, c, :, :].rearrange("p a d -> p (a d)")[:, 0:n], D1, k)

                for u in range(GU):
                    n, v, t = unit(b, g, u), u // TT, u % TT
                    before = use(b, g, v, last)
                    uses, _ = score_uses(before, t)
                    following = last and v >= 2
                    pe_unit(lambda banks: scores(head(b, g, v) + 1, (v + 1) % 2, t, uses, banks),
                            lambda k: pe_transpose(nc, pe, m, a, n, u % SLOTS, k),
                            values(u), None if u == 0 or finishes(last, u - 1) else values(u - 1), finishes(last, u),
                            None if t == 0 else lambda: double_query(before + 3, before + 2))
                    if t == 0:
                        pe.wait_ge(weight_ready[v % 2], 16 * (b * (H // 2) + g * (GH // 2) + v // 2 + 2))
                        project_keys(b + 1 if following else b, v % 2, (before + 1, before + 2))
                    else:
                        project_values(v % 2, before + 3)
                    if last and u == TT * (GH - 2) - 1:
                        turn_context(b + 1, prep_use(b))

            pe.wait_ge(loaded, 16 * LOADS)
            turn_context(0, 0)
            for h in range(2):
                pe.wait_ge(weight_ready[h], 16)
                project_keys(0, h, (1 + 2 * h, 2 + 2 * h))
                double_query(3 + 2 * h, 2 + 2 * h)
                project_values(h, 2 + 2 * h)
            for t in range(AHEAD):
                scores(0, 0, t, [5 + t] * 4)
            with pe.Fori(0, B) as b:
                with pe.Fori(0, NG - 1) as g:
                    turn(b, g, False)
                turn(b, NG - 1, True)
                pe.wait_ge(a.out_taken, 1 + UB * (b + 1))
                for q in range(4):
                    pe.wait_ge(a.bank_free[q], 1 + fin_use(b))
                    for c in range(4 * q, 4 * q + 4):
                        ins = nc.tensor.transpose(m.psS[:, c * P:(c + 1) * P],
                                                  w.out[:, c // 8, (c % 8) * P:(c % 8 + 1) * P], m.ident[:, :])
                    ins.then_inc(a.bank_full, 1)
                for q in range(4):
                    pe.wait_ge(a.bank_free[q], 1 + fin_use(b) + 1)
                for t in range(TT):
                    for c in range(8):
                        o = (t * 8 + c) * P
                        ins = nc.tensor.matmul(m.psM[:, t * P:(t + 1) * P], m.oT[:, o:o + P], w.wo[:, c, :],
                                               start=(c == 0), stop=(c == 7))
                ins.then_inc(fin_full, 1)

        @block.scalar
        def _(act):
            def deviation(nb):
                act.wait_ge(stat, 4 * nb + 3)
                nc.scalar.activation(w.var[:, :], w.var[:, :], ACT.Sqrt).then_inc(root, 1)

            def take_context(before):
                for q in range(2):
                    o, width = SPANS[q]
                    act.wait_ge(a.bank_full, 4 * before + q + 1)
                    nc.scalar.activation(m.ctxT[:, o:o + width], m.psS[:, o:o + width], ACT.Identity,
                                         bias=w.shift[:, :], scale=w.gain[:, :]).then_inc(a.bank_free[q], 1)

            def key_hi(j, before):
                for q, (o, width) in enumerate(SPANS):
                    act.wait_ge(a.bank_free[q], 1 + before + 1)
                    nc.scalar.copy(w.y_hi[:, j, o:o + width], w.y32[:, o:o + width]).then_inc(k_hi, 1)

            def query_hi(j, full):
                act.wait_ge(a.bank_full, full)
                nc.scalar.activation(w.q_hi[:, j, :], m.psS[:, 3 * BANK:3 * BANK + T], ACT.Copy,
                                     scale=float(D1) ** -0.5).then_inc(q_hi, 1)

            def value_hi(slot, full):
                for q, views in enumerate(value_views(m, w, slot, 0)):
                    act.wait_ge(a.bank_full, full + q)
                    for src, dst, _ in views:
                        ins = nc.scalar.copy(dst, src)
                    ins.then_inc(v_hi, 1)

            def turn(b, g, last):
                for u in range(GU):
                    n, v, t = unit(b, g, u), u // TT, u % TT
                    full = 4 * use(b, g, v, last)
                    for k in range(4):
                        if t == 1 and k == 1:
                            query_hi(v % 2, full + 12)
                        act_group_hi(nc, act, m, a, n, u % 2, k)
                    act_exp(nc, act, m, a, n + AHEAD, (u + AHEAD) % SLOTS)
                    if t == 0:
                        key_hi(v % 2, use(b, g, v, last) + 1)
                    else:
                        value_hi((v + 2) % 4, full + 15)
                    if last and u == 0:
                        deviation(b + 1)
                    if last and u == TT * (GH - 2) - 1:
                        take_context(prep_use(b))

            act.wait_ge(loaded, 16 * LOADS)
            deviation(0)
            take_context(0)
            for h in range(2):
                key_hi(h, 1 + 2 * h)
                query_hi(h, 4 + 8 * h + 6)
                value_hi(h, 4 + 8 * h + 7)
            for t in range(AHEAD):
                act_exp(nc, act, m, a, t, t)
            with act.Fori(0, B) as b:
                with act.Fori(0, NG - 1) as g:
                    turn(b, g, False)
                turn(b, NG - 1, True)
                for q in range(2):
                    act.wait_ge(a.bank_full, 4 * fin_use(b) + q + 1)
                    nc.scalar.copy(m.oT[:, q * BANK:(q + 1) * BANK],
                                   m.psS[:, q * BANK:(q + 1) * BANK]).then_inc(a.bank_free[q], 1)

        @block.vector
        def _(dve):
            def statistics(nb):
                dve.wait_ge(ctx_ready, 32 * (nb + 1))
                for c in range(SC):
                    ins = nc.vector.bn_stats(w.stats[0:rows(c), c, :], m.ctx[0:rows(c), c, :])
                ins.then_inc(stat, 1)
                dve.wait_ge(stat, 4 * nb + 1)
                if not isinstance(nb, int):
                    dve.wait_ge(normed_ready, nb)
                    on_its_own(dve, s)
                for c in range(SC):
                    ins = nc.vector.bn_aggr(w.mv[0:rows(c), c, :], w.stats[0:rows(c), c, :])
                ins.then_inc(stat, 1)
                dve.wait_ge(stat, 4 * nb + 2)
                nc.vector.tensor_scalar(w.var[:, :], w.mv[:, :, 1], EPS, None, ALU.add).then_inc(stat, 1)

            def inverse(nb):
                dve.wait_ge(root, nb + 1)
                nc.vector.reciprocal(w.rstd[:, :], w.var[:, :]).then_inc(stat, 1)

            def next_mask(nb):
                nc.vector.tensor_scalar(w.mask[:, :], w.position[:, :], w.lensf[:, bass.ds(nb, 1)], NEG,
                                        ALU.is_ge, ALU.mult).then_inc(mask_done, 1)
                dve.wait_ge(mask_done, nb + 1)

            def take_context(nb, before):
                for q in range(2, 4):
                    o, width = SPANS[q]
                    dve.wait_ge(a.bank_full, 4 * before + q + 1)
                    nc.vector.tensor_scalar(m.ctxT[:, o:o + width], m.psS[:, o:o + width], w.gain[:, :], w.shift[:, :],
                                            ALU.mult, ALU.add).then_inc(a.bank_free[q], 1)
                dve.wait_ge(turned, nb + 1)
                nc.vector.tensor_scalar(m.xT[:, 0:T], m.psM[:, 0:T], w.gain[:, :], w.shift[:, :],
                                        ALU.mult, ALU.add).then_inc(x_taken, 1)

            def fix_x(nb):
                if not isinstance(nb, int):
                    dve.wait_ge(turned, nb)
                nc.vector.tensor_copy(m.xb[:, :, :], m.xn[:, bass.ds(nb * TT, TT), :]).then_inc(x_fixed, 1)

            def rotate(k, j, full, first):
                if not first:
                    dve.wait_ge(keys_ready, 4 * k)
                for q, (o, width) in enumerate(SPANS):
                    dve.wait_ge(a.bank_full, full + q + 1)
                    nc.vector.scalar_tensor_tensor(w.y32[:, o:o + width], m.psS[:, o:o + width],
                                                   w.head_w[:, j, BK:BK + 1], m.cos_sin[:, o:o + width], ALU.add,
                                                   ALU.mult).then_inc(a.bank_free[q], 1)
                dve.wait_ge(a.bank_full, full + 5)
                nc.vector.scalar_tensor_tensor(w.q_rot[:, :], m.psS[:, 2 * BANK:2 * BANK + T],
                                               w.head_w[:, j, BQ:BQ + 1], m.cos_sin[:, 0:T], ALU.add,
                                               ALU.mult).then_inc(a.bank_free[2], 1)

            def query_lo(k, j):
                dve.wait_ge(q_hi, k + 1)
                nc.vector.scalar_tensor_tensor(w.q_lo[:, j, :], m.psS[:, 3 * BANK:3 * BANK + T], float(D1) ** -0.5,
                                               w.q_hi[:, j, :], ALU.mult,
                                               ALU.subtract).then_inc(a.bank_free[3], 1)

            def value_lo(k, slot):
                for q, views in enumerate(value_views(m, w, slot, 1)):
                    dve.wait_ge(v_hi, 2 * k + q + 1)
                    for src, dst, hi in views:
                        ins = nc.vector.tensor_tensor(dst, src, hi, ALU.subtract)
                    ins.then_inc(a.bank_free[q], 1)

            def mask_max(uses, fulls, slot, q):
                return dve_mask_max(nc, dve, m, a, fulls, uses, slot, lambda o, n: w.mask[:, o:o + n], q)

            def turn(b, g, last):
                def take_out(u):
                    o = g * (GH * D1) + (u // TT) * D1
                    return dve_take_out(nc, dve, m, a, unit(b, g, u), u % SLOTS,
                                        w.out[:, u % TT, bass.ds(o, D1)], w.bv[:, bass.ds(o, D1)], D1)

                for u in range(GU):
                    n, v, t = unit(b, g, u), u // TT, u % TT
                    before = use(b, g, v, last)
                    uses, fulls = score_uses(before, t)
                    k = head(b, g, v) + 2
                    if last and u == GU - AHEAD:
                        next_mask(b + 1)
                    dve_unit(nc, dve, m, a, n, u % 2,
                             lambda q: mask_max(uses, fulls, (u + AHEAD) % SLOTS, q),
                             None if u == 0 or finishes(last, u - 1) else take_out(u - 1),
                             take_out(u) if finishes(last, u) else None,
                             None if t == 0 else lambda: query_lo(k, v % 2))
                    if t == 0:
                        rotate(k, v % 2, 4 * before + 4, False)
                    else:
                        value_lo(k, (v + 2) % 4)
                    if last and u == 0:
                        statistics(b + 1)
                    if last and u == 1:
                        inverse(b + 1)
                    if last and u == TT * (GH - 2) - 1:
                        fix_x(b + 1)
                        take_context(b + 1, prep_use(b))

            dve.wait_ge(loaded, 16 * LOADS)
            nc.vector.memset(w.lensf[:, B:B + 1], 0.0)
            nc.vector.memset(w.mv[:, :, :], 0.0)
            nc.vector.tensor_copy(w.lensf[:, 0:B], w.lens[:, :]).then_inc(lens_ready, 1)
            dve.wait_ge(lens_ready, 1)
            fix_x(0)
            next_mask(0)
            statistics(0)
            inverse(0)
            take_context(0, 0)
            for h in range(2):
                rotate(h, h, 4 + 8 * h, h == 0)
                query_lo(h, h)
                value_lo(h, h)
            for t in range(AHEAD):
                fulls = [4 * (5 + t) + q + 1 for q in range(4)]
                for q in range(4):
                    mask_max([5 + t] * 4, fulls, t, q)
                dve_negmax(nc, dve, m, a, [5 + t] * 4, t)
            with dve.Fori(0, B) as b:
                with dve.Fori(0, NG - 1) as g:
                    turn(b, g, False)
                turn(b, NG - 1, True)
                for q in range(2, 4):
                    dve.wait_ge(a.bank_full, 4 * fin_use(b) + q + 1)
                    nc.vector.tensor_copy(m.oT[:, q * BANK:(q + 1) * BANK],
                                          m.psS[:, q * BANK:(q + 1) * BANK]).then_inc(a.bank_free[q], 1)
                dve.wait_ge(fin_full, b + 1)
                for t in range(TT):
                    ins = nc.vector.tensor_tensor(m.tmp[:, t, :], m.psM[:, t * P:(t + 1) * P], w.bo[:, :], ALU.add)
                ins.then_inc(biased, 1)
                dve.wait_ge(biased, b + 1)
                xs = m.x[:, bass.ds(b * TT, TT), :]
                nc.vector.scalar_tensor_tensor(xs, m.tmp[:, :, :], m.gates[:, 2:3], xs,
                                               ALU.mult, ALU.add).then_inc(batch_done, 1)
            dve.wait_ge(batch_done, B)


def value_views(m, w, slot, part):
    whole = FULL - 8

    def views(c0, c1, r, o):
        src = m.psS[0:r, o:o + (c1 - c0) * D1].rearrange("p (c d) -> p c d", d=D1)
        return src, w.values[0:r, slot, c0:c1, part, :], w.values[0:r, slot, c0:c1, 0, :]

    return ([views(0, 8, P, 0)],
            [views(8, FULL, P, BANK), views(FULL, SC, REST, BANK + whole * D1)])


def block_route1(nc, m, s, dram):
    normed, turned, xt_act, xt_dve = (s.sem(f"r1_{n}") for n in ("normed", "turned", "xt_act", "xt_dve"))
    logits_done, sig_done, steps, loaded = (s.sem(f"r1_{n}") for n in ("logits", "sig", "steps", "loaded"))
    with ExitStack() as stack:
        def sb(name, shape, dt=F32):
            return stack.enter_context(nc.sbuf_tensor(name, shape, dt))

        wg, bias = sb("r1_wg", [P, X1]), sb("r1_bias", [P, X1])
        score, masked, above, equal, seen = (sb(f"r1_{n}", [P, NT, X1]) for n in
                                             ("score", "masked", "above", "equal", "seen"))
        best = sb("r1_best", [P, NT, GR])
        first, level = sb("r1_first", [P, NT, GR, GR]), sb("r1_level", [P, NT, GR, GR])
        keep, top8 = sb("r1_keep", [P, NT, GR]), sb("r1_top8", [P, NT, 8])
        total = sb("r1_total", [P, NT])
        lg = m.psT[2][:, :].rearrange("p (k e) -> p k e", e=X1)

        def over_e(ap):
            return ap.to_broadcast([P, NT, X1])

        with nc.Block() as block:
            @block.sync
            def _(sp):
                sp.dma_start(wg[:, :], dram["wg1"]).then_inc(loaded, 16)
                sp.dma_start(bias[:, :], dram["expert_bias"].to_broadcast([P, X1])).then_inc(loaded, 16)

            @block.tensor
            def _(pe):
                pe_turn_x(nc, pe, m, normed, turned)
                pe.wait_ge(xt_act, 1)
                pe.wait_ge(xt_dve, 1)
                pe.wait_ge(loaded, 32)
                for k in range(NT):
                    ins = nc.tensor.matmul(lg[:, k, :], m.xT[:, k * P:(k + 1) * P], wg[:, :], start=True, stop=True)
                ins.then_inc(logits_done, 1)

            @block.scalar
            def _(act):
                ln_scalar(nc, act, m, s, 4)
                act.wait_ge(turned, 1)
                nc.scalar.copy(m.xT[:, 0:TOK // 2], m.psS[:, 0:TOK // 2]).then_inc(xt_act, 1)
                act.wait_ge(logits_done, 1)
                nc.scalar.activation(score[:, :, :], lg, ACT.Sigmoid).then_inc(sig_done, 1)

            @block.vector
            def _(dve):
                ln_vector(nc, dve, m, s, m.x, m.xn, 4)
                nc.vector.memset(total[:, :], 0.0).then_inc(normed, 1)
                dve.wait_ge(turned, 2)
                nc.vector.tensor_copy(m.xT[:, TOK // 2:TOK], m.psS[:, TOK // 2:TOK]).then_inc(xt_dve, 1)
                dve.wait_ge(sig_done, 1)
                dve.wait_ge(loaded, 32)
                step, _ = chain(dve, steps)
                step(nc.vector.tensor_tensor(masked[:, :, :], score[:, :, :],
                                             bias[:, :].unsqueeze(1).to_broadcast([P, NT, X1]), ALU.add))
                step(nc.vector.tensor_reduce(best[:, :, :], masked[:, :, :].rearrange("p k (g i) -> p k g i", g=GR),
                                             AX.X, ALU.max))
                four = [P, NT, GR, GR]
                other, own = best[:, :, :].unsqueeze(2).to_broadcast(four), best[:, :, :].unsqueeze(3).to_broadcast(four)
                step(nc.vector.tensor_tensor(first[:, :, :, :], other, own, ALU.is_gt))
                step(nc.vector.tensor_tensor(level[:, :, :, :], other, own, ALU.is_equal))
                step(nc.vector.tensor_tensor(level[:, :, :, :], level[:, :, :, :],
                                             m.earlier[:, :, :].unsqueeze(1).to_broadcast(four), ALU.mult))
                step(nc.vector.tensor_tensor(first[:, :, :, :], first[:, :, :, :], level[:, :, :, :], ALU.add))
                step(nc.vector.tensor_reduce(keep[:, :, :], first[:, :, :, :], AX.X, ALU.add))
                step(nc.vector.tensor_scalar(keep[:, :, :], keep[:, :, :], float(KEEP), None, ALU.is_lt))
                grouped = masked[:, :, :].rearrange("p k (g i) -> p k g i", g=GR)
                step(nc.vector.tensor_tensor(grouped, grouped,
                                             keep[:, :, :].unsqueeze(3).to_broadcast([P, NT, GR, X1 // GR]), ALU.mult))
                for k in range(NT):
                    ins = nc.vector.max(top8[:, k, :], masked[:, k, :])
                step(ins)
                least = over_e(top8[:, :, TOP - 1:TOP])
                step(nc.vector.tensor_tensor(above[:, :, :], masked[:, :, :], least, ALU.is_gt))
                step(nc.vector.tensor_tensor(equal[:, :, :], masked[:, :, :], least, ALU.is_equal))
                step(nc.vector.tensor_reduce(total[:, :], above[:, :, :], AX.X, ALU.add))
                step(nc.vector.tensor_tensor_scan(seen[:, :, :].rearrange("p k e -> p (k e)"), m.scanreset[:, :],
                                                  equal[:, :, :].rearrange("p k e -> p (k e)"), 0.0,
                                                  ALU.mult, ALU.add))
                step(nc.vector.tensor_tensor(seen[:, :, :], seen[:, :, :], over_e(total[:, :].unsqueeze(2)), ALU.add))
                step(nc.vector.scalar_tensor_tensor(equal[:, :, :], seen[:, :, :], float(TOP), equal[:, :, :],
                                                    ALU.is_le, ALU.mult))
                step(nc.vector.tensor_tensor(above[:, :, :], above[:, :, :], equal[:, :, :], ALU.add))
                step(nc.vector.tensor_tensor(score[:, :, :], score[:, :, :], above[:, :, :], ALU.mult))
                step(nc.vector.tensor_reduce(total[:, :], score[:, :, :], AX.X, ALU.add))
                step(nc.vector.tensor_scalar(total[:, :], total[:, :], 1e-20, None, ALU.add))
                step(nc.vector.reciprocal(total[:, :], total[:, :]))
                step(nc.vector.tensor_tensor(score[:, :, :], score[:, :, :], over_e(total[:, :].unsqueeze(2)), ALU.mult))
                step(nc.vector.tensor_scalar(m.combine[:, :, :], score[:, :, :], SCALE1, None, ALU.mult))


def block_experts1(nc, m, s, dram):
    N = PAIRS + 1
    KB = BANK // P
    loaded, weights_turned, weights_ready, mixed = (s.sem(f"e1_{n}") for n in ("loaded", "turned", "ready", "mixed"))
    projected, silu_done = s.sem("e1_projected"), s.sem("e1_silu")
    inner_done, out_full, added = (s.from_one(f"e1_{n}") for n in ("inner_done", "out_full", "added"))
    with ExitStack() as stack:
        def sb(name, shape, dt=F32):
            return stack.enter_context(nc.sbuf_tensor(name, shape, dt))

        wgate, wup, wdown = (sb(n, [P, N, P]) for n in ("e1_gate", "e1_up", "e1_down"))
        spread = sb("e1_spread", [X1 + 1, N, P])
        cT = sb("e1_cT", [X1 + 1, TOK])
        silu, prod, inner = (sb(f"e1_{n}", [P, 2, BANK]) for n in ("silu", "prod", "inner"))
        prime(nc, s)

        def turn(blk, p):
            return blk * N + p

        banks = [(m.psS[:, 0:BANK], m.psS[:, BANK:2 * BANK], m.psT[0][:, :]),
                 (m.psS[:, 2 * BANK:3 * BANK], m.psS[:, 3 * BANK:4 * BANK], m.psT[1][:, :])]

        with nc.Block() as block:
            @block.sync
            def _(sp):
                for dst, src in ((wgate, dram["e1_gate"]), (wup, dram["e1_up"]), (wdown, dram["e1_down"]), (spread, dram["spread"])):
                    sp.dma_start(dst[:, :, :], src).then_inc(loaded, 16)

            @block.tensor
            def _(pe):
                pe.wait_ge(loaded, 64)
                for k in range(NT):
                    ins = nc.tensor.transpose(m.psS[0:X1, k * P:(k + 1) * P], m.combine[:, k, :], m.ident[:, :])
                ins.then_inc(weights_turned, 1)
                pe.wait_ge(weights_ready, 2)

                def up(blk, p):
                    n = turn(blk, p)
                    gate, upper, weight = banks[p % 2]
                    if p >= 2:
                        pe.wait_ge(inner_done, 1 + n - 1)
                    else:
                        pe.wait_ge(inner_done, 1 + blk * N)
                    x = m.xT[:, bass.ds(blk * BANK, BANK)]
                    nc.tensor.matmul(gate, wgate[:, p, :], x, start=True, stop=True)
                    nc.tensor.matmul(upper, wup[:, p, :], x, start=True, stop=True)
                    nc.tensor.matmul(weight, spread[:, p, :], cT[:, bass.ds(blk * BANK, BANK)],
                                     start=True, stop=True).then_inc(projected, 1)

                def down(blk, p):
                    pe.wait_ge(inner_done, 1 + turn(blk, p) + 1)
                    if p == 0:
                        pe.wait_ge(added, 1 + blk)
                    for k in range(KB):
                        ins = nc.tensor.matmul(m.psO[:, k * P:(k + 1) * P], inner[:, p % 2, k * P:(k + 1) * P],
                                               wdown[:, p, :], start=(p == 0 and k == 0), stop=(p == N - 1),
                                               skip_group_check=True)
                    ins.then_inc(out_full, 1)

                with pe.Fori(0, TOK // BANK) as blk:
                    up(blk, 0)
                    for p in range(N):
                        if p + 1 < N:
                            up(blk, p + 1)
                        down(blk, p)

            @block.scalar
            def _(act):
                act.wait_ge(weights_turned, 1)
                nc.scalar.copy(cT[0:X1, :], m.psS[0:X1, :]).then_inc(weights_ready, 1)
                with act.Fori(0, TOK // BANK) as blk:
                    for p in range(N):
                        n = turn(blk, p)
                        act.wait_ge(projected, n + 1)
                        nc.scalar.activation(silu[:, p % 2, :], banks[p % 2][0], ACT.Silu).then_inc(silu_done, 1)

            @block.vector
            def _(dve):
                nc.vector.memset(cT[X1:X1 + 1, :], 1.0).then_inc(weights_ready, 1)
                with dve.Fori(0, TOK // BANK) as blk:
                    for p in range(N):
                        n = turn(blk, p)
                        dve.wait_ge(silu_done, n + 1)
                        nc.vector.tensor_tensor(prod[:, p % 2, :], banks[p % 2][1], silu[:, p % 2, :],
                                                ALU.mult).then_inc(mixed, 1)
                        dve.wait_ge(mixed, n + 1)
                        if p >= 2:
                            dve.wait_ge(out_full, 1 + n - 1)
                        else:
                            dve.wait_ge(out_full, 1 + blk * N)
                        nc.vector.tensor_tensor(inner[:, p % 2, :], banks[p % 2][2], prod[:, p % 2, :],
                                                ALU.mult).then_inc(inner_done, 1)
                    dve.wait_ge(out_full, 1 + turn(blk, N))
                    xs = m.x[:, bass.ds(blk * KB, KB), :]
                    nc.vector.scalar_tensor_tensor(xs, m.psO[:, :].rearrange("p (k d) -> p k d", d=E),
                                                   m.gates[:, 3:4], xs, ALU.mult, ALU.add).then_inc(added, 1)
                dve.wait_ge(added, 1 + TOK // BANK)


def build(nc, dram):
    with ExitStack() as stack:
        def sb(name, shape, dt=F32):
            return stack.enter_context(nc.sbuf_tensor(name, shape, dt))

        def sem(name):
            return stack.enter_context(nc.semaphore(name))

        to_prime = []

        def from_one(name, start=1):
            to_prime.append((sem(name), start))
            return to_prime[-1][0]

        m, s = Named(), Named()
        m.s = s
        s.sem, s.from_one, s.to_prime = sem, from_one, to_prime
        s.load, s.ln, s.ln_sqrt, s.tanh = (sem(n) for n in ("load", "ln", "ln_sqrt", "tanh"))
        s.stored, s.passed, s.weights = (sem(n) for n in ("stored", "passed", "weights"))
        m.x, m.xn, m.xT = sb("x", [P, NT, E]), sb("xn", [P, NT + TT, E]), sb("xT", [P, TOK])
        m.stats, m.mv = sb("stats", [P, NT, 6]), sb("mv", [P, NT, 2])
        m.var, m.rstd = sb("var", [P, NT]), sb("rstd", [P, NT])
        m.ident, m.fold, m.below, m.ones = (sb(n, [P, P]) for n in ("ident", "fold", "below", "ones"))
        m.cos_sin = sb("cos_sin", [P, S])
        m.earlier, m.weight8 = sb("earlier", [P, GR, GR]), sb("weight8", [P, X0])
        m.headmask, m.scanreset = sb("headmask", [P, 4]), sb("scanreset", [P, NT * X1])
        m.gates = sb("gates", [P, 4])
        m.probs = sb("probs", [P, SLOTS, S])
        m.probsT_hi, m.probsT_lo = sb("probsT_hi", [P, 2, SC, P], F16), sb("probsT_lo", [P, 2, SC, P], F16)
        m.max4, m.negmax = sb("max4", [P, SLOTS, 4]), sb("negmax", [P, SLOTS])
        m.sums, m.rsum, m.part = sb("sums", [P, SLOTS]), sb("rsum", [P, 1]), sb("part", [P, D1])
        m.psS = stack.enter_context(nc.psum_tensor("psS", [P, 4 * BANK], F32))
        m.psT = [stack.enter_context(nc.psum_tensor(f"psT{i}", [P, BANK], F32)) for i in range(3)]
        m.psO = stack.enter_context(nc.psum_tensor("psO", [P, BANK], F32))
        m.psM = m.psO[:, 2 * D1:2 * D1 + T]
        m.ctx, m.ctxT = sb("ctx", [P, SC, E]), sb("ctxT", [P, S])
        m.xb, m.tmp, m.oT = sb("xb", [P, TT, E]), sb("tmp", [P, TT, E]), sb("oT", [P, TT * 1024])
        m.wq0, m.wk0, m.wv0, m.wo0 = (sb(n, [P, P]) for n in ("wq0", "wk0", "wv0", "wo0"))
        m.bq0, m.bk0 = sb("bq0", [P, 1]), sb("bk0", [P, 1])
        m.bv0, m.bo0 = sb("bv0", [P, E]), sb("bo0", [P, E])
        m.gate = sb("gate", [P, NT, X0])
        m.combine = sb("combine", [P, NT, X1])

        m.loaded = dict(ident=m.ident[:, :], fold=m.fold[:, :], below=m.below[:, :], cos_sin=m.cos_sin[:, :],
                        earlier=m.earlier[:, :, :], weight8=m.weight8[:, :], headmask=m.headmask[:, :],
                        scanreset=m.scanreset[:, :], ones=m.ones[:, :], gates=m.gates[:, :],
                        wq0=m.wq0[:, :], wk0=m.wk0[:, :], wv0=m.wv0[:, :],
                        wo0=m.wo0[:, :], bq0=m.bq0[:, :], bk0=m.bk0[:, :], bv0=m.bv0[:, :], bo0=m.bo0[:, :])
        d = dram
        m.source = dict(ident=d["ident"], fold=d["fold"], below=d["below"], cos_sin=d["cos_sin"], earlier=d["earlier"],
                        weight8=d["weight8"], headmask=d["headmask"], scanreset=d["scanreset"], ones=d["ones"],
                        gates=d["gates"].to_broadcast([P, 4]),
                        wq0=d["wq0"], wk0=d["wk0"], wv0=d["wv0"], wo0=d["wo0"], bq0=d["bq0"], bk0=d["bk0"],
                        bv0=d["bv0"].to_broadcast([P, E]), bo0=d["bo0"].to_broadcast([P, E]))

        block_load(nc, m, s, dram)
        block_attention0(nc, m, s, dram)
        block_route0(nc, m, s, dram)
        block_experts0(nc, m, s, dram)
        block_norm1(nc, m, s, dram)
        block_attention1(nc, m, s, dram)
        block_route1(nc, m, s, dram)
        block_experts1(nc, m, s, dram)
        with nc.Block() as block:
            @block.sync
            def _(sp):
                sp.dma_start(dram["out"].rearrange("b (t p) d -> p (b t) d", p=P), m.x[:, :, :]).then_inc(s.stored, 16)
                sp.wait_ge(s.stored, 16)


def constants():
    p = np.arange(P)
    f = np.float32
    inv = (1.0 / np.float64(10000.0) ** (np.arange(0, D1, 2, dtype=np.float64) / D1)).astype(f)
    ang = np.repeat(np.arange(S, dtype=f)[:, None] * inv[None, :], 2, axis=1).T
    sign = np.where(np.arange(D1) % 2 == 0, -1.0, 1.0).astype(f)[:, None]
    return dict(
        ident=np.eye(P, dtype=f),
        fold=(p[:, None] % D1 == p[None, :] % D1).astype(f),
        below=(p[:, None] < p[None, :]).astype(f),
        ones=np.ones((P, P), f),
        cos_sin=np.concatenate([np.cos(ang), np.sin(ang) * sign]).astype(f),
        earlier=np.broadcast_to((np.arange(GR)[None, :] < np.arange(GR)[:, None]).astype(f), (P, GR, GR)).copy(),
        weight8=np.broadcast_to(np.arange(X0, 0, -1).astype(f), (P, X0)).copy(),
        position=np.arange(S, dtype=f)[None, :],
        spread=spread(),
        headmask=((p[:, None] % 32) // D0 == np.arange(4)[None, :]).astype(f),
        scanreset=np.broadcast_to((np.arange(NT * X1) % X1 != 0).astype(f), (P, NT * X1)).copy(),
    )


def spread():
    out = np.zeros((X1 + 1, PAIRS + 1, P), np.float32)
    for e in range(X1):
        out[e, e // 2, e % 2 * I1:(e % 2 + 1) * I1] = 1
    out[X1, PAIRS] = 1
    return out


def pairs(routed, shared):
    return np.concatenate([routed.reshape(PAIRS, P, E), shared[None]]).transpose(2, 0, 1)


def head_weights(a):
    swap = np.arange(D1) ^ 1

    def both(name):
        w = a[f"L1_xattn_{name}"].reshape(-1, H, D1)
        return np.concatenate([w, w[:, :, swap]], axis=2).transpose(1, 0, 2)

    wv = a["L1_xattn_Wv"].reshape(E, H, D1).transpose(1, 0, 2)
    return np.concatenate([both("Wk"), both("Wq"), wv, both("bk").transpose(0, 2, 1),
                           both("bq").transpose(0, 2, 1)], axis=2)


def kernel(**inputs):
    import concourse.bacc as bacc
    from concourse.bass_utils import run_bass_kernel_spmd

    a = {k: np.asarray(v) for k, v in inputs.items()}
    arrays = dict(constants())
    arrays.update(
        x=a["x"], ctx=a["ctx_1024"], attn_mask=a["fside_SxS2_0"], pad=a["mask_BxS2_bf0"],
        gates=np.stack([a["g_xattn"], a["g_ffn"]], axis=1).reshape(1, 4),
        wq0=a["L0_xattn_Wq"].T, wk0=a["L0_xattn_Wk"].T, wv0=a["L0_xattn_Wv"].T, wo0=a["L0_xattn_Wo"].T,
        bq0=a["L0_xattn_bq"][:, None], bk0=a["L0_xattn_bk"][:, None],
        wg=a["L0_ffn_Wg"], w1=a["L0_ffn_W1"], w2=a["L0_ffn_W2"],
        lens=a["_lenS2"][None, :], ln_g=a["L1_xattn_ln_g"][:, None], ln_b=a["L1_xattn_ln_b"][:, None],
        head_w=head_weights(a), wo1=a["L1_xattn_Wo"].reshape(8, P, E).transpose(1, 0, 2),
        bv1=a["L1_xattn_bv"][None, :], bo1=a["L1_xattn_bo"][None, :],
        wg1=a["L1_ffn_gate_weight"].T, expert_bias=a["L1_ffn_e_score_correction_bias"][None, :],
        e1_gate=pairs(a["L1_ffn_experts_gate_up"][:, :I1], a["L1_ffn_shared_gate_w"]),
        e1_up=pairs(a["L1_ffn_experts_gate_up"][:, I1:], a["L1_ffn_shared_up_w"]),
        e1_down=np.concatenate([a["L1_ffn_experts_down"].transpose(0, 2, 1).reshape(PAIRS, P, E),
                                a["L1_ffn_shared_down_w"].T[None]]).transpose(1, 0, 2),
        bv0=a["L0_xattn_bv"][None, :], bo0=a["L0_xattn_bo"][None, :],
    )
    nc = bacc.Bacc("TRN2", target_bir_lowering=False, num_devices=1)
    dram, given = {}, {}
    for name, v in arrays.items():
        v = np.ascontiguousarray(v)
        given[f"in_{name}"] = v
        dram[name] = nc.dram_tensor(f"in_{name}", v.shape, mybir.dt.from_np(v.dtype), kind="ExternalInput").ap()
    dram["out"] = nc.dram_tensor("out_x", (B, T, E), F32, kind="ExternalOutput").ap()
    build(nc, dram)
    result = run_bass_kernel_spmd(nc, [given], core_ids=[0])
    return result.results[0]["out_x"]
```

```python
from contextlib import ExitStack

import numpy as np

import concourse.bass as bass
import concourse.mybir as mybir
from concourse.alu_op_type import AluOpType as ALU

ACT = mybir.ActivationFunctionType
AX = mybir.AxisListType
F32 = mybir.dt.float32
F16 = mybir.dt.float16
I32 = mybir.dt.int32
U8 = mybir.dt.uint8

P = 128
B, T, E = 8, 256, 128
S = 1601
H = 16
TT = T // P
NT = B * TT
TOK = B * T
SC = -(-S // P)
FULL = S // P
REST = S - FULL * P
BANK = 512
SPANS = [(o, min(BANK, S - o)) for o in range(0, S, BANK)]
GROUPS = [range(4 * g, min(4 * g + 4, SC)) for g in range(4)]
D0 = E // H
D1 = 64
EPS = 1e-5
NEG = -1e30
LOWEST = -3e38
X0, CAP = 8, TOK // 8
F0 = 256
X1, I1 = 32, 64
PAIRS = X1 * I1 // P
GR, KEEP, TOP = 8, 4, 6
SCALE1 = 2.5
UB = H * TT
AHEAD = 2
SLOTS = 4


def on_its_own(eng, s):
    eng.sem_inc(s.passed, 1)


def rows(c):
    return P if c < FULL else REST


class Named:
    pass


def prime(nc, s):
    with nc.Block() as block:
        @block.sync
        def _(sp):
            for semaphore in s.to_prime:
                sp.sem_inc(semaphore[0], semaphore[1])
    s.to_prime.clear()


def ln_vector(nc, dve, m, s, src, dst, done_before):
    base = 6 * done_before
    for k in range(NT):
        ins = nc.vector.bn_stats(m.stats[:, k, :], src[:, k, :])
    ins.then_inc(s.ln, 1)
    dve.wait_ge(s.ln, base + 1)
    for k in range(NT):
        ins = nc.vector.bn_aggr(m.mv[:, k, :], m.stats[:, k, :])
    ins.then_inc(s.ln, 1)
    dve.wait_ge(s.ln, base + 2)
    nc.vector.tensor_scalar(m.var[:, 0:NT], m.mv[:, 0:NT, 1], EPS, None, ALU.add).then_inc(s.ln, 1)
    dve.wait_ge(s.ln_sqrt, done_before + 1)
    nc.vector.reciprocal(m.rstd[:, 0:NT], m.var[:, 0:NT]).then_inc(s.ln, 1)
    dve.wait_ge(s.ln, base + 4)
    for k in range(NT):
        ins = nc.vector.tensor_scalar(dst[:, k, :], src[:, k, :], m.mv[:, k, 0:1], m.rstd[:, k:k + 1],
                                      ALU.subtract, ALU.mult)
    ins.then_inc(s.ln, 2)
    dve.wait_ge(s.ln, base + 6)


def ln_scalar(nc, act, m, s, done_before):
    act.wait_ge(s.ln, 6 * done_before + 3)
    nc.scalar.activation(m.var[:, 0:NT], m.var[:, 0:NT], ACT.Sqrt).then_inc(s.ln_sqrt, 1)


def pe_scores(nc, pe, m, a, use, products, banks=range(4)):
    for q in banks:
        o, w = SPANS[q]
        pe.wait_ge(a.bank_free[q], 1 + use)
        terms = products(o, w)
        for i, (lhsT, rhs) in enumerate(terms):
            ins = nc.tensor.matmul(m.psS[:, o:o + w], lhsT, rhs, start=(i == 0), stop=(i == len(terms) - 1))
        ins.then_inc(a.bank_full, 1)


def pe_transpose(nc, pe, m, a, n, slot, g):
    if g == 0:
        pe.wait_ge(a.exp_done, n + 1)
        pe.wait_ge(a.copied_lo, LO_START + 4 * n - 3)
    if g == 1:
        pe.wait_ge(a.copied_lo, LO_START + 4 * n)
    if g == 3:
        pe.wait_ge(a.copied_lo, LO_START + 4 * n + 2)
    for c in GROUPS[g]:
        o = (c % 4) * P
        ins = nc.tensor.transpose(m.psT[GROUP_BANK[g]][0:rows(c), o:o + P],
                                  m.probs[:, slot, c * P:c * P + rows(c)], m.ident[:, :])
    ins.then_inc(a.group_full, 1)


def pe_values(nc, pe, m, a, n, buf, values, d, g):
    if g == 0:
        pe.wait_ge(a.out_taken, 1 + n)
    pe.wait_ge(a.copied_lo, LO_START + 4 * n + g + 1)
    for c in GROUPS[g]:
        r = rows(c)
        nc.tensor.matmul(m.psO[:, 0:2 * d], m.probsT_hi[0:r, buf, c, :], values(c, r, 2 * d),
                         start=(c == 0), stop=False)
        ins = nc.tensor.matmul(m.psO[:, 0:d], m.probsT_lo[0:r, buf, c, :], values(c, r, d),
                               start=False, stop=(c == SC - 1))
    if g == 3:
        ins.then_inc(a.out_full, 1)


def dve_mask_max(nc, dve, m, a, use, slot, mask, q):
    o, w = SPANS[q]
    dve.wait_ge(a.bank_full, 4 * use + q + 1)
    on_its_own(dve, m.s)
    nc.vector.tensor_tensor_reduce(m.probs[:, slot, o:o + w], m.psS[:, o:o + w], mask(o, w), 1.0, LOWEST,
                                   ALU.add, ALU.max, m.max4[:, slot, q:q + 1]).then_inc(a.bank_free[q], 1)


def nothing(group):
    pass


def done():
    pass


def dve_negmax(nc, dve, m, a, use, slot):
    for k in range(4):
        dve.wait_ge(a.bank_free[k], 1 + use + 1)
    nc.vector.tensor_reduce(m.negmax[:, slot:slot + 1], m.max4[:, slot, :], AX.X, ALU.max,
                            negate=True).then_inc(a.max_done, 1)


def act_exp(nc, act, m, a, n, slot):
    act.wait_ge(a.max_done, n + 1)
    nc.scalar.activation(m.probs[:, slot, 0:S], m.probs[:, slot, 0:S], ACT.Exp, bias=m.negmax[:, slot:slot + 1],
                         accum_out=m.sums[:, slot:slot + 1]).then_inc(a.exp_done, 1)


def group_views(m, buf, g):
    chunks = GROUPS[g]
    r = rows(chunks[-1])
    src = m.psT[GROUP_BANK[g]][0:r, 0:len(chunks) * P].rearrange("p (c t) -> p c t", t=P)
    hi, lo = (v[0:r, buf, chunks[0]:chunks[-1] + 1, :] for v in (m.probsT_hi, m.probsT_lo))
    return src, hi, lo


def act_group_hi(nc, act, m, a, n, buf, g):
    src, hi, _ = group_views(m, buf, g)
    act.wait_ge(a.group_full, 4 * n + g + 1)
    nc.scalar.copy(hi, src).then_inc(a.copied_hi, 1)


def dve_group_lo(nc, dve, m, a, n, buf, g):
    src, hi, lo = group_views(m, buf, g)
    dve.wait_ge(a.copied_hi, 4 * n + g + 1)
    nc.vector.tensor_tensor(lo, src, hi, ALU.subtract).then_inc(a.copied_lo, 1)


def dve_take_out(nc, dve, m, a, n, slot, dst, bias, d):
    def over():
        dve.wait_ge(a.out_taken, 1 + n)
        dve.wait_ge(a.exp_done, n + 1)
        nc.vector.reciprocal(m.rsum[:, 0:1], m.sums[:, slot:slot + 1]).then_inc(a.recip_done, 1)

    def low():
        dve.wait_ge(a.recip_done, 2 * n + 1)
        dve.wait_ge(a.out_full, OUT_START + n + 1)
        nc.vector.scalar_tensor_tensor(m.part[:, 0:d], m.psO[:, d:2 * d], m.rsum[:, 0:1], bias,
                                       ALU.mult, ALU.add).then_inc(a.recip_done, 1)

    def high():
        dve.wait_ge(a.recip_done, 2 * n + 2)
        nc.vector.scalar_tensor_tensor(dst, m.psO[:, 0:d], m.rsum[:, 0:1], m.part[:, 0:d],
                                       ALU.mult, ALU.add).then_inc(a.out_taken, 1)

    return [over, low, high]


OUT_START = 8
LO_START = 4
GROUP_BANK = (0, 1, 2, 1)


def attention_sems(s, tag):
    a = Named()
    a.bank_full, a.exp_done, a.group_full = (s.sem(f"{tag}_{n}") for n in ("bank_full", "exp_done", "group_full"))
    a.max_done, a.recip_done, a.copied_hi = (s.sem(f"{tag}_{n}") for n in ("max_done", "recip_done", "copied_hi"))
    a.out_taken, a.copied_lo = s.from_one(f"{tag}_out_taken"), s.from_one(f"{tag}_copied_lo", LO_START)
    a.out_full = s.from_one(f"{tag}_out_full", OUT_START)
    a.bank_free = [s.from_one(f"{tag}_bank_free{q}") for q in range(4)]
    return a


def block_load(nc, m, s, dram):
    with nc.Block() as block:
        @block.sync
        def _(sp):
            sp.dma_start(m.x[:, :, :], dram["x"].rearrange("b (t p) d -> p (b t) d", p=P)).then_inc(s.load, 16)
            for name in LOADED:
                getdst = m.loaded[name]
                sp.dma_start(getdst, m.source[name]).then_inc(s.load, 16)
            sp.wait_ge(s.load, 16 * (1 + len(LOADED)))

        @block.scalar
        def _(act):
            ln_scalar(nc, act, m, s, 0)
            act.wait_ge(s.load, 16 * (1 + len(LOADED)))
            nc.scalar.activation(m.gates[:, :], m.gates[:, :], ACT.Tanh).then_inc(s.tanh, 1)
            act.wait_ge(s.tanh, 1)

        @block.vector
        def _(dve):
            dve.wait_ge(s.load, 16 * (1 + len(LOADED)))
            ln_vector(nc, dve, m, s, m.x, m.xn, 0)
            nc.vector.memset(m.xn[:, NT:NT + TT, :], 0.0)


LOADED = ["ident", "fold", "below", "cos_sin", "earlier", "weight8", "headmask", "scanreset", "ones",
          "gates", "wq0", "wk0", "wv0", "wo0", "bq0", "bk0", "bv0", "bo0"]


def block_attention0(nc, m, s, dram):
    with ExitStack() as stack:
        def sb(name, shape, dt=F32):
            return stack.enter_context(nc.sbuf_tensor(name, shape, dt))

        m.attn_mask, m.mask = sb("attn_mask", [P, TT, S]), sb("mask", [P, TT, S])
        m.pad8 = sb("pad8", [P, S], U8)
        m.o0 = sb("o0", [P, TT, E])
        m.k32, m.q32 = sb("k32", [P, S]), sb("q32", [P, T])
        m.khi, m.klo = sb("khi", [P, S], F16), sb("klo", [P, S], F16)
        m.qhi, m.qlo = sb("qhi", [P, T], F16), sb("qlo", [P, T], F16)
        m.kfan, m.qfan = sb("kfan", [P, 4, S], F16), sb("qfan", [P, 4, T], F16)
        m.qhead, m.vhead = sb("qhead", [P, 4, T], F16), sb("vhead", [P, 4, SC, 2, D0], F16)
        m.v0 = sb("v0", [P, SC, 2, E], F16)
        attention0(nc, m, s, dram)


def attention0(nc, m, s, dram):
    a = attention_sems(s, "a0")
    ctx_ready, x_fixed, x_turned = s.sem("a0_ctx_ready"), s.sem("a0_x_fixed"), s.sem("a0_x_turned")
    mask_loaded, mask_done, x_taken = s.sem("a0_mask_loaded"), s.sem("a0_mask_done"), s.sem("a0_x_taken")
    q_full, q_taken, k_hi, q_hi = (s.sem(f"a0_{n}") for n in ("q_full", "q_taken", "k_hi", "q_hi"))
    k_lo, q_lo, v_hi, head_ready = (s.sem(f"a0_{n}") for n in ("k_lo", "q_lo", "v_hi", "head_ready"))
    fanned, fanned_last, pe_out, dve_out = (s.sem(f"a0_{n}") for n in ("fanned", "fanned_last", "pe_out", "dve_out"))
    batch_done = s.from_one("a0_batch_done")
    GH = 4
    NG = H // GH
    GU = GH * TT
    LAST = (NG - 1) * GU
    USES = UB + 3
    prime(nc, s)

    def unit(b, g, u):
        return b * UB + g * GU + u

    def score_use(b, step):
        return b * USES + 5 + step + max(0, min(3, step - LAST))

    def group_use(b, g, u):
        return b * USES + g * GU + 5 + u if not isinstance(g, int) else score_use(b, g * GU + u)

    def prep_use(b, kind):
        return b * USES + 5 + LAST + 1 + 2 * kind

    def finishes(last, u):
        return u == GU - 1 or (last and u in (0, 1))

    with nc.Block() as block:
        @block.sync
        def _(sp):
            def load(nb, batch):
                sp.dma_start(m.ctx[:, 0:FULL, :], dram["ctx"][bass.ds(batch, 1), 0:FULL * P, :]
                             .rearrange("a (c p) d -> p (a c) d", p=P)).then_inc(ctx_ready, 16)
                sp.dma_start(m.ctx[0:REST, FULL, :], dram["ctx"][bass.ds(batch, 1), FULL * P:S, :]
                             .rearrange("a p d -> p (a d)")).then_inc(ctx_ready, 16)
                sp.dma_start(m.pad8[:, :], dram["pad"][bass.ds(batch, 1), :].to_broadcast([P, S])).then_inc(ctx_ready, 16)

            def fan(groups, done):
                n = len(groups)
                for r in range(4):
                    kpart = m.khi if r % 2 == 0 else m.klo
                    qpart = m.qhi if r < 2 else m.qlo
                    for g in groups:
                        sp.dma_start(m.kfan[32 * r:32 * r + 32, g, :], kpart[32 * g:32 * g + 32, :]).then_inc(done, 16)
                        sp.dma_start(m.qfan[32 * r:32 * r + 32, g, :], qpart[32 * g:32 * g + 32, :]).then_inc(done, 16)

            sp.dma_start(m.attn_mask[:, :, :], dram["attn_mask"].rearrange("(t p) s -> p t s", p=P)).then_inc(mask_loaded, 16)
            load(0, 0)
            sp.wait_ge(k_lo, 1)
            sp.wait_ge(q_lo, 1)
            fan(range(NG - 1), fanned)
            fan([NG - 1], fanned_last)

            def prefetch(b, batch):
                def after(semaphore, value):
                    sp.wait_ge(semaphore, value)
                    on_its_own(sp, s)

                after(x_turned, b + 1)
                after(mask_done, b + 1)
                load(b + 1, batch)
                after(k_lo, b + 2)
                after(q_lo, b + 2)
                after(head_ready, 2 * H * (b + 1))
                after(a.bank_full, 4 * score_use(b, LAST - AHEAD - 1) + 4)
                fan(range(NG - 1), fanned)
                after(a.bank_full, 4 * score_use(b, UB - AHEAD - 1) + 4)
                fan([NG - 1], fanned_last)

            with sp.Fori(0, B - 1) as b:
                prefetch(b, b + 1)
            prefetch(B - 1, 0)
            sp.wait_ge(fanned, 16 * 8 * (NG - 1) * (B + 1))
            sp.wait_ge(fanned_last, 16 * 8 * (B + 1))

        @block.gpsimd
        def _(pool):
            def split(nb):
                pool.wait_ge(k_hi, nb + 1)
                nc.gpsimd.tensor_tensor(m.klo[:, :], m.k32[:, :], m.khi[:, :], ALU.subtract).then_inc(k_lo, 1)
                pool.wait_ge(q_hi, nb + 1)
                nc.gpsimd.tensor_tensor(m.qlo[:, :], m.q32[:, :], m.qhi[:, :], ALU.subtract).then_inc(q_lo, 1)

            def heads(nb, g, first_unit):
                for j in range(GH):
                    if first_unit is not None:
                        pool.wait_ge(a.out_full, OUT_START + first_unit + 2 * j + 2 - GU)
                        on_its_own(pool, s)
                    nc.gpsimd.tensor_copy(m.vhead[:, j, :, :, :],
                                          m.v0[:, :, :, bass.ds(g * (GH * D0) + j * D0, D0)]).then_inc(head_ready, 1)
                    nc.gpsimd.tensor_tensor(m.qhead[:, j, :], m.qfan[:, bass.ds(g, 1), :].rearrange("p a t -> p (a t)"),
                                            m.headmask[:, j:j + 1].to_broadcast([P, T]), ALU.mult).then_inc(head_ready, 1)

            def values_ready(use):
                for q in range(4):
                    pool.wait_ge(a.bank_free[q], 1 + use + 1)
                on_its_own(pool, s)

            split(0)
            values_ready(2)
            pool.wait_ge(fanned, 16 * 8 * (NG - 1))
            heads(0, 0, None)
            with pool.Fori(0, B) as b:
                with pool.Fori(1, NG - 1) as g:
                    heads(b, g, unit(b, g, 0))
                pool.wait_ge(fanned_last, 16 * 8 * (b + 1))
                heads(b, NG - 1, unit(b, NG - 1, 0))
                split(b + 1)
                values_ready(prep_use(b, 2))
                pool.wait_ge(fanned, 16 * 8 * (NG - 1) * (b + 2))
                heads(b + 1, 0, unit(b + 1, 0, 0))

        @block.tensor
        def _(pe):
            def turn_context(nb, use):
                pe.wait_ge(ctx_ready, 48 * (nb + 1))
                for q, chunks in enumerate(GROUPS):
                    pe.wait_ge(a.bank_free[q], 1 + use)
                    for c in chunks:
                        r = rows(c)
                        ins = nc.tensor.transpose(m.psS[:, c * P:c * P + r], m.ctx[0:r, c, :], m.ident[0:r, 0:r])
                    ins.then_inc(a.bank_full, 1)
                pe.wait_ge(x_fixed, nb + 1)
                if not isinstance(nb, int):
                    pe.wait_ge(batch_done, nb)
                for t in range(TT):
                    ins = nc.tensor.transpose(m.psM[:, t * P:(t + 1) * P], m.xb[:, t, :], m.ident[:, :])
                ins.then_inc(x_turned, 1)

            def project_keys(nb, use, units=None):
                for q in (2, 3, 0, 1):
                    pe.wait_ge(a.bank_free[q], 1 + use)
                for o, w in SPANS:
                    nc.tensor.matmul(m.psS[:, o:o + w], m.wk0[:, :], m.ctxT[:, o:o + w],
                                     start=True, stop=True).then_inc(a.bank_full, 1)
                pe.wait_ge(x_taken, nb + 1)
                if units is not None:
                    pe.wait_ge(a.out_taken, 1 + units)
                nc.tensor.matmul(m.psM[:, 0:T], m.wq0[:, :], m.xT[:, 0:T], start=True, stop=True).then_inc(q_full, 1)

            def project_values(nb, use):
                for q, chunks in enumerate(GROUPS):
                    pe.wait_ge(a.bank_free[q], 1 + use)
                    for c in chunks:
                        r = rows(c)
                        ins = nc.tensor.matmul(m.psS[0:r, c * P:(c + 1) * P], m.ctxT[:, c * P:c * P + r], m.wv0[:, :],
                                               start=True, stop=True)
                    ins.then_inc(a.bank_full, 1)

            def scores(head, g, j, t, use, banks=range(4)):
                pe.wait_ge(head_ready, 2 * head + 2)
                pe_scores(nc, pe, m, a, use, lambda o, w: [
                    (m.qhead[:, j, t * P:(t + 1) * P],
                     m.kfan[:, bass.ds(g, 1), o:o + w].rearrange("p a s -> p (a s)"))], banks)

            def group(b, g, last):
                def values(u):
                    return lambda k: pe_values(
                        nc, pe, m, a, unit(b, g, u), u % 2,
                        lambda c, r, d: m.vhead[0:r, u // TT, c, :, :].rearrange("p a d -> p (a d)")[:, 0:d], D0, k)

                for u in range(GU):
                    n = unit(b, g, u)
                    v = (u + AHEAD) % GU
                    if u + AHEAD < GU:
                        to = (b * NG + g) * GH, g
                    elif not last:
                        to = (b * NG + g + 1) * GH, g + 1
                    else:
                        to = (b + 1) * H, 0

                    def ahead(banks):
                        scores(to[0] + v // TT, to[1], v // TT, v % TT, group_use(b, g, u), banks)

                    def turn(k):
                        pe_transpose(nc, pe, m, a, n, u % SLOTS, k)

                    before = nothing if u == 0 or finishes(last, u - 1) else values(u - 1)
                    turn(0)
                    ahead((0, 1))
                    before(0)
                    before(1)
                    turn(1)
                    ahead((2, 3))
                    before(2)
                    before(3)
                    turn(2)
                    turn(3)
                    if finishes(last, u):
                        for k in range(4):
                            values(u)(k)
                    if last and u == 0:
                        turn_context(b + 1, prep_use(b, 0))
                    if last and u == 1:
                        project_keys(b + 1, prep_use(b, 1), n + 1)
                    if last and u == 2:
                        project_values(b + 1, prep_use(b, 2))

            pe.wait_ge(mask_loaded, 16)
            turn_context(0, 0)
            project_keys(0, 1)
            project_values(0, 2)
            for u in range(AHEAD):
                scores(0, 0, 0, u, 3 + u)
            with pe.Fori(0, B) as b:
                with pe.Fori(0, NG - 1) as g:
                    group(b, g, False)
                group(b, NG - 1, True)
                pe.wait_ge(a.out_taken, 1 + UB * (b + 1))
                pe.wait_ge(q_taken, b + 2)
                for t in range(TT):
                    ins = nc.tensor.transpose(m.psM[:, t * P:(t + 1) * P], m.o0[:, t, :], m.ident[:, :])
                ins.then_inc(pe_out, 1)
                pe.wait_ge(dve_out, 2 * b + 1)
                for t in range(TT):
                    ins = nc.tensor.matmul(m.psM[:, t * P:(t + 1) * P], m.oT[:, t * P:(t + 1) * P], m.wo0[:, :],
                                           start=True, stop=True)
                ins.then_inc(pe_out, 1)

        @block.scalar
        def _(act):
            def take_context(nb, use):
                for q in range(2):
                    act.wait_ge(a.bank_full, 4 * use + q + 1)
                    o, w = SPANS[q]
                    nc.scalar.copy(m.ctxT[:, o:o + w], m.psS[:, o:o + w]).then_inc(a.bank_free[q], 1)

            def take_keys(nb, use):
                if not isinstance(nb, int):
                    act.wait_ge(k_lo, nb)
                for q in range(2):
                    act.wait_ge(a.bank_full, 4 * use + q + 1)
                    o, w = SPANS[q]
                    nc.scalar.activation(m.k32[:, o:o + w], m.psS[:, o:o + w], ACT.Identity,
                                         bias=m.bk0[:, 0:1]).then_inc(a.bank_free[q], 1)
                for q in range(4):
                    act.wait_ge(a.bank_free[q], 1 + use + 1)
                nc.scalar.copy(m.khi[:, :], m.k32[:, :]).then_inc(k_hi, 1)
                act.wait_ge(q_taken, nb + 1)
                nc.scalar.copy(m.qhi[:, :], m.q32[:, :]).then_inc(q_hi, 1)

            def take_values(nb, use):
                if not isinstance(nb, int):
                    act.wait_ge(head_ready, 2 * H * nb)
                for q, chunks in enumerate(GROUPS):
                    act.wait_ge(a.bank_full, 4 * use + q + 1)
                    c0, c1 = chunks[0], chunks[-1] + 1
                    r = rows(c1 - 1)
                    nc.scalar.copy(m.v0[0:r, c0:c1, 0, :],
                                   m.psS[0:r, c0 * P:c1 * P].rearrange("p (c d) -> p c d", d=E)).then_inc(v_hi, 1)

            def group(b, g, last):
                for u in range(GU):
                    n = unit(b, g, u)
                    for k in range(4):
                        act_group_hi(nc, act, m, a, n, u % 2, k)
                    act_exp(nc, act, m, a, n + AHEAD, (u + AHEAD) % SLOTS)
                    if last and u == 0:
                        take_context(b + 1, prep_use(b, 0))
                    if last and u == 1:
                        take_keys(b + 1, prep_use(b, 1))
                    if last and u == 2:
                        take_values(b + 1, prep_use(b, 2))

            take_context(0, 0)
            take_keys(0, 1)
            take_values(0, 2)
            for u in range(AHEAD):
                act_exp(nc, act, m, a, u, u)
            with act.Fori(0, B) as b:
                with act.Fori(0, NG - 1) as g:
                    group(b, g, False)
                group(b, NG - 1, True)

        @block.vector
        def _(dve):
            def next_mask(nb):
                dve.wait_ge(ctx_ready, 48 * (nb + 1))
                for t in range(TT):
                    ins = nc.vector.scalar_tensor_tensor(m.mask[:, t, :], m.pad8[:, :], NEG, m.attn_mask[:, t, :],
                                                         ALU.mult, ALU.add)
                ins.then_inc(mask_done, 1)
                dve.wait_ge(mask_done, nb + 1)

            def fix_x(nb):
                if not isinstance(nb, int):
                    dve.wait_ge(x_turned, nb)
                nc.vector.tensor_copy(m.xb[:, :, :], m.xn[:, bass.ds(nb * TT, TT), :]).then_inc(x_fixed, 1)

            def take_context(nb, use):
                for q in range(2, 4):
                    dve.wait_ge(a.bank_full, 4 * use + q + 1)
                    o, w = SPANS[q]
                    nc.vector.tensor_copy(m.ctxT[:, o:o + w], m.psS[:, o:o + w]).then_inc(a.bank_free[q], 1)
                dve.wait_ge(x_turned, nb + 1)
                nc.vector.tensor_copy(m.xT[:, 0:T], m.psM[:, 0:T]).then_inc(x_taken, 1)

            def take_keys(nb, use):
                if not isinstance(nb, int):
                    dve.wait_ge(k_lo, nb)
                for q in range(2, 4):
                    dve.wait_ge(a.bank_full, 4 * use + q + 1)
                    o, w = SPANS[q]
                    nc.vector.tensor_scalar(m.k32[:, o:o + w], m.psS[:, o:o + w], m.bk0[:, 0:1], None,
                                            ALU.add).then_inc(a.bank_free[q], 1)
                dve.wait_ge(q_full, nb + 1)
                if not isinstance(nb, int):
                    dve.wait_ge(q_lo, nb)
                nc.vector.tensor_scalar(m.q32[:, :], m.psM[:, 0:T], m.bq0[:, 0:1], float(D0) ** -0.5,
                                        ALU.add, ALU.mult).then_inc(q_taken, 1)

            def take_values(nb, use):
                for q, chunks in enumerate(GROUPS):
                    dve.wait_ge(v_hi, 4 * nb + q + 1)
                    c0, c1 = chunks[0], chunks[-1] + 1
                    r = rows(c1 - 1)
                    nc.vector.tensor_tensor(m.v0[0:r, c0:c1, 1, :],
                                            m.psS[0:r, c0 * P:c1 * P].rearrange("p (c d) -> p c d", d=E),
                                            m.v0[0:r, c0:c1, 0, :], ALU.subtract).then_inc(a.bank_free[q], 1)

            def mask_max(use, t, slot, q):
                dve_mask_max(nc, dve, m, a, use, slot, lambda o, w: m.mask[:, t, o:o + w], q)

            def group(b, g, last):
                def take_out(u):
                    o = g * (GH * D0) + (u // TT) * D0
                    return dve_take_out(nc, dve, m, a, unit(b, g, u), u % SLOTS,
                                        m.o0[:, u % TT, bass.ds(o, D0)], m.bv0[:, bass.ds(o, D0)], D0)

                for u in range(GU):
                    n = unit(b, g, u)
                    if last and u == GU - AHEAD:
                        next_mask(b + 1)

                    def ahead(q):
                        mask_max(group_use(b, g, u), u % TT, (u + AHEAD) % SLOTS, q)

                    def rest(k):
                        dve_group_lo(nc, dve, m, a, n, u % 2, k)

                    over, low, high = [done] * 3 if u == 0 or finishes(last, u - 1) else take_out(u - 1)
                    over()
                    ahead(0)
                    ahead(1)
                    rest(0)
                    ahead(2)
                    rest(1)
                    ahead(3)
                    low()
                    dve_negmax(nc, dve, m, a, group_use(b, g, u), (u + AHEAD) % SLOTS)
                    rest(2)
                    high()
                    rest(3)
                    if finishes(last, u):
                        for step in take_out(u):
                            step()
                    if last and u == 0:
                        fix_x(b + 1)
                        take_context(b + 1, prep_use(b, 0))
                    if last and u == 1:
                        take_keys(b + 1, prep_use(b, 1))
                    if last and u == 2:
                        take_values(b + 1, prep_use(b, 2))

            nc.vector.memset(m.v0[:, FULL, :, :], 0.0)
            dve.wait_ge(mask_loaded, 16)
            fix_x(0)
            next_mask(0)
            take_context(0, 0)
            take_keys(0, 1)
            take_values(0, 2)
            for u in range(AHEAD):
                for q in range(4):
                    mask_max(3 + u, u, u, q)
                dve_negmax(nc, dve, m, a, 3 + u, u)
            with dve.Fori(0, B) as b:
                with dve.Fori(0, NG - 1) as g:
                    group(b, g, False)
                group(b, NG - 1, True)
                dve.wait_ge(pe_out, 2 * b + 1)
                nc.vector.tensor_copy(m.oT[:, 0:T], m.psM[:, 0:T]).then_inc(dve_out, 1)
                dve.wait_ge(pe_out, 2 * b + 2)
                for t in range(TT):
                    ins = nc.vector.tensor_tensor(m.tmp[:, t, :], m.psM[:, t * P:(t + 1) * P], m.bo0[:, :], ALU.add)
                ins.then_inc(dve_out, 1)
                dve.wait_ge(dve_out, 2 * b + 2)
                xs = m.x[:, bass.ds(b * TT, TT), :]
                nc.vector.scalar_tensor_tensor(xs, m.tmp[:, :, :], m.gates[:, 0:1], xs,
                                               ALU.mult, ALU.add).then_inc(batch_done, 1)


def chain(eng, sem):
    count = [0]

    def step(ins):
        count[0] += 1
        ins.then_inc(sem, 1)
        eng.wait_ge(sem, count[0])
    return step, count


def to_tokens(t):
    return t.unsqueeze(2)


def pe_turn_x(nc, pe, m, normed, turned):
    pe.wait_ge(normed, 1)
    for k in range(NT):
        ins = nc.tensor.transpose(m.psS[:, k * P:(k + 1) * P], m.xn[:, k, :], m.ident[:, :])
        if k in (NT // 2 - 1, NT - 1):
            ins.then_inc(turned, 1)


def block_route0(nc, m, s, dram):
    normed, turned, xt_act, xt_dve = (s.sem(f"r0_{n}") for n in ("normed", "turned", "xt_act", "xt_dve"))
    logits_done, exp_done, counts, counted, steps = (s.sem(f"r0_{n}") for n in ("logits", "exp", "counts", "counted", "steps"))
    BITS, STEPS = 30, 6
    with ExitStack() as stack:
        def sb(name, shape, dt=F32):
            return stack.enter_context(nc.sbuf_tensor(name, shape, dt))

        wg = sb("wg", [P, X0])
        probs, ge, flag, val = (sb(n, [P, NT, X0]) for n in ("r0_probs", "r0_ge", "r0_flag", "r0_val"))
        gt, eq, before = (sb(n, [P, NT, X0]) for n in ("r0_gt", "r0_eq", "r0_before"))
        geT = sb("r0_geT", [P, X0, NT])
        top, total = sb("r0_top", [P, NT]), sb("r0_total", [P, NT])
        count, need = sb("r0_count", [P, X0]), sb("r0_need", [P, X0])
        bit, cur, cand, take = (sb(n, [P, X0], I32) for n in ("r0_bit", "r0_cur", "r0_cand", "r0_take"))
        lg = m.psT[2][:, 0:NT * X0].rearrange("p (k e) -> p k e", e=X0)
        rank = lg
        sums = m.psO[:, 0:X0]
        curf, candf = cur[:, :].bitcast(F32), cand[:, :].bitcast(F32)

        def over_k(ap):
            return ap.unsqueeze(1).to_broadcast([P, NT, X0])

        def over_e(ap):
            return ap.unsqueeze(2).to_broadcast([P, NT, X0])

        with nc.Block() as block:
            @block.sync
            def _(sp):
                sp.dma_start(wg[:, :], dram["wg"]).then_inc(s.weights, 16)

            @block.tensor
            def _(pe):
                pe_turn_x(nc, pe, m, normed, turned)
                pe.wait_ge(xt_act, 1)
                pe.wait_ge(xt_dve, 1)
                pe.wait_ge(s.weights, 16)
                for k in range(NT):
                    ins = nc.tensor.matmul(lg[:, k, :], m.xT[:, k * P:(k + 1) * P], wg[:, :], start=True, stop=True)
                ins.then_inc(logits_done, 1)
                with pe.Fori(0, BITS) as i:
                    pe.wait_ge(counts, i + 1)
                    nc.tensor.matmul(sums, m.ones[:, :], count[:, :], start=True, stop=True).then_inc(counted, 1)
                pe.wait_ge(counts, BITS + 1)
                nc.tensor.matmul(sums, m.ones[:, :], count[:, :], start=True, stop=True).then_inc(counted, 1)
                pe.wait_ge(counts, BITS + 2)
                eq2, before2 = (v[:, :, :].rearrange("p k e -> p (k e)") for v in (eq, before))
                nc.tensor.matmul(m.psT[2][:, 0:NT * X0], m.below[:, :], eq2, start=True, stop=False)
                nc.tensor.matmul(m.psT[2][:, 0:NT * X0], m.ones[:, :], before2, start=False, stop=True).then_inc(counted, 1)

            @block.scalar
            def _(act):
                ln_scalar(nc, act, m, s, 1)
                act.wait_ge(turned, 1)
                nc.scalar.copy(m.xT[:, 0:TOK // 2], m.psS[:, 0:TOK // 2]).then_inc(xt_act, 1)
                act.wait_ge(steps, 2)
                nc.scalar.activation(probs[:, :, :], probs[:, :, :], ACT.Exp).then_inc(exp_done, 1)

            @block.vector
            def _(dve):
                ln_vector(nc, dve, m, s, m.x, m.xn, 1)
                nc.vector.memset(cur[:, :], 0).then_inc(normed, 1)
                nc.vector.memset(bit[:, :], 1 << (BITS - 1))
                dve.wait_ge(turned, 2)
                nc.vector.tensor_copy(m.xT[:, TOK // 2:TOK], m.psS[:, TOK // 2:TOK]).then_inc(xt_dve, 1)
                step, done = chain(dve, steps)
                dve.wait_ge(logits_done, 1)
                step(nc.vector.tensor_reduce(top[:, :], lg, AX.X, ALU.max))
                step(nc.vector.tensor_tensor(probs[:, :, :], lg, over_e(top[:, :]), ALU.subtract))
                dve.wait_ge(exp_done, 1)
                step(nc.vector.tensor_reduce(total[:, :], probs[:, :, :], AX.X, ALU.add))
                step(nc.vector.reciprocal(top[:, :], total[:, :]))
                step(nc.vector.tensor_tensor(probs[:, :, :], probs[:, :, :], over_e(top[:, :]), ALU.mult))
                first = done[0]
                with dve.Fori(0, BITS) as i:
                    now = i * STEPS + first
                    nc.vector.tensor_tensor(cand[:, :], cur[:, :], bit[:, :], ALU.bitwise_or).then_inc(steps, 1)
                    dve.wait_ge(steps, now + 1)
                    nc.vector.tensor_tensor(ge[:, :, :], probs[:, :, :], over_k(candf), ALU.is_ge).then_inc(steps, 1)
                    dve.wait_ge(steps, now + 2)
                    nc.vector.tensor_reduce(count[:, :], ge[:, :, :].rearrange("p k e -> p e k"), AX.X,
                                            ALU.add).then_inc(counts, 1)
                    nc.vector.tensor_scalar(bit[:, :], bit[:, :], 1, None, ALU.logical_shift_right).then_inc(steps, 1)
                    dve.wait_ge(counted, i + 1)
                    nc.vector.tensor_scalar(take[:, :], sums, float(CAP), None, ALU.is_ge).then_inc(steps, 1)
                    dve.wait_ge(steps, now + 4)
                    on_its_own(dve, s)
                    nc.vector.copy_predicated(cur[:, :], take[:, :], cand[:, :]).then_inc(steps, 2)
                    dve.wait_ge(steps, now + STEPS)
                    on_its_own(dve, s)
                done[0] = first + BITS * STEPS
                step(nc.vector.tensor_tensor(gt[:, :, :], probs[:, :, :], over_k(curf), ALU.is_gt))
                step(nc.vector.tensor_tensor(eq[:, :, :], probs[:, :, :], over_k(curf), ALU.is_equal))
                nc.vector.tensor_reduce(count[:, :], gt[:, :, :].rearrange("p k e -> p e k"), AX.X,
                                        ALU.add).then_inc(counts, 1)
                step(nc.vector.memset(before[:, 0, :], 0.0))
                for k in range(NT - 1):
                    step(nc.vector.tensor_tensor(before[:, k + 1, :], before[:, k, :], eq[:, k, :], ALU.add))
                nc.vector.memset(flag[:, :, :], 0.0).then_inc(counts, 1)
                dve.wait_ge(counted, BITS + 1)
                step(nc.vector.tensor_scalar(need[:, :], sums, -1.0, float(CAP), ALU.mult, ALU.add))
                dve.wait_ge(counted, BITS + 2)
                dve.wait_ge(counts, BITS + 2)
                step(nc.vector.tensor_tensor(flag[:, :, :], rank, over_k(need[:, :]), ALU.is_lt))
                step(nc.vector.tensor_tensor(flag[:, :, :], flag[:, :, :], eq[:, :, :], ALU.mult))
                step(nc.vector.tensor_tensor(flag[:, :, :], flag[:, :, :], gt[:, :, :], ALU.add))
                step(nc.vector.tensor_reduce(top[:, :], flag[:, :, :], AX.X, ALU.max))
                step(nc.vector.tensor_scalar(top[:, :], top[:, :], -1.0, 1.0, ALU.mult, ALU.add))
                step(nc.vector.tensor_tensor(flag[:, :, :], flag[:, :, :], over_e(top[:, :]), ALU.add))
                step(nc.vector.tensor_tensor(val[:, :, :], probs[:, :, :], flag[:, :, :], ALU.mult))
                step(nc.vector.scalar_tensor_tensor(val[:, :, :], flag[:, :, :], -1.0, val[:, :, :], ALU.add, ALU.add))
                step(nc.vector.tensor_reduce(top[:, :], val[:, :, :], AX.X, ALU.max))
                step(nc.vector.tensor_tensor(flag[:, :, :], val[:, :, :], over_e(top[:, :]), ALU.is_equal))
                step(nc.vector.tensor_tensor(flag[:, :, :], flag[:, :, :], over_k(m.weight8[:, :]), ALU.mult))
                step(nc.vector.tensor_reduce(top[:, :], flag[:, :, :], AX.X, ALU.max))
                step(nc.vector.tensor_tensor(flag[:, :, :], flag[:, :, :], over_e(top[:, :]), ALU.is_equal))
                nc.vector.tensor_tensor(m.gate[:, :, :], flag[:, :, :], probs[:, :, :], ALU.mult)


def block_experts0(nc, m, s, dram):
    hidden = s.sem("e0_hidden")
    gelu_done, out_full, added = (s.from_one(f"e0_{n}") for n in ("gelu_done", "out_full", "added"))
    KB = BANK // P
    with ExitStack() as stack:
        def sb(name, shape, dt=F32):
            return stack.enter_context(nc.sbuf_tensor(name, shape, dt))

        w1, w2 = sb("w1", [P, X0, F0]), sb("w2", [P, X0, F0 // P, E])
        act_out = sb("e0_gelu", [P, 2, 2 * BANK])
        acc = sb("e0_acc", [P, NT, E])
        loaded, zeroed = s.sem("e0_loaded"), s.sem("e0_zeroed")
        prime(nc, s)

        def turn(blk, e):
            return blk * X0 + e

        with nc.Block() as block:
            @block.sync
            def _(sp):
                sp.dma_start(w1[:, :, :], dram["w1"].rearrange("e d f -> d e f")).then_inc(loaded, 16)
                sp.dma_start(w2[:, :, :, :], dram["w2"].rearrange("e (h f) d -> f e h d", f=P)).then_inc(loaded, 16)

            @block.tensor
            def _(pe):
                pe.wait_ge(loaded, 32)

                def up(blk, e):
                    n = turn(blk, e)
                    if e >= 2:
                        pe.wait_ge(gelu_done, 1 + n - 1)
                    else:
                        pe.wait_ge(gelu_done, 1 + blk * X0)
                    for h in range(2):
                        o = (2 * (e % 2) + h) * BANK
                        ins = nc.tensor.matmul(m.psS[:, o:o + BANK], w1[:, e, h * P:(h + 1) * P],
                                               m.xT[:, bass.ds(blk * BANK, BANK)], start=True, stop=True)
                    ins.then_inc(hidden, 1)

                def down(blk, e):
                    n = turn(blk, e)
                    pe.wait_ge(gelu_done, 1 + n + 1)
                    if e >= 2:
                        pe.wait_ge(added, 1 + n - 1)
                    else:
                        pe.wait_ge(added, 1 + blk * X0)
                    for k in range(KB):
                        for h in range(2):
                            o = h * BANK + k * P
                            ins = nc.tensor.matmul(m.psT[e % 2][:, k * P:(k + 1) * P], act_out[:, e % 2, o:o + P],
                                                   w2[:, e, h, :], start=(h == 0), stop=(h == 1))
                    ins.then_inc(out_full, 1)

                with pe.Fori(0, TOK // BANK) as blk:
                    up(blk, 0)
                    for e in range(X0):
                        if e + 1 < X0:
                            up(blk, e + 1)
                        down(blk, e)

            @block.scalar
            def _(act):
                with act.Fori(0, TOK // BANK) as blk:
                    for e in range(X0):
                        n = turn(blk, e)
                        act.wait_ge(hidden, n + 1)
                        if e >= 2:
                            act.wait_ge(out_full, 1 + n - 1)
                        else:
                            act.wait_ge(out_full, 1 + blk * X0)
                        o = 2 * (e % 2) * BANK
                        nc.scalar.activation(act_out[:, e % 2, :], m.psS[:, o:o + 2 * BANK], ACT.Gelu).then_inc(gelu_done, 1)

            @block.vector
            def _(dve):
                nc.vector.memset(acc[:, :, :], 0.0).then_inc(zeroed, 1)
                dve.wait_ge(zeroed, 1)
                with dve.Fori(0, TOK // BANK) as blk:
                    for e in range(X0):
                        n = turn(blk, e)
                        dve.wait_ge(out_full, 1 + n + 1)
                        dve.wait_ge(added, 1 + n)
                        for k in range(KB):
                            tile = acc[:, bass.ds(blk * KB + k, 1), :].rearrange("p a d -> p (a d)")
                            ins = nc.vector.scalar_tensor_tensor(
                                tile, m.psT[e % 2][:, k * P:(k + 1) * P],
                                m.gate[:, bass.ds(blk * KB + k, 1), e:e + 1].rearrange("p a e -> p (a e)"), tile,
                                ALU.mult, ALU.add)
                        ins.then_inc(added, 1)
                dve.wait_ge(added, 1 + X0 * TOK // BANK)
                nc.vector.scalar_tensor_tensor(m.x[:, :, :], acc[:, :, :], m.gates[:, 1:2], m.x[:, :, :],
                                               ALU.mult, ALU.add).then_inc(zeroed, 1)
                dve.wait_ge(zeroed, 2)


def block_norm1(nc, m, s, dram):
    with nc.Block() as block:
        @block.scalar
        def _(act):
            ln_scalar(nc, act, m, s, 2)
            ln_scalar(nc, act, m, s, 3)

        @block.vector
        def _(dve):
            ln_vector(nc, dve, m, s, m.x, m.xn, 2)
            ln_vector(nc, dve, m, s, m.xn, m.xn, 3)


def block_attention1(nc, m, s, dram):
    with ExitStack() as stack:
        def sb(name, shape, dt=F32):
            return stack.enter_context(nc.sbuf_tensor(name, shape, dt))

        w = Named()
        w.mask, w.position = sb("a1_mask", [P, S]), sb("position", [P, S])
        w.lens, w.lensf = sb("lens", [P, B], I32), sb("lensf", [P, B + 1])
        w.gain, w.shift = sb("ln_g", [P, 1]), sb("ln_b", [P, 1])
        w.wo, w.bv, w.bo = sb("wo1", [P, 8, E]), sb("bv1", [P, H * D1]), sb("bo1", [P, E])
        w.head_w = sb("head_w", [P, 2, HEAD_WIDTH])
        w.w_hi, w.w_lo = sb("w_hi", [P, 2, BK], F16), sb("w_lo", [P, 2, BK], F16)
        w.c_hi, w.c_lo = sb("c_hi", [P, S], F16), sb("c_lo", [P, S], F16)
        w.y32 = sb("y32", [P, S])
        w.y_hi, w.y_lo = sb("y_hi", [P, 2, S], F16), sb("y_lo", [P, 2, S], F16)
        w.q_rot = sb("q_rot", [P, T])
        w.q_hi, w.q_lo = sb("q_hi", [P, 2, T], F16), sb("q_lo", [P, 2, T], F16)
        w.values = sb("values1", [P, 4, SC, 2, D1], F16)
        w.out = sb("out1", [P, TT, H * D1])
        w.stats, w.mv = sb("a1_stats", [P, SC, 6]), sb("a1_mv", [P, SC, 2])
        w.var, w.rstd = sb("a1_var", [P, SC]), sb("a1_rstd", [P, SC])
        w.normed = sb("a1_normed", [P, SC, E])
        attention1(nc, m, s, dram, w)


WV, BK, BQ, HEAD_WIDTH = 2 * P, 2 * P + D1, 2 * P + D1 + 1, 2 * P + D1 + 2


def attention1(nc, m, s, dram, w):
    a = attention_sems(s, "a1")
    ctx_ready, loaded, stat, root = (s.sem(f"a1_{n}") for n in ("ctx_ready", "loaded", "stat", "root"))
    normed_ready, x_fixed, turned, x_taken = (s.sem(f"a1_{n}") for n in ("normed_ready", "x_fixed", "turned", "x_taken"))
    k_hi, keys_ready, lens_ready = (s.sem(f"a1_{n}") for n in ("k_hi", "keys_ready", "lens_ready"))
    q_hi, v_hi, fin_full = (s.sem(f"a1_{n}") for n in ("q_hi", "v_hi", "fin_full"))
    biased, batch_done, mask_done = s.sem("a1_biased"), s.sem("a1_batch_done"), s.sem("a1_mask_done")
    weight_ready, weight_split = ([s.sem(f"a1_weight_{n}{j}") for j in range(2)] for n in ("ready", "split"))
    ctx_hi, ctx_split = s.sem("a1_ctx_hi"), s.sem("a1_ctx_split")
    LOADS = 7
    GH = 4
    NG = H // GH
    GU = GH * TT
    START, USES, PREP_HEAD = 7, 4 * H + 2, H - 2
    prime(nc, s)

    def unit(b, g, u):
        return b * UB + g * GU + u

    def use(b, g, v, last):
        return b * USES + g * (4 * GH) + START + 4 * v + (1 if last and v >= 2 else 0)

    def prep_use(b):
        return b * USES + START + 4 * PREP_HEAD

    def fin_use(b):
        return b * USES + START + 4 * H + 1

    def head(b, g, v):
        return b * H + g * GH + v

    def finishes(last, u):
        return u == GU - 1 or (last and u == TT * (GH - 2) - 1)

    with nc.Block() as block:
        @block.sync
        def _(sp):
            def after(semaphore, value):
                sp.wait_ge(semaphore, value)
                on_its_own(sp, s)

            def load_context(batch):
                sp.dma_start(m.ctx[:, 0:FULL, :], dram["ctx"][bass.ds(batch, 1), 0:FULL * P, :]
                             .rearrange("a (c p) d -> p (a c) d", p=P)).then_inc(ctx_ready, 16)
                sp.dma_start(m.ctx[0:REST, FULL, :], dram["ctx"][bass.ds(batch, 1), FULL * P:S, :]
                             .rearrange("a p d -> p (a d)")).then_inc(ctx_ready, 16)

            def load_weights(j, h):
                sp.dma_start(w.head_w[:, j, :], dram["head_w"][bass.ds(h, 1), :, :]
                             .rearrange("a p w -> p (a w)")).then_inc(weight_ready[j], 16)

            load_context(0)
            for dst, src in ((w.position[:, :], dram["position"].to_broadcast([P, S])),
                             (w.lens[:, :], dram["lens"].to_broadcast([P, B])), (w.gain[:, :], dram["ln_g"]),
                             (w.shift[:, :], dram["ln_b"]), (w.wo[:, :, :], dram["wo1"]),
                             (w.bv[:, :], dram["bv1"].to_broadcast([P, H * D1])),
                             (w.bo[:, :], dram["bo1"].to_broadcast([P, E]))):
                sp.dma_start(dst, src).then_inc(loaded, 16)
            for h in range(2):
                load_weights(h, h)
            for h in range(2):
                sp.wait_ge(a.bank_full, 4 + 8 * (h + 1))
                load_weights(h, h + 2)

            def turn(b, g, last):
                for v in range(GH):
                    after(a.bank_full, 4 * use(b, g, v, last) + 12)
                    load_weights(v % 2, v if last else g * GH + v + GH)

            def batch(b, following):
                after(normed_ready, SC * (b + 1))
                load_context(following)
                with sp.Fori(0, NG - 1) as g:
                    turn(b, g, False)
                turn(b, NG - 1, True)

            with sp.Fori(0, B - 1) as b:
                batch(b, b + 1)
            batch(B - 1, 0)
            for j in range(2):
                sp.wait_ge(weight_ready[j], 16 * (2 + B * H // 2))

        @block.gpsimd
        def _(pool):
            def norm_wait(nb):
                pool.wait_ge(stat, 4 * nb + 4)
                on_its_own(pool, s)
                if not isinstance(nb, int):
                    pool.wait_ge(turned, nb)
                    on_its_own(pool, s)

            def norm_chunks(chunks):
                for c in chunks:
                    r = rows(c)
                    nc.gpsimd.tensor_scalar(w.normed[0:r, c, :], m.ctx[0:r, c, :], w.mv[0:r, c, 0:1],
                                            w.rstd[0:r, c:c + 1], ALU.subtract, ALU.mult).then_inc(normed_ready, 1)

            def context_rest(nb):
                for q, (o, width) in enumerate(SPANS):
                    pool.wait_ge(ctx_hi, 4 * nb + q + 1)
                    nc.gpsimd.tensor_tensor(w.c_lo[:, o:o + width], m.ctxT[:, o:o + width],
                                            w.c_hi[:, o:o + width], ALU.subtract).then_inc(ctx_split, 1)

            def split_weights(j, full, count):
                pool.wait_ge(weight_ready[j], 16 * count)
                on_its_own(pool, s)
                if full is not None:
                    pool.wait_ge(a.bank_full, full)
                    on_its_own(pool, s)
                nc.gpsimd.tensor_copy(w.w_hi[:, j, :], w.head_w[:, j, 0:BK]).then_inc(weight_split[j], 1)
                pool.wait_ge(weight_split[j], 2 * count - 1)
                nc.gpsimd.tensor_tensor(w.w_lo[:, j, :], w.head_w[:, j, 0:BK], w.w_hi[:, j, :],
                                        ALU.subtract).then_inc(weight_split[j], 1)

            def key_rest(k, j):
                for q, (o, width) in enumerate(SPANS):
                    pool.wait_ge(k_hi, 4 * k + q + 1)
                    nc.gpsimd.tensor_tensor(w.y_lo[:, j, o:o + width], w.y32[:, o:o + width],
                                            w.y_hi[:, j, o:o + width], ALU.subtract).then_inc(keys_ready, 1)

            def turn(b, g, last):
                for v in range(GH):
                    if last and v == 2:
                        context_rest(b + 1)
                    if last and v == 0:
                        norm_wait(b + 1)
                        norm_chunks(range(0, 8))
                    if last and v == 1:
                        norm_chunks(range(8, SC))
                    key_rest(head(b, g, v) + 2, v % 2)
                    split_weights(v % 2, 4 * use(b, g, v, last) + 12, b * (H // 2) + g * (GH // 2) + v // 2 + 3)

            for j in range(2):
                split_weights(j, None, 1)
            norm_wait(0)
            norm_chunks(range(SC))
            context_rest(0)
            for j in range(2):
                key_rest(j, j)
                split_weights(j, 4 + 8 * (j + 1), 2)
            with pool.Fori(0, B) as b:
                with pool.Fori(0, NG - 1) as g:
                    turn(b, g, False)
                turn(b, NG - 1, True)

        @block.tensor
        def _(pe):
            def turn_context(nb, before):
                pe.wait_ge(normed_ready, SC * (nb + 1))
                for q, chunks in enumerate(GROUPS):
                    pe.wait_ge(a.bank_free[q], 1 + before)
                    for c in chunks:
                        r = rows(c)
                        ins = nc.tensor.transpose(m.psS[:, c * P:c * P + r], w.normed[0:r, c, :], m.ident[0:r, 0:r])
                    ins.then_inc(a.bank_full, 1)
                pe.wait_ge(x_fixed, nb + 1)
                for t in range(TT):
                    ins = nc.tensor.transpose(m.psM[:, t * P:(t + 1) * P], m.xb[:, t, :], m.ident[:, :])
                ins.then_inc(turned, 1)

            def project_keys(nb, j, before, banks=range(4)):
                for q in banks:
                    o, width = SPANS[q]
                    pe.wait_ge(ctx_split, 4 * nb + q + 1)
                    pe.wait_ge(a.bank_free[q], 1 + before)
                    hi, lo = w.c_hi[:, o:o + width], w.c_lo[:, o:o + width]
                    nc.tensor.matmul(m.psS[:, o:o + width], w.w_hi[:, j, 0:P], hi, start=True, stop=False)
                    nc.tensor.matmul(m.psS[:, o:o + width], w.w_lo[:, j, 0:P], hi, start=False, stop=False)
                    nc.tensor.matmul(m.psS[:, o:o + width], w.w_hi[:, j, 0:P], lo,
                                     start=False, stop=True).then_inc(a.bank_full, 1)

            def project_queries(nb, j, before):
                pe.wait_ge(x_taken, nb + 1)
                pe.wait_ge(a.bank_free[0], 1 + before)
                nc.tensor.matmul(m.psS[:, 0:T], w.head_w[:, j, P:2 * P], m.xT[:, 0:T],
                                 start=True, stop=True).then_inc(a.bank_full, 1)

            def double_query(before):
                pe.wait_ge(a.bank_free[0], 1 + before + 1)
                pe.wait_ge(a.bank_free[3], 1 + before)
                nc.tensor.matmul(m.psS[:, 3 * BANK:3 * BANK + T], m.fold[:, :], w.q_rot[:, :],
                                 start=True, stop=True).then_inc(a.bank_full, 1)

            def project_values(j, before, banks=(1, 2)):
                for q in banks:
                    pe.wait_ge(a.bank_free[q], 1 + before)
                    for c in VALUE_CHUNKS[q]:
                        r = rows(c)
                        o = q * BANK + (c - VALUE_CHUNKS[q][0]) * D1
                        hi, lo = w.c_hi[:, c * P:c * P + r], w.c_lo[:, c * P:c * P + r]
                        wv_hi, wv_lo = w.w_hi[:, j, WV:WV + D1], w.w_lo[:, j, WV:WV + D1]
                        nc.tensor.matmul(m.psS[0:r, o:o + D1], hi, wv_hi, start=True, stop=False)
                        nc.tensor.matmul(m.psS[0:r, o:o + D1], hi, wv_lo, start=False, stop=False)
                        ins = nc.tensor.matmul(m.psS[0:r, o:o + D1], lo, wv_hi, start=False, stop=True)
                    ins.then_inc(a.bank_full, 1)

            def scores(k, j, t, use, banks=range(4)):
                if t == 0 and banks[0] == 0:
                    pe.wait_ge(keys_ready, 4 * k + 4)
                    pe.wait_ge(a.bank_free[3], use)
                qh, ql = (v[:, j, t * P:(t + 1) * P] for v in (w.q_hi, w.q_lo))
                pe_scores(nc, pe, m, a, use, lambda o, n: [
                    (qh, w.y_hi[:, j, o:o + n]), (ql, w.y_hi[:, j, o:o + n]), (qh, w.y_lo[:, j, o:o + n])], banks)

            def turn(b, g, last):
                def values(u):
                    return lambda k: pe_values(
                        nc, pe, m, a, unit(b, g, u), u % 2,
                        lambda c, r, n: w.values[0:r, u // TT, c, :, :].rearrange("p a d -> p (a d)")[:, 0:n], D1, k)

                for u in range(GU):
                    n, v, t = unit(b, g, u), u // TT, u % TT
                    before = use(b, g, v, last)
                    nb = b + 1 if last and v >= 2 else b
                    k = head(b, g, v) + 1

                    def turn(group):
                        pe_transpose(nc, pe, m, a, n, u % SLOTS, group)

                    out = nothing if u == 0 or finishes(last, u - 1) else values(u - 1)
                    turn(0)
                    if t == 0:
                        scores(k, (v + 1) % 2, t, before, (0, 1))
                        out(0)
                        out(1)
                        turn(1)
                        scores(k, (v + 1) % 2, t, before, (2, 3))
                        out(2)
                        out(3)
                        pe.wait_ge(weight_split[v % 2], 2 * (b * (H // 2) + g * (GH // 2) + v // 2 + 2))
                        project_keys(nb, v % 2, before + 1, (0,))
                        turn(2)
                        project_keys(nb, v % 2, before + 1, (1, 2))
                        turn(3)
                        project_keys(nb, v % 2, before + 1, (3,))
                    else:
                        project_queries(nb, v % 2, before + 2)
                        project_values(v % 2, before + 2, (1,))
                        out(0)
                        out(1)
                        turn(1)
                        project_values(v % 2, before + 2, (2,))
                        out(2)
                        out(3)
                        double_query(before + 2)
                        scores(k, (v + 1) % 2, t, before + 3, (0,))
                        turn(2)
                        scores(k, (v + 1) % 2, t, before + 3, (1,))
                        turn(3)
                        scores(k, (v + 1) % 2, t, before + 3, (2, 3))
                    if finishes(last, u):
                        for group in range(4):
                            values(u)(group)
                    if last and u == TT * (GH - 2) - 1:
                        turn_context(b + 1, prep_use(b))

            pe.wait_ge(loaded, 16 * LOADS)
            turn_context(0, 0)
            for h in range(2):
                pe.wait_ge(weight_split[h], 2)
                project_keys(0, h, 1 + 2 * h)
                project_queries(0, h, 2 + 2 * h)
                project_values(h, 2 + 2 * h)
                double_query(2 + 2 * h)
            for t in range(AHEAD):
                scores(0, 0, t, 5 + t)
            with pe.Fori(0, B) as b:
                with pe.Fori(0, NG - 1) as g:
                    turn(b, g, False)
                turn(b, NG - 1, True)
                pe.wait_ge(a.out_taken, 1 + UB * (b + 1))
                for q in range(4):
                    pe.wait_ge(a.bank_free[q], 1 + fin_use(b))
                    for c in range(4 * q, 4 * q + 4):
                        ins = nc.tensor.transpose(m.psS[:, c * P:(c + 1) * P],
                                                  w.out[:, c // 8, (c % 8) * P:(c % 8 + 1) * P], m.ident[:, :])
                    ins.then_inc(a.bank_full, 1)
                for q in range(4):
                    pe.wait_ge(a.bank_free[q], 1 + fin_use(b) + 1)
                for t in range(TT):
                    for c in range(8):
                        o = (t * 8 + c) * P
                        ins = nc.tensor.matmul(m.psM[:, t * P:(t + 1) * P], m.oT[:, o:o + P], w.wo[:, c, :],
                                               start=(c == 0), stop=(c == 7))
                ins.then_inc(fin_full, 1)

        @block.scalar
        def _(act):
            def deviation(nb):
                act.wait_ge(stat, 4 * nb + 3)
                nc.scalar.activation(w.var[:, :], w.var[:, :], ACT.Sqrt).then_inc(root, 1)

            def take_context(before):
                for q in range(2):
                    o, width = SPANS[q]
                    act.wait_ge(a.bank_full, 4 * before + q + 1)
                    nc.scalar.activation(m.ctxT[:, o:o + width], m.psS[:, o:o + width], ACT.Identity,
                                         bias=w.shift[:, :], scale=w.gain[:, :]).then_inc(a.bank_free[q], 1)

            def context_hi(before):
                for q, (o, width) in enumerate(SPANS):
                    act.wait_ge(a.bank_free[q], 1 + before + 1)
                    nc.scalar.copy(w.c_hi[:, o:o + width], m.ctxT[:, o:o + width]).then_inc(ctx_hi, 1)

            def key_hi(j, before, banks=range(4)):
                for q in banks:
                    o, width = SPANS[q]
                    act.wait_ge(a.bank_free[q], 1 + before + 1)
                    nc.scalar.copy(w.y_hi[:, j, o:o + width], w.y32[:, o:o + width]).then_inc(k_hi, 1)

            def query_hi(j, before):
                act.wait_ge(a.bank_full, 4 * before + 4)
                nc.scalar.activation(w.q_hi[:, j, :], m.psS[:, 3 * BANK:3 * BANK + T], ACT.Copy,
                                     scale=float(D1) ** -0.5).then_inc(q_hi, 1)

            def value_hi(slot, before, banks=(1, 2)):
                for q in banks:
                    act.wait_ge(a.bank_full, 4 * before + q + 1)
                    for src, dst, _ in value_views(m, w, slot, 0)[q]:
                        ins = nc.scalar.copy(dst, src)
                    ins.then_inc(v_hi, 1)

            def turn(b, g, last):
                for u in range(GU):
                    n, v, t = unit(b, g, u), u // TT, u % TT
                    before = use(b, g, v, last)

                    def high(*groups):
                        for k in groups:
                            act_group_hi(nc, act, m, a, n, u % 2, k)

                    if t == 0:
                        high(0, 1)
                        act_exp(nc, act, m, a, n + 1, (u + 1) % SLOTS)
                        high(2, 3)
                        act_exp(nc, act, m, a, n + 2, (u + 2) % SLOTS)
                    else:
                        high(0)
                        value_hi((v + 2) % 4, before + 2, (1,))
                        key_hi(v % 2, before + 1, (0, 1))
                        high(1)
                        value_hi((v + 2) % 4, before + 2, (2,))
                        key_hi(v % 2, before + 1, (2, 3))
                        query_hi(v % 2, before + 2)
                        high(2, 3)
                    if last and u == TT * (GH - 2) - 1:
                        take_context(prep_use(b))
                        context_hi(prep_use(b))

            act.wait_ge(loaded, 16 * LOADS)
            deviation(0)
            take_context(0)
            context_hi(0)
            for h in range(2):
                key_hi(h, 1 + 2 * h)
                value_hi(h, 2 + 2 * h)
                query_hi(h, 2 + 2 * h)
            act_exp(nc, act, m, a, 0, 0)
            with act.Fori(0, B) as b:
                with act.Fori(0, NG - 1) as g:
                    turn(b, g, False)
                deviation(b + 1)
                turn(b, NG - 1, True)
                for q in range(2):
                    act.wait_ge(a.bank_full, 4 * fin_use(b) + q + 1)
                    nc.scalar.copy(m.oT[:, q * BANK:(q + 1) * BANK],
                                   m.psS[:, q * BANK:(q + 1) * BANK]).then_inc(a.bank_free[q], 1)

        @block.vector
        def _(dve):
            def statistics(nb):
                dve.wait_ge(ctx_ready, 32 * (nb + 1))
                for c in range(SC):
                    ins = nc.vector.bn_stats(w.stats[0:rows(c), c, :], m.ctx[0:rows(c), c, :])
                ins.then_inc(stat, 1)
                dve.wait_ge(stat, 4 * nb + 1)
                if not isinstance(nb, int):
                    dve.wait_ge(normed_ready, SC * nb)
                    on_its_own(dve, s)
                for c in range(SC):
                    ins = nc.vector.bn_aggr(w.mv[0:rows(c), c, :], w.stats[0:rows(c), c, :])
                ins.then_inc(stat, 1)
                dve.wait_ge(stat, 4 * nb + 2)
                nc.vector.tensor_scalar(w.var[:, :], w.mv[:, :, 1], EPS, None, ALU.add).then_inc(stat, 1)

            def inverse(nb):
                dve.wait_ge(root, nb + 1)
                nc.vector.reciprocal(w.rstd[:, :], w.var[:, :]).then_inc(stat, 1)

            def next_mask(nb):
                nc.vector.tensor_scalar(w.mask[:, :], w.position[:, :], w.lensf[:, bass.ds(nb, 1)], NEG,
                                        ALU.is_ge, ALU.mult).then_inc(mask_done, 1)
                dve.wait_ge(mask_done, nb + 1)

            def take_context(nb, before):
                for q in range(2, 4):
                    o, width = SPANS[q]
                    dve.wait_ge(a.bank_full, 4 * before + q + 1)
                    nc.vector.tensor_scalar(m.ctxT[:, o:o + width], m.psS[:, o:o + width], w.gain[:, :], w.shift[:, :],
                                            ALU.mult, ALU.add).then_inc(a.bank_free[q], 1)
                dve.wait_ge(turned, nb + 1)
                nc.vector.tensor_scalar(m.xT[:, 0:T], m.psM[:, 0:T], w.gain[:, :], w.shift[:, :],
                                        ALU.mult, ALU.add).then_inc(x_taken, 1)

            def fix_x(nb):
                if not isinstance(nb, int):
                    dve.wait_ge(turned, nb)
                nc.vector.tensor_copy(m.xb[:, :, :], m.xn[:, bass.ds(nb * TT, TT), :]).then_inc(x_fixed, 1)

            def rotate(k, j, before, banks=range(4)):
                if not isinstance(k, int) or k > 0:
                    dve.wait_ge(keys_ready, 4 * k)
                for q in banks:
                    o, width = SPANS[q]
                    dve.wait_ge(a.bank_full, 4 * before + q + 1)
                    nc.vector.scalar_tensor_tensor(w.y32[:, o:o + width], m.psS[:, o:o + width],
                                                   w.head_w[:, j, BK:BK + 1], m.cos_sin[:, o:o + width], ALU.add,
                                                   ALU.mult).then_inc(a.bank_free[q], 1)

            def rotate_query(j, before):
                dve.wait_ge(a.bank_full, 4 * before + 1)
                nc.vector.scalar_tensor_tensor(w.q_rot[:, :], m.psS[:, 0:T],
                                               w.head_w[:, j, BQ:BQ + 1], m.cos_sin[:, 0:T], ALU.add,
                                               ALU.mult).then_inc(a.bank_free[0], 1)

            def query_lo(k, j):
                dve.wait_ge(q_hi, k + 1)
                nc.vector.scalar_tensor_tensor(w.q_lo[:, j, :], m.psS[:, 3 * BANK:3 * BANK + T], float(D1) ** -0.5,
                                               w.q_hi[:, j, :], ALU.mult,
                                               ALU.subtract).then_inc(a.bank_free[3], 1)

            def value_lo(k, slot, banks=(1, 2)):
                for q in banks:
                    dve.wait_ge(v_hi, 2 * k + q)
                    for src, dst, hi in value_views(m, w, slot, 1)[q]:
                        ins = nc.vector.tensor_tensor(dst, src, hi, ALU.subtract)
                    ins.then_inc(a.bank_free[q], 1)

            def mask_max(use, slot, q):
                dve_mask_max(nc, dve, m, a, use, slot, lambda o, n: w.mask[:, o:o + n], q)

            def turn(b, g, last):
                def take_out(u):
                    o = g * (GH * D1) + (u // TT) * D1
                    return dve_take_out(nc, dve, m, a, unit(b, g, u), u % SLOTS,
                                        w.out[:, u % TT, bass.ds(o, D1)], w.bv[:, bass.ds(o, D1)], D1)

                for u in range(GU):
                    n, v, t = unit(b, g, u), u // TT, u % TT
                    before = use(b, g, v, last)
                    k, slot = head(b, g, v) + 2, (u + AHEAD) % SLOTS
                    if last and u == GU - AHEAD:
                        next_mask(b + 1)

                    def ahead(*banks):
                        for q in banks:
                            mask_max(before + 3 * t, slot, q)

                    def rest(group):
                        dve_group_lo(nc, dve, m, a, n, u % 2, group)

                    over, low, high = [done] * 3 if u == 0 or finishes(last, u - 1) else take_out(u - 1)
                    over()
                    if t == 0:
                        ahead(0, 1)
                        rest(0)
                        ahead(2)
                        rest(1)
                        ahead(3)
                        low()
                        dve_negmax(nc, dve, m, a, before, slot)
                        rotate(k, v % 2, before + 1, (0,))
                        rest(2)
                        high()
                        rotate(k, v % 2, before + 1, (1,))
                        rest(3)
                        rotate(k, v % 2, before + 1, (2, 3))
                    else:
                        rotate_query(v % 2, before + 2)
                        rest(0)
                        value_lo(k, (v + 2) % 4, (1,))
                        rest(1)
                        value_lo(k, (v + 2) % 4, (2,))
                        query_lo(k, v % 2)
                        low()
                        ahead(0)
                        rest(2)
                        high()
                        ahead(1)
                        rest(3)
                        ahead(2, 3)
                        dve_negmax(nc, dve, m, a, before + 3, slot)
                    if finishes(last, u):
                        for step in take_out(u):
                            step()
                    if last and u == TT * (GH - 2) - 1:
                        fix_x(b + 1)
                        take_context(b + 1, prep_use(b))

            dve.wait_ge(loaded, 16 * LOADS)
            nc.vector.memset(w.lensf[:, B:B + 1], 0.0)
            nc.vector.memset(w.mv[:, :, :], 0.0)
            nc.vector.tensor_copy(w.lensf[:, 0:B], w.lens[:, :]).then_inc(lens_ready, 1)
            dve.wait_ge(lens_ready, 1)
            fix_x(0)
            next_mask(0)
            statistics(0)
            inverse(0)
            take_context(0, 0)
            for h in range(2):
                rotate(h, h, 1 + 2 * h)
                rotate_query(h, 2 + 2 * h)
                value_lo(h, h)
                query_lo(h, h)
            for t in range(AHEAD):
                for q in range(4):
                    mask_max(5 + t, t, q)
                dve_negmax(nc, dve, m, a, 5 + t, t)
            with dve.Fori(0, B) as b:
                with dve.Fori(0, NG - 1) as g:
                    turn(b, g, False)
                statistics(b + 1)
                inverse(b + 1)
                turn(b, NG - 1, True)
                for q in range(2, 4):
                    dve.wait_ge(a.bank_full, 4 * fin_use(b) + q + 1)
                    nc.vector.tensor_copy(m.oT[:, q * BANK:(q + 1) * BANK],
                                          m.psS[:, q * BANK:(q + 1) * BANK]).then_inc(a.bank_free[q], 1)
                dve.wait_ge(fin_full, b + 1)
                for t in range(TT):
                    ins = nc.vector.tensor_tensor(m.tmp[:, t, :], m.psM[:, t * P:(t + 1) * P], w.bo[:, :], ALU.add)
                ins.then_inc(biased, 1)
                dve.wait_ge(biased, b + 1)
                xs = m.x[:, bass.ds(b * TT, TT), :]
                nc.vector.scalar_tensor_tensor(xs, m.tmp[:, :, :], m.gates[:, 2:3], xs,
                                               ALU.mult, ALU.add).then_inc(batch_done, 1)
            dve.wait_ge(batch_done, B)


VALUE_CHUNKS = {1: range(0, 8), 2: range(8, SC)}


def value_views(m, w, slot, part):
    def views(c0, c1, r, o):
        src = m.psS[0:r, o:o + (c1 - c0) * D1].rearrange("p (c d) -> p c d", d=D1)
        return src, w.values[0:r, slot, c0:c1, part, :], w.values[0:r, slot, c0:c1, 0, :]

    return {1: [views(0, 8, P, BANK)],
            2: [views(8, FULL, P, 2 * BANK), views(FULL, SC, REST, 2 * BANK + (FULL - 8) * D1)]}


def block_route1(nc, m, s, dram):
    normed, turned, xt_act, xt_dve = (s.sem(f"r1_{n}") for n in ("normed", "turned", "xt_act", "xt_dve"))
    logits_done, sig_done, steps, loaded = (s.sem(f"r1_{n}") for n in ("logits", "sig", "steps", "loaded"))
    with ExitStack() as stack:
        def sb(name, shape, dt=F32):
            return stack.enter_context(nc.sbuf_tensor(name, shape, dt))

        wg, bias = sb("r1_wg", [P, X1]), sb("r1_bias", [P, X1])
        score, masked, above, equal, seen = (sb(f"r1_{n}", [P, NT, X1]) for n in
                                             ("score", "masked", "above", "equal", "seen"))
        best = sb("r1_best", [P, NT, GR])
        first, level = sb("r1_first", [P, NT, GR, GR]), sb("r1_level", [P, NT, GR, GR])
        keep, top8 = sb("r1_keep", [P, NT, GR]), sb("r1_top8", [P, NT, 8])
        total = sb("r1_total", [P, NT])
        lg = m.psT[2][:, :].rearrange("p (k e) -> p k e", e=X1)

        def over_e(ap):
            return ap.to_broadcast([P, NT, X1])

        with nc.Block() as block:
            @block.sync
            def _(sp):
                sp.dma_start(wg[:, :], dram["wg1"]).then_inc(loaded, 16)
                sp.dma_start(bias[:, :], dram["expert_bias"].to_broadcast([P, X1])).then_inc(loaded, 16)

            @block.tensor
            def _(pe):
                pe_turn_x(nc, pe, m, normed, turned)
                pe.wait_ge(xt_act, 1)
                pe.wait_ge(xt_dve, 1)
                pe.wait_ge(loaded, 32)
                for k in range(NT):
                    ins = nc.tensor.matmul(lg[:, k, :], m.xT[:, k * P:(k + 1) * P], wg[:, :], start=True, stop=True)
                ins.then_inc(logits_done, 1)

            @block.scalar
            def _(act):
                ln_scalar(nc, act, m, s, 4)
                act.wait_ge(turned, 1)
                nc.scalar.copy(m.xT[:, 0:TOK // 2], m.psS[:, 0:TOK // 2]).then_inc(xt_act, 1)
                act.wait_ge(logits_done, 1)
                nc.scalar.activation(score[:, :, :], lg, ACT.Sigmoid).then_inc(sig_done, 1)

            @block.vector
            def _(dve):
                ln_vector(nc, dve, m, s, m.x, m.xn, 4)
                nc.vector.memset(total[:, :], 0.0).then_inc(normed, 1)
                dve.wait_ge(turned, 2)
                nc.vector.tensor_copy(m.xT[:, TOK // 2:TOK], m.psS[:, TOK // 2:TOK]).then_inc(xt_dve, 1)
                dve.wait_ge(sig_done, 1)
                dve.wait_ge(loaded, 32)
                step, _ = chain(dve, steps)
                step(nc.vector.tensor_tensor(masked[:, :, :], score[:, :, :],
                                             bias[:, :].unsqueeze(1).to_broadcast([P, NT, X1]), ALU.add))
                step(nc.vector.tensor_reduce(best[:, :, :], masked[:, :, :].rearrange("p k (g i) -> p k g i", g=GR),
                                             AX.X, ALU.max))
                four = [P, NT, GR, GR]
                other, own = best[:, :, :].unsqueeze(2).to_broadcast(four), best[:, :, :].unsqueeze(3).to_broadcast(four)
                step(nc.vector.tensor_tensor(first[:, :, :, :], other, own, ALU.is_gt))
                step(nc.vector.tensor_tensor(level[:, :, :, :], other, own, ALU.is_equal))
                step(nc.vector.tensor_tensor(level[:, :, :, :], level[:, :, :, :],
                                             m.earlier[:, :, :].unsqueeze(1).to_broadcast(four), ALU.mult))
                step(nc.vector.tensor_tensor(first[:, :, :, :], first[:, :, :, :], level[:, :, :, :], ALU.add))
                step(nc.vector.tensor_reduce(keep[:, :, :], first[:, :, :, :], AX.X, ALU.add))
                step(nc.vector.tensor_scalar(keep[:, :, :], keep[:, :, :], float(KEEP), None, ALU.is_lt))
                grouped = masked[:, :, :].rearrange("p k (g i) -> p k g i", g=GR)
                step(nc.vector.tensor_tensor(grouped, grouped,
                                             keep[:, :, :].unsqueeze(3).to_broadcast([P, NT, GR, X1 // GR]), ALU.mult))
                for k in range(NT):
                    ins = nc.vector.max(top8[:, k, :], masked[:, k, :])
                step(ins)
                least = over_e(top8[:, :, TOP - 1:TOP])
                step(nc.vector.tensor_tensor(above[:, :, :], masked[:, :, :], least, ALU.is_gt))
                step(nc.vector.tensor_tensor(equal[:, :, :], masked[:, :, :], least, ALU.is_equal))
                step(nc.vector.tensor_reduce(total[:, :], above[:, :, :], AX.X, ALU.add))
                step(nc.vector.tensor_tensor_scan(seen[:, :, :].rearrange("p k e -> p (k e)"), m.scanreset[:, :],
                                                  equal[:, :, :].rearrange("p k e -> p (k e)"), 0.0,
                                                  ALU.mult, ALU.add))
                step(nc.vector.tensor_tensor(seen[:, :, :], seen[:, :, :], over_e(total[:, :].unsqueeze(2)), ALU.add))
                step(nc.vector.scalar_tensor_tensor(equal[:, :, :], seen[:, :, :], float(TOP), equal[:, :, :],
                                                    ALU.is_le, ALU.mult))
                step(nc.vector.tensor_tensor(above[:, :, :], above[:, :, :], equal[:, :, :], ALU.add))
                step(nc.vector.tensor_tensor(score[:, :, :], score[:, :, :], above[:, :, :], ALU.mult))
                step(nc.vector.tensor_reduce(total[:, :], score[:, :, :], AX.X, ALU.add))
                step(nc.vector.tensor_scalar(total[:, :], total[:, :], 1e-20, None, ALU.add))
                step(nc.vector.reciprocal(total[:, :], total[:, :]))
                step(nc.vector.tensor_tensor(score[:, :, :], score[:, :, :], over_e(total[:, :].unsqueeze(2)), ALU.mult))
                step(nc.vector.tensor_scalar(m.combine[:, :, :], score[:, :, :], SCALE1, None, ALU.mult))


def block_experts1(nc, m, s, dram):
    N = PAIRS + 1
    KB = BANK // P
    loaded, weights_turned, weights_ready, mixed = (s.sem(f"e1_{n}") for n in ("loaded", "turned", "ready", "mixed"))
    projected, silu_done = s.sem("e1_projected"), s.sem("e1_silu")
    inner_done, out_full, added = (s.from_one(f"e1_{n}") for n in ("inner_done", "out_full", "added"))
    with ExitStack() as stack:
        def sb(name, shape, dt=F32):
            return stack.enter_context(nc.sbuf_tensor(name, shape, dt))

        wgate, wup, wdown = (sb(n, [P, N, P]) for n in ("e1_gate", "e1_up", "e1_down"))
        spread = sb("e1_spread", [X1 + 1, N, P], F16)
        c_hi, c_lo = sb("e1_c_hi", [X1 + 1, TOK], F16), sb("e1_c_lo", [X1, TOK], F16)
        silu, prod, inner = (sb(f"e1_{n}", [P, 2, BANK]) for n in ("silu", "prod", "inner"))
        prime(nc, s)

        def turn(blk, p):
            return blk * N + p

        banks = [(m.psS[:, 0:BANK], m.psS[:, BANK:2 * BANK], m.psT[0][:, :]),
                 (m.psS[:, 2 * BANK:3 * BANK], m.psS[:, 3 * BANK:4 * BANK], m.psT[1][:, :])]

        with nc.Block() as block:
            @block.sync
            def _(sp):
                for dst, src in ((wgate, dram["e1_gate"]), (wup, dram["e1_up"]), (wdown, dram["e1_down"]), (spread, dram["spread"])):
                    sp.dma_start(dst[:, :, :], src).then_inc(loaded, 16)

            @block.tensor
            def _(pe):
                pe.wait_ge(loaded, 64)
                for k in range(NT):
                    ins = nc.tensor.transpose(m.psS[0:X1, k * P:(k + 1) * P], m.combine[:, k, :], m.ident[:, :])
                ins.then_inc(weights_turned, 1)
                pe.wait_ge(weights_ready, 3)

                def up(blk, p):
                    n = turn(blk, p)
                    gate, upper, weight = banks[p % 2]
                    if p >= 2:
                        pe.wait_ge(inner_done, 1 + n - 1)
                    else:
                        pe.wait_ge(inner_done, 1 + blk * N)
                    x = m.xT[:, bass.ds(blk * BANK, BANK)]
                    nc.tensor.matmul(gate, wgate[:, p, :], x, start=True, stop=True)
                    nc.tensor.matmul(upper, wup[:, p, :], x, start=True, stop=True)
                    tokens = bass.ds(blk * BANK, BANK)
                    nc.tensor.matmul(weight, spread[:, p, :], c_hi[:, tokens], start=True, stop=False)
                    nc.tensor.matmul(weight, spread[0:X1, p, :], c_lo[:, tokens],
                                     start=False, stop=True).then_inc(projected, 1)

                def down(blk, p):
                    pe.wait_ge(inner_done, 1 + turn(blk, p) + 1)
                    if p == 0:
                        pe.wait_ge(added, 1 + blk)
                    for k in range(KB):
                        ins = nc.tensor.matmul(m.psO[:, k * P:(k + 1) * P], inner[:, p % 2, k * P:(k + 1) * P],
                                               wdown[:, p, :], start=(p == 0 and k == 0), stop=(p == N - 1),
                                               skip_group_check=True)
                    ins.then_inc(out_full, 1)

                with pe.Fori(0, TOK // BANK) as blk:
                    up(blk, 0)
                    for p in range(N):
                        if p + 1 < N:
                            up(blk, p + 1)
                        down(blk, p)

            @block.scalar
            def _(act):
                act.wait_ge(weights_turned, 1)
                nc.scalar.copy(c_hi[0:X1, :], m.psS[0:X1, :]).then_inc(weights_ready, 1)
                with act.Fori(0, TOK // BANK) as blk:
                    for p in range(N):
                        n = turn(blk, p)
                        act.wait_ge(projected, n + 1)
                        nc.scalar.activation(silu[:, p % 2, :], banks[p % 2][0], ACT.Silu).then_inc(silu_done, 1)

            @block.vector
            def _(dve):
                nc.vector.memset(c_hi[X1:X1 + 1, :], 1.0).then_inc(weights_ready, 1)
                dve.wait_ge(weights_ready, 2)
                nc.vector.tensor_tensor(c_lo[:, :], m.psS[0:X1, :], c_hi[0:X1, :], ALU.subtract).then_inc(weights_ready, 1)
                with dve.Fori(0, TOK // BANK) as blk:
                    for p in range(N):
                        n = turn(blk, p)
                        dve.wait_ge(silu_done, n + 1)
                        nc.vector.tensor_tensor(prod[:, p % 2, :], banks[p % 2][1], silu[:, p % 2, :],
                                                ALU.mult).then_inc(mixed, 1)
                        dve.wait_ge(mixed, n + 1)
                        if p >= 2:
                            dve.wait_ge(out_full, 1 + n - 1)
                        else:
                            dve.wait_ge(out_full, 1 + blk * N)
                        nc.vector.tensor_tensor(inner[:, p % 2, :], banks[p % 2][2], prod[:, p % 2, :],
                                                ALU.mult).then_inc(inner_done, 1)
                    dve.wait_ge(out_full, 1 + turn(blk, N))
                    xs = m.x[:, bass.ds(blk * KB, KB), :]
                    nc.vector.scalar_tensor_tensor(xs, m.psO[:, :].rearrange("p (k d) -> p k d", d=E),
                                                   m.gates[:, 3:4], xs, ALU.mult, ALU.add).then_inc(added, 1)
                dve.wait_ge(added, 1 + TOK // BANK)


def build(nc, dram):
    with ExitStack() as stack:
        def sb(name, shape, dt=F32):
            return stack.enter_context(nc.sbuf_tensor(name, shape, dt))

        def sem(name):
            return stack.enter_context(nc.semaphore(name))

        to_prime = []

        def from_one(name, start=1):
            to_prime.append((sem(name), start))
            return to_prime[-1][0]

        m, s = Named(), Named()
        m.s = s
        s.sem, s.from_one, s.to_prime = sem, from_one, to_prime
        s.load, s.ln, s.ln_sqrt, s.tanh = (sem(n) for n in ("load", "ln", "ln_sqrt", "tanh"))
        s.stored, s.passed, s.weights = (sem(n) for n in ("stored", "passed", "weights"))
        m.x, m.xn, m.xT = sb("x", [P, NT, E]), sb("xn", [P, NT + TT, E]), sb("xT", [P, TOK])
        m.stats, m.mv = sb("stats", [P, NT, 6]), sb("mv", [P, NT, 2])
        m.var, m.rstd = sb("var", [P, NT]), sb("rstd", [P, NT])
        m.ident, m.fold, m.below, m.ones = (sb(n, [P, P]) for n in ("ident", "fold", "below", "ones"))
        m.cos_sin = sb("cos_sin", [P, S])
        m.earlier, m.weight8 = sb("earlier", [P, GR, GR]), sb("weight8", [P, X0])
        m.headmask, m.scanreset = sb("headmask", [P, 4]), sb("scanreset", [P, NT * X1])
        m.gates = sb("gates", [P, 4])
        m.probs = sb("probs", [P, SLOTS, S])
        m.probsT_hi, m.probsT_lo = sb("probsT_hi", [P, 2, SC, P], F16), sb("probsT_lo", [P, 2, SC, P], F16)
        m.max4, m.negmax = sb("max4", [P, SLOTS, 4]), sb("negmax", [P, SLOTS])
        m.sums, m.rsum, m.part = sb("sums", [P, SLOTS]), sb("rsum", [P, 1]), sb("part", [P, D1])
        m.psS = stack.enter_context(nc.psum_tensor("psS", [P, 4 * BANK], F32))
        m.psT = [stack.enter_context(nc.psum_tensor(f"psT{i}", [P, BANK], F32)) for i in range(3)]
        m.psO = stack.enter_context(nc.psum_tensor("psO", [P, BANK], F32))
        m.psM = m.psO[:, 2 * D1:2 * D1 + T]
        m.ctx, m.ctxT = sb("ctx", [P, SC, E]), sb("ctxT", [P, S])
        m.xb, m.tmp, m.oT = sb("xb", [P, TT, E]), sb("tmp", [P, TT, E]), sb("oT", [P, TT * 1024])
        m.wq0, m.wk0, m.wv0, m.wo0 = (sb(n, [P, P]) for n in ("wq0", "wk0", "wv0", "wo0"))
        m.bq0, m.bk0 = sb("bq0", [P, 1]), sb("bk0", [P, 1])
        m.bv0, m.bo0 = sb("bv0", [P, E]), sb("bo0", [P, E])
        m.gate = sb("gate", [P, NT, X0])
        m.combine = sb("combine", [P, NT, X1])

        m.loaded = dict(ident=m.ident[:, :], fold=m.fold[:, :], below=m.below[:, :], cos_sin=m.cos_sin[:, :],
                        earlier=m.earlier[:, :, :], weight8=m.weight8[:, :], headmask=m.headmask[:, :],
                        scanreset=m.scanreset[:, :], ones=m.ones[:, :], gates=m.gates[:, :],
                        wq0=m.wq0[:, :], wk0=m.wk0[:, :], wv0=m.wv0[:, :],
                        wo0=m.wo0[:, :], bq0=m.bq0[:, :], bk0=m.bk0[:, :], bv0=m.bv0[:, :], bo0=m.bo0[:, :])
        d = dram
        m.source = dict(ident=d["ident"], fold=d["fold"], below=d["below"], cos_sin=d["cos_sin"], earlier=d["earlier"],
                        weight8=d["weight8"], headmask=d["headmask"], scanreset=d["scanreset"], ones=d["ones"],
                        gates=d["gates"].to_broadcast([P, 4]),
                        wq0=d["wq0"], wk0=d["wk0"], wv0=d["wv0"], wo0=d["wo0"], bq0=d["bq0"], bk0=d["bk0"],
                        bv0=d["bv0"].to_broadcast([P, E]), bo0=d["bo0"].to_broadcast([P, E]))

        block_load(nc, m, s, dram)
        block_attention0(nc, m, s, dram)
        block_route0(nc, m, s, dram)
        block_experts0(nc, m, s, dram)
        block_norm1(nc, m, s, dram)
        block_attention1(nc, m, s, dram)
        block_route1(nc, m, s, dram)
        block_experts1(nc, m, s, dram)
        with nc.Block() as block:
            @block.sync
            def _(sp):
                sp.dma_start(dram["out"].rearrange("b (t p) d -> p (b t) d", p=P), m.x[:, :, :]).then_inc(s.stored, 16)
                sp.wait_ge(s.stored, 16)


def constants():
    p = np.arange(P)
    f = np.float32
    inv = (1.0 / np.float64(10000.0) ** (np.arange(0, D1, 2, dtype=np.float64) / D1)).astype(f)
    ang = np.repeat(np.arange(S, dtype=f)[:, None] * inv[None, :], 2, axis=1).T
    sign = np.where(np.arange(D1) % 2 == 0, -1.0, 1.0).astype(f)[:, None]
    return dict(
        ident=np.eye(P, dtype=f),
        fold=(p[:, None] % D1 == p[None, :] % D1).astype(f),
        below=(p[:, None] < p[None, :]).astype(f),
        ones=np.ones((P, P), f),
        cos_sin=np.concatenate([np.cos(ang), np.sin(ang) * sign]).astype(f),
        earlier=np.broadcast_to((np.arange(GR)[None, :] < np.arange(GR)[:, None]).astype(f), (P, GR, GR)).copy(),
        weight8=np.broadcast_to(np.arange(X0, 0, -1).astype(f), (P, X0)).copy(),
        position=np.arange(S, dtype=f)[None, :],
        spread=spread(),
        headmask=((p[:, None] % 32) // D0 == np.arange(4)[None, :]).astype(f),
        scanreset=np.broadcast_to((np.arange(NT * X1) % X1 != 0).astype(f), (P, NT * X1)).copy(),
    )


def spread():
    out = np.zeros((X1 + 1, PAIRS + 1, P), np.float16)
    for e in range(X1):
        out[e, e // 2, e % 2 * I1:(e % 2 + 1) * I1] = 1
    out[X1, PAIRS] = 1
    return out


def pairs(routed, shared):
    return np.concatenate([routed.reshape(PAIRS, P, E), shared[None]]).transpose(2, 0, 1)


def head_weights(a):
    swap = np.arange(D1) ^ 1

    def both(name):
        w = a[f"L1_xattn_{name}"].reshape(-1, H, D1)
        return np.concatenate([w, w[:, :, swap]], axis=2).transpose(1, 0, 2)

    wv = a["L1_xattn_Wv"].reshape(E, H, D1).transpose(1, 0, 2)
    return np.concatenate([both("Wk"), both("Wq"), wv, both("bk").transpose(0, 2, 1),
                           both("bq").transpose(0, 2, 1)], axis=2)


def kernel(**inputs):
    import concourse.bacc as bacc
    from concourse.bass_utils import run_bass_kernel_spmd

    a = {k: np.asarray(v) for k, v in inputs.items()}
    arrays = dict(constants())
    arrays.update(
        x=a["x"], ctx=a["ctx_1024"], attn_mask=a["fside_SxS2_0"], pad=a["mask_BxS2_bf0"],
        gates=np.stack([a["g_xattn"], a["g_ffn"]], axis=1).reshape(1, 4),
        wq0=a["L0_xattn_Wq"].T, wk0=a["L0_xattn_Wk"].T, wv0=a["L0_xattn_Wv"].T, wo0=a["L0_xattn_Wo"].T,
        bq0=a["L0_xattn_bq"][:, None], bk0=a["L0_xattn_bk"][:, None],
        wg=a["L0_ffn_Wg"], w1=a["L0_ffn_W1"], w2=a["L0_ffn_W2"],
        lens=a["_lenS2"][None, :], ln_g=a["L1_xattn_ln_g"][:, None], ln_b=a["L1_xattn_ln_b"][:, None],
        head_w=head_weights(a), wo1=a["L1_xattn_Wo"].reshape(8, P, E).transpose(1, 0, 2),
        bv1=a["L1_xattn_bv"][None, :], bo1=a["L1_xattn_bo"][None, :],
        wg1=a["L1_ffn_gate_weight"].T, expert_bias=a["L1_ffn_e_score_correction_bias"][None, :],
        e1_gate=pairs(a["L1_ffn_experts_gate_up"][:, :I1], a["L1_ffn_shared_gate_w"]),
        e1_up=pairs(a["L1_ffn_experts_gate_up"][:, I1:], a["L1_ffn_shared_up_w"]),
        e1_down=np.concatenate([a["L1_ffn_experts_down"].transpose(0, 2, 1).reshape(PAIRS, P, E),
                                a["L1_ffn_shared_down_w"].T[None]]).transpose(1, 0, 2),
        bv0=a["L0_xattn_bv"][None, :], bo0=a["L0_xattn_bo"][None, :],
    )
    nc = bacc.Bacc("TRN2", target_bir_lowering=False, num_devices=1)
    dram, given = {}, {}
    for name, v in arrays.items():
        v = np.ascontiguousarray(v)
        given[f"in_{name}"] = v
        dram[name] = nc.dram_tensor(f"in_{name}", v.shape, mybir.dt.from_np(v.dtype), kind="ExternalInput").ap()
    dram["out"] = nc.dram_tensor("out_x", (B, T, E), F32, kind="ExternalOutput").ap()
    build(nc, dram)
    result = run_bass_kernel_spmd(nc, [given], core_ids=[0])
    return result.results[0]["out_x"]
```
